# Optimizing a Trainium2 kernel written in Bass

```python
import numpy as np
import jax
import jax.numpy as jnp

def _softmax(x, axis=-1):
    return jax.nn.softmax(x, axis=axis)

def _gelu(x):
    return jax.nn.gelu(x, approximate=True)

def _silu(x):
    return jax.nn.silu(x)

def _sigmoid(x):
    return jax.nn.sigmoid(x)

def _layernorm(x, axis=-1, eps=1e-05):
    m = jnp.mean(x, axis=axis, keepdims=True)
    v = jnp.var(x, axis=axis, keepdims=True)
    return (x - m) / jnp.sqrt(v + eps)

def _scatter_add(tgt, idx, src, axis=0):
    return tgt.at[idx].add(src)

def _segment_sum(src, seg, n):
    return jax.ops.segment_sum(src, seg, n)
kernel_name = 'mk_macaron_d1_jaxref_r4_58db85'

def setup_inputs(seed: int=0):
    np.random.seed(seed)
    _w = jnp.asarray

    def _L0_attn_setup():
        import jax, jax.numpy as jnp
        import numpy as np
        from jax import lax
        HID = 512
        NH = 64
        P = 64
        N = 128
        G = 1
        CS = 64
        K = 4
        D_INNER = NH * P
        CONV_DIM = D_INNER + 2 * G * N
        PROJ = D_INNER + CONV_DIM + NH
        EPS = 1e-05
        BATCH, SEQ = (2, 512)

        def _segsum(x):
            T = x.shape[-1]
            xc = jnp.cumsum(x, axis=-1)
            seg = xc[..., :, None] - xc[..., None, :]
            mask = jnp.tril(jnp.ones((T, T), dtype=bool))
            return jnp.where(mask, seg, -jnp.inf)

        def _mamba2_forward(hidden_states, W_in, conv_w, conv_b, dt_bias, A_log, D_param, norm_w, W_out):
            B_, L_ = hidden_states.shape[:2]
            proj = hidden_states @ W_in.T
            z = proj[..., :D_INNER]
            xBC = proj[..., D_INNER:D_INNER + CONV_DIM]
            dt = proj[..., D_INNER + CONV_DIM:]
            xc = lax.conv_general_dilated(jnp.transpose(xBC, (0, 2, 1)), conv_w, window_strides=(1,), padding=[(K - 1, 0)], feature_group_count=CONV_DIM)
            xc = xc + conv_b[None, :, None]
            xBC = jax.nn.silu(jnp.transpose(xc, (0, 2, 1)))
            x = xBC[..., :D_INNER].reshape(B_, L_, NH, P)
            Bm = xBC[..., D_INNER:D_INNER + G * N].reshape(B_, L_, G, N)
            Cm = xBC[..., D_INNER + G * N:].reshape(B_, L_, G, N)
            dt = jax.nn.softplus(dt + dt_bias)
            A = -jnp.exp(A_log)
            Bh = jnp.repeat(Bm, NH // G, axis=2)
            Ch = jnp.repeat(Cm, NH // G, axis=2)
            nc = L_ // CS
            x_dt = (x * dt[..., None]).reshape(B_, nc, CS, NH, P)
            B_c = Bh.reshape(B_, nc, CS, NH, N)
            C_c = Ch.reshape(B_, nc, CS, NH, N)
            dA = jnp.transpose((dt * A).reshape(B_, nc, CS, NH), (0, 3, 1, 2))
            A_cum = jnp.cumsum(dA, axis=-1)
            Lmat = jnp.exp(_segsum(dA))
            Y_diag = jnp.einsum('bclhn,bcshn,bhcls,bcshp->bclhp', C_c, B_c, Lmat, x_dt)
            decay_states = jnp.exp(A_cum[..., -1:] - A_cum)
            states = jnp.einsum('bclhn,bhcl,bclhp->bchpn', B_c, decay_states, x_dt)
            da_last = A_cum[..., -1]

            def step(prev, inp):
                s_k, d_k = inp
                new = prev * jnp.exp(d_k)[..., None, None] + s_k
                return (new, prev)
            _, prev_states = lax.scan(step, jnp.zeros((B_, NH, P, N), dtype=x.dtype), (jnp.transpose(states, (1, 0, 2, 3, 4)), jnp.transpose(da_last, (2, 0, 1))))
            prev_states = jnp.transpose(prev_states, (1, 2, 0, 3, 4))
            Y_off = jnp.einsum('bclhn,bhcpn,bhcl->bclhp', C_c, prev_states, jnp.exp(A_cum))
            y = (Y_diag + Y_off).reshape(B_, L_, NH, P) + D_param[None, None, :, None] * x
            y = y.reshape(B_, L_, D_INNER)
            g = y * jax.nn.silu(z)
            gs = D_INNER // G
            gr = g.reshape(B_, L_, G, gs)
            var = jnp.mean(gr * gr, axis=-1, keepdims=True)
            gn = (gr * lax.rsqrt(var + EPS)).reshape(B_, L_, D_INNER) * norm_w
            return gn @ W_out.T
        key = jax.random.key(seed)
        ks = jax.random.split(key, 8)
        hidden_states = jax.random.normal(ks[0], (BATCH, SEQ, HID), dtype=jnp.float32)
        W_in = jax.random.normal(ks[1], (PROJ, HID), dtype=jnp.float32) * 0.02
        conv_w = jax.random.normal(ks[2], (CONV_DIM, 1, K), dtype=jnp.float32) * 0.2
        conv_b = jax.random.normal(ks[3], (CONV_DIM,), dtype=jnp.float32) * 0.02
        dt = jnp.exp(jax.random.uniform(ks[4], (NH,)) * (np.log(0.1) - np.log(0.001)) + np.log(0.001))
        dt_bias = (dt + jnp.log(-jnp.expm1(-dt))).astype(jnp.float32)
        A_log = jnp.log(jnp.arange(1, NH + 1, dtype=jnp.float32))
        D_param = jnp.ones((NH,), dtype=jnp.float32)
        norm_w = jnp.ones((D_INNER,), dtype=jnp.float32)
        W_out = jax.random.normal(ks[5], (HID, D_INNER), dtype=jnp.float32) * 0.02
        return {'hidden_states': hidden_states, 'W_in': W_in, 'conv_w': conv_w, 'conv_b': conv_b, 'dt_bias': dt_bias, 'A_log': A_log, 'D_param': D_param, 'norm_w': norm_w, 'W_out': W_out}
    _L0_attn_in = _L0_attn_setup()

    def _L0_ffn_setup():
        import jax, jax.numpy as jnp
        import numpy as np
        H = 512
        E = 8
        K = 2
        I = 256
        NS = 1
        B, S = (2, 512)
        key = jax.random.key(seed)
        ks = jax.random.split(key, 12)
        std = 0.02
        return {'hidden_states': jax.random.normal(ks[0], (B, S, H), dtype=jnp.float32), 'router_w': jax.random.normal(ks[1], (E, H), dtype=jnp.float32) * std, 'wg': jax.random.normal(ks[2], (E, H, I), dtype=jnp.float32) * std, 'wu': jax.random.normal(ks[3], (E, H, I), dtype=jnp.float32) * std, 'wd': jax.random.normal(ks[4], (E, I, H), dtype=jnp.float32) * std, 'sg_w': jax.random.normal(ks[5], (H, I * NS), dtype=jnp.float32) * std, 'sg_b': jnp.zeros((I * NS,), dtype=jnp.float32), 'su_w': jax.random.normal(ks[6], (H, I * NS), dtype=jnp.float32) * std, 'su_b': jnp.zeros((I * NS,), dtype=jnp.float32), 'sd_w': jax.random.normal(ks[7], (I * NS, H), dtype=jnp.float32) * std, 'sd_b': jnp.zeros((H,), dtype=jnp.float32)}
    _L0_ffn_in = _L0_ffn_setup()
    _d = {'L0_attn_hidden_states': _L0_attn_in['hidden_states'], 'L0_attn_W_in': _L0_attn_in['W_in'], 'L0_attn_conv_w': _L0_attn_in['conv_w'], 'L0_attn_conv_b': _L0_attn_in['conv_b'], 'L0_attn_dt_bias': _L0_attn_in['dt_bias'], 'L0_attn_A_log': _L0_attn_in['A_log'], 'L0_attn_D_param': _L0_attn_in['D_param'], 'L0_attn_norm_w': _L0_attn_in['norm_w'], 'L0_attn_W_out': _L0_attn_in['W_out'], 'L0_ffn_router_w': _L0_ffn_in['router_w'], 'L0_ffn_wg': _L0_ffn_in['wg'], 'L0_ffn_wu': _L0_ffn_in['wu'], 'L0_ffn_wd': _L0_ffn_in['wd'], 'L0_ffn_sg_w': _L0_ffn_in['sg_w'], 'L0_ffn_sg_b': _L0_ffn_in['sg_b'], 'L0_ffn_su_w': _L0_ffn_in['su_w'], 'L0_ffn_su_b': _L0_ffn_in['su_b'], 'L0_ffn_sd_w': _L0_ffn_in['sd_w'], 'L0_ffn_sd_b': _L0_ffn_in['sd_b']}
    _x0 = _d['L0_attn_hidden_states']
    _d['L0_attn_hidden_states'] = jax.random.normal(jax.random.fold_in(jax.random.key(seed), 1), (2, 1024, 512), dtype=_x0.dtype)
    del _x0
    return _d

def reference(L0_attn_hidden_states, L0_attn_W_in, L0_attn_conv_w, L0_attn_conv_b, L0_attn_dt_bias, L0_attn_A_log, L0_attn_D_param, L0_attn_norm_w, L0_attn_W_out, L0_ffn_router_w, L0_ffn_wg, L0_ffn_wu, L0_ffn_wd, L0_ffn_sg_w, L0_ffn_sg_b, L0_ffn_su_w, L0_ffn_su_b, L0_ffn_sd_w, L0_ffn_sd_b):

    def _L0_attn_ref(hidden_states, W_in, conv_w, conv_b, dt_bias, A_log, D_param, norm_w, W_out):
        import jax, jax.numpy as jnp
        import numpy as np
        from jax import lax
        HID = 512
        NH = 64
        P = 64
        N = 128
        G = 1
        CS = 64
        K = 4
        D_INNER = NH * P
        CONV_DIM = D_INNER + 2 * G * N
        PROJ = D_INNER + CONV_DIM + NH
        EPS = 1e-05
        BATCH, SEQ = (2, 512)

        def _segsum(x):
            T = x.shape[-1]
            xc = jnp.cumsum(x, axis=-1)
            seg = xc[..., :, None] - xc[..., None, :]
            mask = jnp.tril(jnp.ones((T, T), dtype=bool))
            return jnp.where(mask, seg, -jnp.inf)

        def _mamba2_forward(hidden_states, W_in, conv_w, conv_b, dt_bias, A_log, D_param, norm_w, W_out):
            B_, L_ = hidden_states.shape[:2]
            proj = hidden_states @ W_in.T
            z = proj[..., :D_INNER]
            xBC = proj[..., D_INNER:D_INNER + CONV_DIM]
            dt = proj[..., D_INNER + CONV_DIM:]
            xc = lax.conv_general_dilated(jnp.transpose(xBC, (0, 2, 1)), conv_w, window_strides=(1,), padding=[(K - 1, 0)], feature_group_count=CONV_DIM)
            xc = xc + conv_b[None, :, None]
            xBC = jax.nn.silu(jnp.transpose(xc, (0, 2, 1)))
            x = xBC[..., :D_INNER].reshape(B_, L_, NH, P)
            Bm = xBC[..., D_INNER:D_INNER + G * N].reshape(B_, L_, G, N)
            Cm = xBC[..., D_INNER + G * N:].reshape(B_, L_, G, N)
            dt = jax.nn.softplus(dt + dt_bias)
            A = -jnp.exp(A_log)
            Bh = jnp.repeat(Bm, NH // G, axis=2)
            Ch = jnp.repeat(Cm, NH // G, axis=2)
            nc = L_ // CS
            x_dt = (x * dt[..., None]).reshape(B_, nc, CS, NH, P)
            B_c = Bh.reshape(B_, nc, CS, NH, N)
            C_c = Ch.reshape(B_, nc, CS, NH, N)
            dA = jnp.transpose((dt * A).reshape(B_, nc, CS, NH), (0, 3, 1, 2))
            A_cum = jnp.cumsum(dA, axis=-1)
            Lmat = jnp.exp(_segsum(dA))
            Y_diag = jnp.einsum('bclhn,bcshn,bhcls,bcshp->bclhp', C_c, B_c, Lmat, x_dt)
            decay_states = jnp.exp(A_cum[..., -1:] - A_cum)
            states = jnp.einsum('bclhn,bhcl,bclhp->bchpn', B_c, decay_states, x_dt)
            da_last = A_cum[..., -1]

            def step(prev, inp):
                s_k, d_k = inp
                new = prev * jnp.exp(d_k)[..., None, None] + s_k
                return (new, prev)
            _, prev_states = lax.scan(step, jnp.zeros((B_, NH, P, N), dtype=x.dtype), (jnp.transpose(states, (1, 0, 2, 3, 4)), jnp.transpose(da_last, (2, 0, 1))))
            prev_states = jnp.transpose(prev_states, (1, 2, 0, 3, 4))
            Y_off = jnp.einsum('bclhn,bhcpn,bhcl->bclhp', C_c, prev_states, jnp.exp(A_cum))
            y = (Y_diag + Y_off).reshape(B_, L_, NH, P) + D_param[None, None, :, None] * x
            y = y.reshape(B_, L_, D_INNER)
            g = y * jax.nn.silu(z)
            gs = D_INNER // G
            gr = g.reshape(B_, L_, G, gs)
            var = jnp.mean(gr * gr, axis=-1, keepdims=True)
            gn = (gr * lax.rsqrt(var + EPS)).reshape(B_, L_, D_INNER) * norm_w
            return gn @ W_out.T
        return _mamba2_forward(hidden_states, W_in, conv_w, conv_b, dt_bias, A_log, D_param, norm_w, W_out)

    def _L0_ffn_ref(hidden_states, router_w, wg, wu, wd, sg_w, sg_b, su_w, su_b, sd_w, sd_b):
        import jax, jax.numpy as jnp
        import numpy as np
        H = 512
        E = 8
        K = 2
        I = 256
        NS = 1
        B, S = (2, 512)
        x = hidden_states.reshape(-1, H)
        T = x.shape[0]
        logits = x @ router_w.T
        scores, top_idx = jax.lax.top_k(logits, K)
        comb = jnp.zeros((T, E), dtype=x.dtype).at[jnp.arange(T)[:, None], top_idx].set(scores)
        g = jnp.einsum('td,edi->eti', x, wg)
        u = jnp.einsum('td,edi->eti', x, wu)
        h = jax.nn.silu(g) * u
        y = jnp.einsum('eti,eid->etd', h, wd)
        moe_out = jnp.einsum('etd,te->td', y, comb)
        se = jax.nn.silu(x @ sg_w + sg_b) * (x @ su_w + su_b) @ sd_w + sd_b
        out = (moe_out + se).reshape(hidden_states.shape)
        return out
    x = L0_attn_hidden_states
    x = x + 0.5 * _L0_ffn_ref(_layernorm(x, axis=-1), L0_ffn_router_w, L0_ffn_wg, L0_ffn_wu, L0_ffn_wd, L0_ffn_sg_w, L0_ffn_sg_b, L0_ffn_su_w, L0_ffn_su_b, L0_ffn_sd_w, L0_ffn_sd_b)
    x = x + _L0_attn_ref(_layernorm(x, axis=-1), L0_attn_W_in, L0_attn_conv_w, L0_attn_conv_b, L0_attn_dt_bias, L0_attn_A_log, L0_attn_D_param, L0_attn_norm_w, L0_attn_W_out)
    x = x + 0.5 * _L0_ffn_ref(_layernorm(x, axis=-1), L0_ffn_router_w, L0_ffn_wg, L0_ffn_wu, L0_ffn_wd, L0_ffn_sg_w, L0_ffn_sg_b, L0_ffn_su_w, L0_ffn_su_b, L0_ffn_sd_w, L0_ffn_sd_b)
    return x

_drawn_inputs = setup_inputs


def setup_inputs(seed=0):
    import zlib

    import numpy as np

    out = dict(_drawn_inputs(seed))
    spreads = {'L0_attn_D_param': (1.0, 0.2),
     'L0_attn_norm_w': (1.0, 0.2),
     'L0_ffn_sg_b': (0.0, 0.8),
     'L0_ffn_su_b': (0.0, 0.8),
     'L0_ffn_sd_b': (0.0, 0.1)}
    factors = {'L0_attn_dt_bias': 8.0, 'L0_attn_A_log': 8.0}
    for name, (base, spread) in spreads.items():
        noise = np.random.default_rng([zlib.crc32(name.encode()), seed]).standard_normal(out[name].shape)
        drawn = base * np.exp(spread * noise) if base else spread * noise
        out[name] = jnp.asarray(drawn.astype(out[name].dtype))
    for name, factor in factors.items():
        out[name] = (out[name] * factor).astype(out[name].dtype)
    return out
```

```python
from contextlib import ExitStack

import concourse.bass as bass
from concourse import mybir

F32 = mybir.dt.float32
F32R = mybir.dt.float32r
BF16 = mybir.dt.bfloat16
ALU = mybir.AluOpType
ACT = mybir.ActivationFunctionType
AX = mybir.AxisListType


P = 128
D = 512
KT = D // P
BLK = 512
TPB = BLK // P
LN_EPS = 1e-5


class Sems:

    def __init__(self, nc, ctx, phase):
        self.nc, self.ctx, self.phase = nc, ctx, phase

    def __call__(self, name):
        return self.ctx.enter_context(self.nc.semaphore(f"{self.phase}_{name}"))


def link(eng, sem, base=0):
    n = [0]

    def done(ins):
        n[0] += 1
        ins.then_inc(sem, 1)
        eng.wait_ge(sem, base + n[0])

    return done



class LayerNorm:

    def __init__(self, nc, ctx, sem, tiles, x_tile, xt_hi, xt_lo, ident, psum, xn=None):
        self.tiles, self.blocks = tiles, tiles // TPB
        self.x_tile, self.xt_hi, self.xt_lo, self.ident, self.psum = x_tile, xt_hi, xt_lo, ident, psum

        def sb(name, shape):
            return ctx.enter_context(nc.sbuf_tensor(f"{sem.phase}_{name}", shape, F32))

        self.stats = sb("ln_stats", [P, 2, 6])
        self.moments = sb("ln_moments", [P, tiles, 2])
        self.var = sb("ln_var", [P, tiles])
        self.root = sb("ln_root", [P, tiles])
        self.rstd = sb("ln_rstd", [P, tiles])
        self.tmp = sb("ln_tmp", [P, tiles])
        self.xn = sb("ln_xn", [P, 2, D]) if xn is None else xn
        self.s_stat, self.s_var, self.s_root = sem("ln_stat"), sem("ln_var"), sem("ln_root")
        self.s_chain, self.s_xn, self.s_tr = sem("ln_chain"), sem("ln_xn"), sem("ln_tr")
        self.s_hi, self.s_lo = sem("ln_hi"), sem("ln_lo")

    def vector(self, eng, call, loaded=None):
        T, B = self.tiles, self.blocks
        n_stat = [0]
        n_chain = [0]

        def stats(b):
            if loaded is not None:
                eng.wait_ge(loaded[b], 16)
            for t in range(b * TPB, b * TPB + TPB):
                eng.bn_stats(self.stats[:, t % 2, :], self.x_tile(t)).then_inc(self.s_stat, 1)
                n_stat[0] += 1
                eng.wait_ge(self.s_stat, call * (2 * T) + n_stat[0])
                eng.bn_aggr(self.moments[:, t, :], self.stats[:, t % 2, :]).then_inc(self.s_stat, 1)
                n_stat[0] += 1
            eng.wait_ge(self.s_stat, call * (2 * T) + n_stat[0])
            s = slice(b * TPB, b * TPB + TPB)
            eng.tensor_scalar(self.var[:, s], self.moments[:, s, 1], LN_EPS, None,
                              ALU.add).then_inc(self.s_var, 1)

        def chain(ins):
            n_chain[0] += 1
            ins.then_inc(self.s_chain, 1)
            eng.wait_ge(self.s_chain, call * (5 * B) + n_chain[0])

        def normalise(b):
            s = slice(b * TPB, b * TPB + TPB)
            eng.wait_ge(self.s_root, call * B + b + 1)
            refine_rsqrt(eng, chain, self.rstd[:, s], self.root[:, s], self.var[:, s], self.tmp[:, s])
            for t in range(b * TPB, b * TPB + TPB):
                if t >= 2:
                    eng.wait_ge(self.s_tr, call * T + t - 1)
                eng.tensor_scalar(self.xn[:, t % 2, :], self.x_tile(t), self.moments[:, t, 0:1],
                                  self.rstd[:, t:t + 1], ALU.subtract, ALU.mult).then_inc(self.s_xn, 1)
                if t >= 1:
                    low(t - 1)

        def low(t):
            eng.wait_ge(self.s_hi, call * T + t + 1)
            c = slice(t * P, t * P + P)
            eng.tensor_tensor(self.xt_lo[:, :, c], self.psum(t), self.xt_hi[:, :, c].bitcast(F32),
                              ALU.subtract).then_inc(self.s_lo, 1)

        stats(0)
        for b in range(B):
            if b + 1 < B:
                stats(b + 1)
            normalise(b)
        low(T - 1)

    def scalar(self, eng, call):
        T, B = self.tiles, self.blocks

        def root(b):
            s = slice(b * TPB, b * TPB + TPB)
            eng.wait_ge(self.s_var, call * B + b + 1)
            eng.activation(self.root[:, s], self.var[:, s], ACT.Sqrt).then_inc(self.s_root, 1)

        root(0)
        for b in range(B):
            if b + 1 < B:
                root(b + 1)
            for t in range(b * TPB, b * TPB + TPB):
                eng.wait_ge(self.s_tr, call * T + t + 1)
                eng.activation(self.xt_hi[:, :, t * P:(t + 1) * P], self.psum(t),
                               ACT.Copy).then_inc(self.s_hi, 1)

    def tensor(self, eng, call):
        T = self.tiles
        for t in range(T):
            eng.wait_ge(self.s_xn, call * T + t + 1)
            if t >= 2:
                eng.wait_ge(self.s_lo, call * T + t - 1)
            for k in range(KT):
                last = eng.transpose(self.psum(t)[:, k, :], self.xn[:, t % 2, k * P:(k + 1) * P],
                                     self.ident)
            last.then_inc(self.s_tr, 1)


def refine_rsqrt(eng, chain, r, root, v, tmp):
    chain(eng.reciprocal(r, root))
    chain(eng.tensor_tensor(tmp, r, r, ALU.mult))
    chain(eng.tensor_tensor(tmp, tmp, v, ALU.mult))
    chain(eng.tensor_scalar(tmp, tmp, -0.5, 1.5, ALU.mult, ALU.add))
    chain(eng.tensor_tensor(r, r, tmp, ALU.mult))


def build_identity(pool, ident, sem, at):
    pool.memset(ident, 0.0).then_inc(sem, 1)
    pool.wait_ge(sem, at + 1)
    pool.affine_select(out=ident, in_=ident, compare_op=ALU.not_equal, fill=1.0, base=0,
                       pattern=[[-1, P]], channel_multiplier=1).then_inc(sem, 1)



def ffn_phase(nc, phase, x, hidden, w, out):
    E, _, I = w["wg"].shape
    IT = I // P
    T = x.shape[1]
    NB = T // TPB
    PAIR = 2 * NB
    LAST = E * NB + NB - 1
    ctx = ExitStack()
    with ctx:
        sem = Sems(nc, ctx, phase)

        def sb(name, shape, dt=F32):
            return ctx.enter_context(nc.sbuf_tensor(f"{phase}_{name}", shape, dt))

        def ps(name, shape):
            return ctx.enter_context(nc.psum_tensor(f"{phase}_{name}", shape, F32))

        xt_hi, xt_lo = sb("xt_hi", [P, KT, T * P], F32R), sb("xt_lo", [P, KT, T * P], F32R)
        ident = sb("ident", [P, P])
        raw_in = sb("raw_in", [P, 2, KT, I])
        raw_out = sb("raw_out", [P, IT, D])
        in_hi, in_lo = sb("in_hi", [P, 2, 2, KT, I], F32R), sb("in_lo", [P, 2, 2, KT, I], F32R)
        out_hi, out_lo = sb("out_hi", [P, 2, IT, D], F32R), sb("out_lo", [P, 2, IT, D], F32R)
        sil = sb("sil", [P, IT, BLK])
        h = sb("h", [P, IT, BLK])
        h_hi, h_lo = sb("h_hi", [P, 2, IT, BLK], F32R), sb("h_lo", [P, 2, IT, BLK], F32R)
        router = sb("router", [P, KT, E])
        router_hi, router_lo = sb("router_hi", [P, KT, E], F32R), sb("router_lo", [P, KT, E], F32R)
        gate_bias, up_bias = sb("gate_bias", [P, IT]), sb("up_bias", [P, IT])
        one = sb("one", [P, 1])
        down_bias = sb("down_bias", [P, D])
        logits = sb("logits", [P, T, E])
        above = sb("above", [P, T, E, E])
        equal = sb("equal", [P, T, E, E])
        earlier = sb("earlier", [P, E, E])
        rank = sb("rank", [P, T, E])
        chosen = sb("chosen", [P, T, E])
        weight = sb("weight", [P, (E + 1) * T])

        p_gate, p_up = ps("p_gate", [P, IT, BLK]), ps("p_up", [P, IT, BLK])
        p_down = ps("p_down", [P, TPB, D])
        p_logits = p_down[:, 2, 0:T * E].rearrange("p (t e) -> p t e", t=T)

        s_const, s_small, s_route = sem("const"), sem("small"), sem("route")
        s_x = [sem(f"x{b}") for b in range(NB)]
        s_raw_in, s_raw_out, s_split = sem("raw_in"), sem("raw_out"), sem("split")
        s_gate, s_up, s_down = sem("gate"), sem("up"), sem("down")
        s_sil, s_h, s_hi, s_lo, s_acc = sem("sil"), sem("h"), sem("hi"), sem("lo"), sem("acc")
        s_bias, s_logits, s_rank, s_weight, s_out = (sem("bias"), sem("logits"), sem("rank"),
                                                     sem("weight"), sem("out"))
        SPLITS = 6

        ln = LayerNorm(nc, ctx, sem, T, lambda t: x[:, t, :], xt_hi, xt_lo, ident[:, :],
                       lambda t: p_down[:, t % 2, :].rearrange("p (k c) -> p k c", k=KT))

        block = ctx.enter_context(nc.Block())

        @block.sync
        def _(sp):
            if hidden is not None:
                rows = hidden.rearrange("a (t p) d -> p a t d", p=P)
                per = rows.shape[2]
                for b in range(NB):
                    a, t = b * TPB // per, b * TPB % per
                    sp.dma_start(x[:, b * TPB:(b + 1) * TPB, :],
                                 rows[:, a, t:t + TPB, :]).then_inc(s_x[b], 16)

            def load(turn, gate, up, down, first=False):
                if not first:
                    sp.wait_ge(s_split, turn * SPLITS - 2)
                sp.dma_start(raw_in[:, 0, :, :], gate.rearrange("(k p) i -> p k i", p=P)).then_inc(s_raw_in, 16)
                sp.dma_start(raw_in[:, 1, :, :], up.rearrange("(k p) i -> p k i", p=P)).then_inc(s_raw_in, 16)
                if not first:
                    sp.wait_ge(s_split, turn * SPLITS)
                sp.dma_start(raw_out[:, :, :], down.rearrange("(k p) d -> p k d", p=P)).then_inc(s_raw_out, 16)

            with nc.allow_non_contiguous_dma(reason="short vectors, once"):
                sp.dma_start(router[:, :, :], w["router_t"].rearrange("(k p) e -> p k e", p=P)).then_inc(s_small, 16)
                sp.dma_start(down_bias[:, :], w["sd_b"].partition_broadcast(P)).then_inc(s_small, 16)
                sp.dma_start(gate_bias[:, :], w["sg_b"].rearrange("(i p) -> p i", p=P)).then_inc(s_small, 16)
                sp.dma_start(up_bias[:, :], w["su_b"].rearrange("(i p) -> p i", p=P)).then_inc(s_small, 16)
            load(0, w["sg_w"], w["su_w"], w["sd_w"], first=True)
            with sp.Fori(0, E) as e:
                load(e + 1, w["wg"][e], w["wu"][e], w["wd"][e])
            if out is not None:
                rows = out.rearrange("a (t p) d -> p a t d", p=P)
                per = rows.shape[2]
                for b in range(NB):
                    a, t = b * TPB // per, b * TPB % per
                    sp.wait_ge(s_acc, (E * NB + b + 1) * TPB)
                    sp.dma_start(rows[:, a, t:t + TPB, :],
                                 x[:, b * TPB:(b + 1) * TPB, :]).then_inc(s_out, 16)
                sp.wait_ge(s_out, 16 * NB)

        @block.gpsimd
        def _(pool):
            build_identity(pool, ident[:, :], s_const, 0)
            pool.memset(one[:, :], 1.0).then_inc(s_const, 1)
            pool.memset(weight[:, E * T:(E + 1) * T], 0.5).then_inc(s_const, 1)
            pool.memset(earlier[:, :, :], 0.0).then_inc(s_const, 1)
            pool.wait_ge(s_const, 5)
            pool.affine_select(out=earlier[:, :, :], in_=earlier[:, :, :], compare_op=ALU.is_ge, fill=1.0,
                               base=0, pattern=[[-1, E], [1, E]], channel_multiplier=0).then_inc(s_const, 1)
            pool.wait_ge(s_small, 64)
            pool.tensor_copy(router_hi[:, :, :], router[:, :, :]).then_inc(s_route, 1)
            pool.wait_ge(s_route, 1)
            pool.tensor_tensor(router_lo[:, :, :], router[:, :, :], router_hi[:, :, :].bitcast(F32),
                               ALU.subtract).then_inc(s_route, 1)
            pool.tensor_scalar(down_bias[:, :], down_bias[:, :], 0.5, None, ALU.mult).then_inc(s_route, 1)

            def split(turn, parity, behind):
                n = [0]

                def part(hi, lo, raw):
                    pool.tensor_tensor(hi, raw, one[:, :].broadcast_to(raw.shape) if len(raw.shape) == 2 else
                                       one[:, :].unsqueeze(1).broadcast_to(raw.shape),
                                       ALU.mult).then_inc(s_split, 1)
                    n[0] += 1
                    pool.wait_ge(s_split, turn * SPLITS + n[0])
                    pool.tensor_tensor(lo, raw, hi.bitcast(F32), ALU.subtract).then_inc(s_split, 1)
                    n[0] += 1

                if behind:
                    pool.wait_ge(s_down, (turn - 1) * NB * TPB)
                for j in range(2):
                    pool.wait_ge(s_raw_in, turn * 32 + 32)
                    part(in_hi[:, parity, j, :, :], in_lo[:, parity, j, :, :], raw_in[:, j, :, :])
                pool.wait_ge(s_raw_out, turn * 16 + 16)
                part(out_hi[:, parity, :, :], out_lo[:, parity, :, :], raw_out[:, :, :])

            split(0, 0, behind=False)
            pool.wait_ge(s_route, 3)
            for t in range(T):
                pool.wait_ge(ln.s_xn, t + 1)
                pool.tensor_tensor(x[:, t, :], x[:, t, :], down_bias[:, :], ALU.add).then_inc(s_bias, 1)
            split(1, 1, behind=False)
            with pool.Fori(1, E // 2) as i:
                split(i * 2, 0, behind=True)
                split(i * 2 + 1, 1, behind=True)
            split(E, 0, behind=True)

        @block.scalar
        def _(act):
            ln.scalar(act, 0)
            act.wait_ge(s_small, 64)

            def gate(unit, parity, bias=None, first=False):
                for i in range(IT):
                    act.wait_ge(s_gate, unit * IT + i + 1)
                    if not first:
                        act.wait_ge(s_h, unit * IT - IT + i + 1)
                    act.activation(sil[:, i, :], p_gate[:, i, :], ACT.Silu,
                                   bias=0.0 if bias is None else bias[:, i:i + 1]).then_inc(s_sil, 1)
                for i in range(IT):
                    act.wait_ge(s_h, unit * IT + i + 1)
                    if not first:
                        act.wait_ge(s_down, unit * TPB - TPB)
                    act.activation(h_hi[:, parity, i, :], h[:, i, :], ACT.Copy).then_inc(s_hi, 1)

            for b in range(NB):
                gate(b, b % 2, gate_bias, first=b == 0)
            with act.Fori(0, E // 2) as i:
                for u in range(PAIR):
                    gate(i * PAIR + NB + u, u % 2)

        @block.vector
        def _(dve):
            ln.vector(dve, 0, s_x if hidden is not None else None)
            dve.wait_ge(s_logits, 1)
            dve.tensor_copy(logits[:, :, :], p_logits).then_inc(s_rank, 1)
            dve.wait_ge(s_rank, 1)
            l_f = logits[:, :, :].unsqueeze(2).broadcast_to([P, T, E, E])
            l_e = logits[:, :, :].unsqueeze(3).broadcast_to([P, T, E, E])
            dve.tensor_tensor(above[:, :, :, :], l_f, l_e, ALU.is_gt).then_inc(s_rank, 1)
            dve.tensor_tensor(equal[:, :, :, :], l_f, l_e, ALU.is_equal).then_inc(s_rank, 1)
            dve.wait_ge(s_rank, 3)
            dve.wait_ge(s_const, 6)
            dve.tensor_tensor(equal[:, :, :, :], equal[:, :, :, :],
                              earlier[:, :, :].unsqueeze(1).broadcast_to([P, T, E, E]),
                              ALU.mult).then_inc(s_rank, 1)
            dve.wait_ge(s_rank, 4)
            dve.tensor_tensor(above[:, :, :, :], above[:, :, :, :], equal[:, :, :, :],
                              ALU.add).then_inc(s_rank, 1)
            dve.wait_ge(s_rank, 5)
            dve.tensor_reduce(rank[:, :, :], above[:, :, :, :], AX.X, ALU.add).then_inc(s_rank, 1)
            dve.wait_ge(s_rank, 6)
            dve.tensor_scalar(chosen[:, :, :], rank[:, :, :], 2.0, 0.5, ALU.is_lt,
                              ALU.mult).then_inc(s_rank, 1)
            dve.wait_ge(s_rank, 7)
            dve.tensor_tensor(weight[:, 0:E * T].rearrange("p (e t) -> p t e", e=E), chosen[:, :, :],
                              logits[:, :, :], ALU.mult).then_inc(s_weight, 1)
            dve.wait_ge(s_weight, 1)
            dve.wait_ge(s_small, 64)

            def inner(unit, parity, bias=None, first=False):
                for i in range(IT):
                    dve.wait_ge(s_up, unit * IT + i + 1)
                    dve.wait_ge(s_sil, unit * IT + i + 1)
                    if not first:
                        dve.wait_ge(s_lo, unit * IT - IT + i + 1)
                    if bias is None:
                        dve.tensor_tensor(h[:, i, :], p_up[:, i, :], sil[:, i, :], ALU.mult).then_inc(s_h, 1)
                    else:
                        dve.scalar_tensor_tensor(h[:, i, :], p_up[:, i, :], bias[:, i:i + 1], sil[:, i, :],
                                                 ALU.add, ALU.mult).then_inc(s_h, 1)
                for i in range(IT):
                    dve.wait_ge(s_hi, unit * IT + i + 1)
                    dve.tensor_tensor(h_lo[:, parity, i, :], h[:, i, :],
                                      h_hi[:, parity, i, :].bitcast(F32), ALU.subtract).then_inc(s_lo, 1)

            def accumulate(unit, e, b):
                for t in range(TPB):
                    tile = b * TPB + t
                    dve.wait_ge(s_down, unit * TPB + t + 1)
                    dve.scalar_tensor_tensor(x[:, tile, :], p_down[:, t, :],
                                             weight[:, bass.ds(e * T + tile, 1)], x[:, tile, :],
                                             ALU.mult, ALU.add).then_inc(s_acc, 1)

            SHARED = E
            for b in range(NB):
                inner(b, b % 2, up_bias, first=b == 0)
                if b == 1:
                    dve.wait_ge(s_bias, T)
                    dve.wait_ge(s_const, 6)
                if b >= 1:
                    accumulate(b - 1, SHARED, b - 1)
            inner(NB, NB % 2)
            accumulate(NB - 1, SHARED, NB - 1)
            with dve.Fori(0, E // 2 - 1) as i:
                for u in range(1, PAIR + 1):
                    inner(i * PAIR + NB + u, u % 2)
                    accumulate(i * PAIR + NB + u - 1, i * 2 + (u - 1) // NB, (u - 1) % NB)
            for n in range(LAST - PAIR + 2, LAST + 2):
                if n <= LAST:
                    inner(n, n % 2)
                accumulate(n - 1, (n - 1) // NB - 1, (n - 1) % NB)

        @block.tensor
        def _(pe):
            pe.wait_ge(s_const, 2)
            ln.tensor(pe, 0)
            pe.wait_ge(s_route, 2)
            pe.wait_ge(ln.s_lo, T)
            for t in range(T):
                c = slice(t * P, (t + 1) * P)
                for k in range(KT):
                    for j, (a, b) in enumerate([(xt_lo, router_lo), (xt_lo, router_hi),
                                                (xt_hi, router_lo), (xt_hi, router_hi)]):
                        last = pe.matmul(p_logits[:, t, :], a[:, k, c], b[:, k, :],
                                         start=(k == 0 and j == 0), stop=(k == KT - 1 and j == 3))
            last.then_inc(s_logits, 1)

            def inner(unit, turn, parity, b, first=False):
                c = slice(b * BLK, (b + 1) * BLK)
                for i in range(IT):
                    if not first:
                        pe.wait_ge(s_h, unit * IT - IT + i + 1)
                    for j, (bank, done) in enumerate([(p_gate, s_gate), (p_up, s_up)]):
                        if b == 0:
                            pe.wait_ge(s_split, turn * SPLITS + 2 * j + 2)
                        for k in range(KT):
                            wh = in_hi[:, parity, j, k, i * P:(i + 1) * P]
                            wl = in_lo[:, parity, j, k, i * P:(i + 1) * P]
                            pe.matmul(bank[:, i, :], wh, xt_lo[:, k, c], start=(k == 0), stop=False)
                            pe.matmul(bank[:, i, :], wh, xt_hi[:, k, c], start=False, stop=False)
                            last = pe.matmul(bank[:, i, :], wl, xt_hi[:, k, c], start=False,
                                             stop=(k == KT - 1))
                        last.then_inc(done, 1)

            def outer(unit, turn, parity, b, first=False):
                pe.wait_ge(s_lo, unit * IT + IT)
                if b == 0:
                    pe.wait_ge(s_split, turn * SPLITS + SPLITS)
                if first:
                    pe.wait_ge(s_rank, 1)
                for t in range(TPB):
                    if not first:
                        pe.wait_ge(s_acc, unit * TPB - TPB + t + 1)
                    c = slice(t * P, (t + 1) * P)
                    for k in range(IT):
                        hh, hl = h_hi[:, b % 2, k, c], h_lo[:, b % 2, k, c]
                        pe.matmul(p_down[:, t, :], hh, out_lo[:, parity, k, :], start=(k == 0), stop=False)
                        pe.matmul(p_down[:, t, :], hh, out_hi[:, parity, k, :], start=False, stop=False)
                        last = pe.matmul(p_down[:, t, :], hl, out_hi[:, parity, k, :], start=False,
                                         stop=(k == IT - 1))
                    last.then_inc(s_down, 1)

            for b in range(NB):
                inner(b, 0, 0, b, first=b == 0)
                if b >= 1:
                    outer(b - 1, 0, 0, b - 1, first=b == 1)
            with pe.Fori(0, E // 2) as i:
                for u in range(PAIR):
                    turn = i * 2 + u // NB + 1
                    inner(i * PAIR + NB + u, turn, (u // NB + 1) % 2, u % NB)
                    if u == 0:
                        outer(i * PAIR + NB - 1, i * 2, 0, NB - 1)
                    else:
                        outer(i * PAIR + NB + u - 1, i * 2 + (u - 1) // NB + 1, ((u - 1) // NB + 1) % 2,
                              (u - 1) % NB)
            outer(LAST, E, 0, NB - 1)



def mamba_phase(nc, phase, x, batches, w):
    DI, _ = w["out_t"].shape
    HEADS = w["dt_bias"].shape[0]
    HD = DI // HEADS
    N = P
    T = x.shape[1] // batches
    NB = T // TPB
    CT = 2
    GC = CT * P
    GH = GC // HD
    G = DI // GC
    CPB = TPB
    UNITS = G * NB
    TAPS = w["conv_w"].shape[2]
    HALO = TAPS - 1
    CONV_TILES = w["conv_w"].shape[0] // P
    RMS_EPS = 1e-5
    Z0, X0, B0, DT0 = 0, DI, 2 * DI, 2 * DI + 2 * N
    assert NB == 2 and N == P and HEADS * 2 == P
    ctx = ExitStack()
    with ctx:
        sem = Sems(nc, ctx, phase)

        def sb(name, shape, dt=F32):
            return ctx.enter_context(nc.sbuf_tensor(f"{phase}_{name}", shape, dt))

        def ps(name, shape):
            return ctx.enter_context(nc.psum_tensor(f"{phase}_{name}", shape, F32))

        ident, ident16 = sb("ident", [P, P]), sb("ident16", [P, P], BF16)
        causal = sb("causal", [P, P])
        never = sb("never", [P, P], BF16)
        ones = sb("ones", [P, 2])
        one = sb("one", [P, 1])
        head_of = sb("head_of", [P, HEADS], BF16)
        taps = sb("taps", [P, CONV_TILES, TAPS])
        conv_bias = sb("conv_bias", [P, CONV_TILES])
        skip = sb("skip", [P, DI // P])
        norm_w = sb("norm_w", [P, DI // P])
        dt_bias, decay_rate = sb("dt_bias", [P, HEADS]), sb("decay_rate", [P, HEADS])
        xt_hi, xt_lo = sb("xt_hi", [P, KT, T * P], F32R), sb("xt_lo", [P, KT, T * P], F32R)
        raw_x, raw_z = sb("raw_x", [P, KT, GC]), sb("raw_z", [P, KT, GC])
        raw_out = sb("raw_out", [P, CT, D])
        in_hi, in_lo = sb("in_hi", [P, 2 * CT, KT, P], F32R), sb("in_lo", [P, 2 * CT, KT, P], F32R)
        out_hi, out_lo = sb("out_hi", [P, CT, D], F32R), sb("out_lo", [P, CT, D], F32R)
        bc = sb("bc", [P, 2, T * P])
        b_rows = sb("b_rows", [P, T, N])
        scores = sb("scores", [P, T, P])
        dt = sb("dt", [P, T, HEADS])
        cum = sb("cum", [P, T, HEADS])
        exp_cum = sb("exp_cum", [P, T, HEADS])
        to_end = sb("to_end", [P, T, HEADS])
        exp_last = sb("exp_last", [P, T, HEADS])
        cum_hm, cum_l = sb("cum_hm", [P, T * P], BF16), sb("cum_l", [P, T * P], BF16)
        square_sum = sb("square_sum", [P, T * P])
        total = sb("total", [P, T, D])
        neg_cum_g, exp_last_g, to_end_g = (sb(n, [P, T, GH]) for n in ("neg_cum_g", "exp_last_g", "to_end_g"))
        head_g = sb("head_g", [P, GH], BF16)
        state, decayed = sb("state", [P, GH, HD]), sb("decayed", [P, GH, HD])
        xraw = sb("xraw", [P, NB, CT, HALO + BLK])
        xs = sb("xs", [P, 2, CT, BLK])
        zs = sb("zs", [P, 2, CT, BLK])
        xdt = sb("xdt", [P, CPB, GH, HD])
        xend = sb("xend", [P, CPB, GH, HD])
        mix = sb("mix", [P, 2, GH, P])
        y = sb("y", [P, CPB, GC])
        g = sb("g", [P, CT, BLK])
        g_hi, g_lo = sb("g_hi", [P, CT, BLK], F32R), sb("g_lo", [P, CT, BLK], F32R)
        work = zs[:, :, :, :].rearrange("p a c t -> p (a c t)")[:, 0:3 * T * HEADS].rearrange("p (a t) -> p a t", a=3)
        parts = g[:, :, :].rearrange("p c t -> p (c t)").bitcast(BF16).rearrange("p (j t a h) -> p j t a h", j=2, t=T, a=2)
        part_hm = parts[:, 0]
        part_l = parts[:, 1]

        p_proj = ps("p_proj", [P, CT, BLK])
        p_tr, p_dec = ps("p_tr", [P, BLK]), ps("p_dec", [P, GH, P])
        p_y, p_st = ps("p_y", [P, 2, GH, HD]), ps("p_st", [P, BLK])
        p_out = ps("p_out", [P, 2, D])
        p_y_flat = p_y[:, :, :, :].rearrange("p a h d -> p (a h d)")

        s_const, s_small, s_rate = sem("const"), sem("small"), sem("rate")
        s_raw_x, s_raw_z, s_raw_out = sem("raw_x"), sem("raw_z"), sem("raw_out")
        s_split_x, s_split_z, s_scaled, s_split_out = (sem("split_x"), sem("split_z"), sem("scaled"),
                                                       sem("split_out"))
        s_dt, s_arg, s_u, s_soft, s_cum, s_cumc = (sem("dt"), sem("arg"), sem("u"), sem("soft"), sem("cum"),
                                                   sem("cumc"))
        s_parts, s_last, s_clamp, s_exps, s_partt, s_partc = (sem("parts"), sem("last"), sem("clamp"),
                                                              sem("exps"), sem("partt"), sem("partc"))
        s_brow, s_browc, s_score, s_scorec, s_clear = (sem("brow"), sem("browc"), sem("score"),
                                                       sem("scorec"), sem("clear"))
        s_px, s_pz, s_xtr, s_dec, s_y2, s_st, s_ytr, s_pout = (
            sem("px"), sem("pz"), sem("xtr"), sem("dec"), sem("y2"), sem("st"), sem("ytr"), sem("pout"))
        s_xraw, s_xs, s_zs, s_exp, s_ghi, s_sq = (sem("xraw"), sem("xs"), sem("zs"), sem("exp"),
                                                  sem("ghi"), sem("sq"))
        s_conv, s_skip, s_g, s_glo, s_xdt, s_mix = (sem("conv"), sem("skip"), sem("g"), sem("glo"),
                                                    sem("xdt"), sem("mix"))
        s_car, s_y, s_state, s_zero, s_acc, s_stage = (sem("car"), sem("y"), sem("state"), sem("zero"),
                                                       sem("acc"), sem("stage"))
        s_xend, s_decayed, s_sqs = sem("xend"), sem("decayed"), sem("sqs")
        s_var, s_vara, s_root, s_fin, s_add = (sem("var"), sem("vara"), sem("root"), sem("fin"),
                                               sem("add"))

        lns = LayerNorm(nc, ctx, sem, T, None, xt_hi, xt_lo, ident[:, :],
                        lambda t: p_out[:, t % 2, :].rearrange("p (k c) -> p k c", k=KT),
                        xn=y[:, :, :].rearrange("p c d -> p (c d)").rearrange("p (a d) -> p a d", a=2))

        var, root, rstd, tmp = lns.var, lns.root, lns.rstd, lns.tmp

        CONVS = UNITS + NB
        SMALL = 16 * (5 + P // HD)
        SOFT_STEPS = 20
        FIN_STEPS = 5

        def unit(k, gi, b):
            u = gi * NB + b
            return u + k * UNITS, u + NB + k * CONVS

        block = ctx.enter_context(nc.Block())

        @block.sync
        def _(sp):
            with nc.allow_non_contiguous_dma(reason="short vectors, once"):
                sp.dma_start(taps[:, :, :], w["conv_w"].rearrange("(j p) a k -> p j (a k)", p=P)).then_inc(s_small, 16)
                sp.dma_start(conv_bias[:, :], w["conv_b"].rearrange("(j p) -> p j", p=P)).then_inc(s_small, 16)
                sp.dma_start(norm_w[:, :], w["norm_w"].rearrange("(j p) -> p j", p=P)).then_inc(s_small, 16)
                per = P // HD
                d = w["D_param"].rearrange("(j a) -> a j", a=per)
                for a in range(per):
                    sp.dma_start(skip[a * HD:(a + 1) * HD, :], d[a].partition_broadcast(HD)).then_inc(s_small, 16)
                sp.dma_start(dt_bias[:, :], w["dt_bias"].partition_broadcast(P)).then_inc(s_small, 16)
                sp.dma_start(decay_rate[:, :], w["A_log"].partition_broadcast(P)).then_inc(s_small, 16)
            in_t = w["in_t"].rearrange("(k p) c -> p k c", p=P)

            def load_in(stream, x0, z_steps, z0, n=GC):
                if not isinstance(stream, int) or stream > 0:
                    sp.wait_ge(s_split_x, stream * 4)
                    sp.wait_ge(s_split_z, z_steps)
                sp.dma_start(raw_x[:, :, :], in_t[:, :, bass.ds(x0, GC)]).then_inc(s_raw_x, 16)
                sp.dma_start(raw_z[:, :, 0:n], in_t[:, :, bass.ds(z0, n)]).then_inc(s_raw_z, 16)

            def load_out(n, gi):
                if not isinstance(n, int) or n > 0:
                    sp.wait_ge(s_split_out, n * 4)
                sp.dma_start(raw_out[:, :, :],
                             w["out_t"][bass.ds(gi * GC, GC), :].rearrange("(k p) d -> p k d", p=P)).then_inc(s_raw_out, 16)

            for k in range(batches):
                sx, sz = k * (G + 1), k * (4 * G + 2)
                load_in(sx, B0, sz, DT0, HEADS)
                load_in(sx + 1, X0, sz + 2, Z0)
                load_out(k * G, 0)
                with sp.Fori(1, G) as gi:
                    load_in(gi + (sx + 1), gi * GC + X0, gi * 4 + (sz + 2), gi * GC + Z0)
                    load_out(gi + k * G, gi)

        @block.gpsimd
        def _(pool):
            build_identity(pool, ident[:, :], s_const, 0)
            build_identity(pool, ident16[:, :], s_const, 2)
            pool.memset(causal[:, :], 1.0).then_inc(s_const, 1)
            pool.memset(head_of[:, :], 0.0).then_inc(s_const, 1)
            pool.memset(never[:, :], 0.0).then_inc(s_const, 1)
            pool.wait_ge(s_const, 7)
            pool.affine_select(out=never[:, :], in_=never[:, :], compare_op=ALU.is_ge, fill=-1e37, base=0,
                               pattern=[[1, P]], channel_multiplier=-1).then_inc(s_const, 1)
            pool.affine_select(out=causal[:, :], in_=causal[:, :], compare_op=ALU.is_ge, fill=0.0, base=0,
                               pattern=[[1, P]], channel_multiplier=-1).then_inc(s_const, 1)
            for a in range(P // HEADS):
                pool.affine_select(out=head_of[:, :], in_=head_of[:, :], compare_op=ALU.not_equal, fill=1.0,
                                   base=-a * HEADS, pattern=[[-1, HEADS]],
                                   channel_multiplier=1).then_inc(s_const, 1)
                pool.wait_ge(s_const, 10 + a)
            pool.memset(ones[:, :], 1.0).then_inc(s_const, 1)
            pool.memset(one[:, :], 1.0).then_inc(s_const, 1)
            pool.memset(xraw[:, 0, :, 0:HALO], 0.0).then_inc(s_const, 1)
            pool.wait_ge(s_const, 14)

            def split(hi, lo, raw, done, at):
                unit_col = one[:, :] if len(raw.shape) == 2 else one[:, :].unsqueeze(1)
                pool.tensor_tensor(hi, raw, unit_col.broadcast_to(raw.shape), ALU.mult).then_inc(done, 1)
                pool.wait_ge(done, at + 1)
                pool.tensor_tensor(lo, raw, hi.bitcast(F32), ALU.subtract).then_inc(done, 1)

            def split_x(stream, ct):
                pool.wait_ge(s_raw_x, stream * 16 + 16)
                split(in_hi[:, ct, :, :], in_lo[:, ct, :, :], raw_x[:, :, ct * P:(ct + 1) * P],
                      s_split_x, stream * 4 + 2 * ct)

            def split_z(loads, steps, ct):
                pool.wait_ge(s_raw_z, loads * 16)
                split(in_hi[:, CT + ct, :, :], in_lo[:, CT + ct, :, :], raw_z[:, :, ct * P:(ct + 1) * P],
                      s_split_z, steps + 2 * ct)

            def split_out(n):
                for ct in range(CT):
                    pool.wait_ge(s_scaled, n * CT + ct + 1)
                    split(out_hi[:, ct, :], out_lo[:, ct, :], raw_out[:, ct, :], s_split_out, n * 4 + 2 * ct)

            def add_squares(U, b, ct, first=False):
                pool.wait_ge(s_sq, U * CT + ct + 1)
                if not first:
                    pool.wait_ge(s_sqs, U * CT + ct)
                c = slice(b * BLK, (b + 1) * BLK)
                pool.tensor_tensor(square_sum[:, c], square_sum[:, c], zs[:, b, ct, :], ALU.add).then_inc(s_sqs, 1)

            def slot(k, gi, b, first=False, second=False, last_group=False):
                U, V = unit(k, gi, b)
                for j in range(CPB // 2):
                    pool.wait_ge(s_xdt, U * 2 + j + 1)
                    if not first:
                        pool.wait_ge(s_st, U * CPB - CPB + 2 * j + 2)
                    c = b * CPB + 2 * j
                    pool.tensor_tensor(xend[:, 2 * j:2 * j + 2, :, :], xdt[:, 2 * j:2 * j + 2, :, :],
                                       to_end_g[:, c:c + 2, :].unsqueeze(3).broadcast_to([P, 2, GH, HD]),
                                       ALU.mult).then_inc(s_xend, 1)
                for c in range(CPB):
                    if b == 0 and c == 0:
                        pool.wait_ge(s_zero, gi + (k * G + 1))
                    else:
                        pool.wait_ge(s_state, U * CPB + c)
                    pool.tensor_tensor(decayed[:, :, :], state[:, :, :],
                                       exp_last_g[:, b * CPB + c, :].unsqueeze(2).broadcast_to([P, GH, HD]),
                                       ALU.mult).then_inc(s_decayed, 1)
                    if c >= 2 and not first:
                        add_squares(U - 1, 1 - b, c - 2, second and c == 2)
                    if b == 0 and not last_group:
                        if c < CT:
                            pool.wait_ge(s_px, V * CT + CT + c + 1)
                            split_x(gi + (k * (G + 1) + 2), c)
                        else:
                            pool.wait_ge(s_pz, U * CT + c + 1)
                            split_z(gi + (k * (G + 1) + 3), gi * 4 + (k * (4 * G + 2) + 6), c - CT)
                if b == 0 and not first:
                    pool.wait_ge(s_pout, U * TPB)
                    split_out(gi + k * G)

            for k in range(batches):
                split_x_base = k * (G + 1)
                if k > 0:
                    pool.wait_ge(s_add, k * T)
                pool.memset(square_sum[:, :], 0.0).then_inc(s_clear, 1)
                pool.memset(total[:, :, :], 0.0).then_inc(s_clear, 1)
                if k > 0:
                    pool.wait_ge(s_px, k * CONVS * CT)
                    pool.wait_ge(s_pz, k * UNITS * CT)
                for ct in range(CT):
                    split_x(split_x_base, ct)
                pool.wait_ge(s_raw_z, split_x_base * 16 + 16)
                split(in_hi[:, CT, :, 0:HEADS], in_lo[:, CT, :, 0:HEADS], raw_z[:, :, 0:HEADS],
                      s_split_z, k * (4 * G + 2))
                for ct in range(CT):
                    pool.wait_ge(s_px, (k * CONVS + NB - 1) * CT + ct + 1)
                    split_x(split_x_base + 1, ct)
                pool.wait_ge(s_dt, k + 1)
                for ct in range(CT):
                    split_z(split_x_base + 2, k * (4 * G + 2) + 2, ct)
                if k > 0:
                    pool.wait_ge(s_pout, k * UNITS * TPB)
                split_out(k * G)
                pool.wait_ge(s_stage, k * G + 1)
                slot(k, 0, 0, first=True)
                pool.wait_ge(s_clear, (k + 1) * 2)
                slot(k, 0, 1, second=True)
                with pool.Fori(1, G - 1) as gi:
                    pool.wait_ge(s_stage, gi + (k * G + 1))
                    slot(k, gi, 0)
                    slot(k, gi, 1)
                pool.wait_ge(s_stage, (k + 1) * G)
                slot(k, G - 1, 0, last_group=True)
                slot(k, G - 1, 1, last_group=True)
                U = (k + 1) * UNITS - 1
                for ct in range(CT):
                    add_squares(U, NB - 1, ct)

        @block.scalar
        def _(act):
            act.wait_ge(s_small, SMALL)
            act.activation(decay_rate[:, :], decay_rate[:, :], ACT.Exp).then_inc(s_rate, 1)

            def raw(V, b, ct, first=False):
                act.wait_ge(s_px, V * CT + ct + 1)
                if not first:
                    act.wait_ge(s_conv, V * (CT * TAPS) - CT * TAPS + (ct + 1) * TAPS)
                if b > 0:
                    act.activation(xraw[:, b, ct, 0:HALO], xraw[:, b - 1, ct, BLK:BLK + HALO], ACT.Copy)
                act.activation(xraw[:, b, ct, HALO:], p_proj[:, ct, :], ACT.Copy).then_inc(s_xraw, 1)

            def silu_x(V, parity, ct):
                act.wait_ge(s_conv, V * (CT * TAPS) + (ct + 1) * TAPS)
                act.activation(xs[:, parity, ct, :], xs[:, parity, ct, :], ACT.Silu).then_inc(s_xs, 1)

            def silu_z(U, parity, ct, young=False):
                act.wait_ge(s_pz, U * CT + ct + 1)
                if not young:
                    act.wait_ge(s_sqs, U * CT - 2 * CT + ct + 1)
                act.activation(zs[:, parity, ct, :], p_proj[:, ct, :], ACT.Silu).then_inc(s_zs, 1)

            def gated(U, b, second=False):
                for ct in range(CT):
                    act.wait_ge(s_g, U * CT + ct + 1)
                    if not second:
                        act.wait_ge(s_pout, U * TPB)
                    act.activation(g_hi[:, ct, :], g[:, ct, :], ACT.Copy).then_inc(s_ghi, 1)
                for ct in range(CT):
                    act.activation(zs[:, b, ct, :], g[:, ct, :], ACT.Square).then_inc(s_sq, 1)

            def slot(k, gi, b, first=False, second=False, last=False):
                U, V = unit(k, gi, b)
                if not first:
                    gated(U - 1, 1 - b, second)
                if b == 0:
                    act.wait_ge(s_stage, gi + (k * G + 1))
                for c in range(CPB):
                    act.wait_ge(s_dec, U * CPB + c + 1)
                    if not (first and c < 2):
                        act.wait_ge(s_y2, U * CPB + c - 1)
                    for h in range(GH):
                        ins = act.activation(mix[:, c % 2, h, :], p_dec[:, h, :], ACT.Exp,
                                             bias=neg_cum_g[:, b * CPB + c, h:h + 1])
                    ins.then_inc(s_exp, 1)
                    if c < CT and not last:
                        raw(V + 1, 1 - b, c)
                if not last:
                    for ct in range(CT):
                        silu_x(V + 1, 1 - b, ct)
                    for ct in range(CT):
                        silu_z(U + 1, 1 - b, ct, first)

            for k in range(batches):
                lns.scalar(act, k)
                V0 = k * CONVS
                for b in range(NB):
                    for ct in range(CT):
                        raw(V0 + b, b, ct, first=b == 0 and k == 0)
                act.wait_ge(s_arg, (k + 1) * 4)
                act.activation(work[:, 0, :], work[:, 1, :], ACT.Exp).then_inc(s_u, 1)
                act.wait_ge(s_cumc, k + 1)
                act.activation(exp_cum[:, :, :], cum[:, :, :], ACT.Exp).then_inc(s_exps, 1)
                act.wait_ge(s_last, k + 1)
                act.activation(exp_last[:, :, :], p_st[:, :].rearrange("p (t h) -> p t h", t=T),
                               ACT.Exp).then_inc(s_exps, 1)
                act.wait_ge(s_clamp, (k + 1) * 2)
                act.activation(to_end[:, :, :], to_end[:, :, :], ACT.Exp).then_inc(s_exps, 1)
                act.wait_ge(s_partt, k * 2 + 1)
                act.activation(cum_hm[:, :], p_tr[:, :].bitcast(BF16), ACT.Copy).then_inc(s_partc, 1)
                act.wait_ge(s_partt, k * 2 + 2)
                act.activation(cum_l[:, :], p_dec[:, :, :].rearrange("p h c -> p (h c)").bitcast(BF16),
                               ACT.Copy).then_inc(s_partc, 1)
                for b in range(NB):
                    for ct in range(CT):
                        act.wait_ge(s_conv, (V0 + b) * (CT * TAPS) + (ct + 1) * TAPS)
                        c = slice(b * BLK, (b + 1) * BLK)
                        act.activation(bc[:, ct, c], bc[:, ct, c], ACT.Silu).then_inc(s_xs, 1)
                for j in range(2):
                    act.wait_ge(s_brow, k * 2 + j + 1)
                    act.activation(b_rows[:, 4 * j:4 * j + 4, :], (p_y_flat, p_st[:, :])[j].rearrange("p (t n) -> p t n", t=4),
                                   ACT.Copy).then_inc(s_browc, 1)
                U0, V0 = unit(k, 0, 0)
                for ct in range(CT):
                    raw(V0, 0, ct)
                for ct in range(CT):
                    silu_x(V0, 0, ct)
                for ct in range(CT):
                    silu_z(U0, 0, ct, True)
                slot(k, 0, 0, first=True)
                slot(k, 0, 1, second=True)
                with act.Fori(1, G - 1) as gi:
                    slot(k, gi, 0)
                    slot(k, gi, 1)
                slot(k, G - 1, 0)
                slot(k, G - 1, 1, last=True)
                gated((k + 1) * UNITS - 1, NB - 1)
                act.wait_ge(s_vara, k + 1)
                act.activation(root[:, :], var[:, :], ACT.Sqrt).then_inc(s_root, 1)

        @block.vector
        def _(dve):
            def conv(V, b, ct, tile, dst):
                n = V * (CT * TAPS) + ct * TAPS
                dve.wait_ge(s_xraw, V * CT + ct + 1)
                src = xraw[:, b, ct, :]
                tap = taps[:, bass.ds(tile, 1), :]
                dve.tensor_scalar(dst, src[:, HALO:HALO + BLK], tap[:, 0, HALO:HALO + 1],
                                  conv_bias[:, bass.ds(tile, 1)], ALU.mult, ALU.add).then_inc(s_conv, 1)
                for i in range(1, TAPS):
                    dve.wait_ge(s_conv, n + i)
                    j = HALO - i
                    dve.scalar_tensor_tensor(dst, src[:, j:j + BLK], tap[:, 0, j:j + 1], dst,
                                             ALU.mult, ALU.add).then_inc(s_conv, 1)

            def conv_x(k, gi, b, ct, young):
                U, V = unit(k, gi, b)
                if not young:
                    dve.wait_ge(s_skip, U * CT - 2 * CT + CT)
                conv(V, b, ct, gi * CT + ct, xs[:, b, ct, :])

            def gate(k, gi, b, first=False):
                U, V = unit(k, gi, b)
                for ct in range(CT):
                    dve.wait_ge(s_ytr, U * CT + ct + 1)
                    if not first:
                        dve.wait_ge(s_sq, U * CT - CT + ct + 1)
                        dve.wait_ge(s_glo, U * CT - CT + ct + 1)
                    dve.scalar_tensor_tensor(g[:, ct, :], xs[:, b, ct, :], skip[:, bass.ds(gi * CT + ct, 1)],
                                             (p_tr[:, :], p_out[:, 1, :])[ct], ALU.mult,
                                             ALU.add).then_inc(s_skip, 1)
                for ct in range(CT):
                    dve.wait_ge(s_skip, U * CT + ct + 1)
                    dve.wait_ge(s_zs, U * CT + ct + 1)
                    dve.tensor_tensor(g[:, ct, :], g[:, ct, :], zs[:, b, ct, :], ALU.mult).then_inc(s_g, 1)

            def gate_low(U):
                for ct in range(CT):
                    dve.wait_ge(s_ghi, U * CT + ct + 1)
                    dve.tensor_tensor(g_lo[:, ct, :], g[:, ct, :], g_hi[:, ct, :].bitcast(F32),
                                      ALU.subtract).then_inc(s_glo, 1)

            def accumulate(U, b, t):
                dve.wait_ge(s_pout, U * TPB + t + 1)
                tile = b * TPB + t
                dve.tensor_tensor(total[:, tile, :], p_out[:, t % 2, :], total[:, tile, :],
                                  ALU.add).then_inc(s_acc, 1)

            def stage(k, gi, first=False):
                heads = bass.ds(gi * GH, GH)
                U, _ = unit(k, gi, 0)
                if not first:
                    dve.wait_ge(s_exp, U * CPB)
                    dve.wait_ge(s_decayed, U * CPB)
                    dve.wait_ge(s_xend, U * 2)
                    dve.wait_ge(s_state, U * CPB)
                dve.memset(state[:, :, :], 0.0).then_inc(s_zero, 1)
                dve.tensor_scalar(neg_cum_g[:, :, :], cum[:, :, heads], -1.0, None, ALU.mult)
                dve.tensor_copy(exp_last_g[:, :, :], exp_last[:, :, heads])
                dve.tensor_copy(head_g[:, :], head_of[:, heads])
                dve.tensor_copy(to_end_g[:, :, :], to_end[:, :, heads]).then_inc(s_stage, 1)

            def slot(k, gi, b, first=False, second=False, last=False):
                U, V = unit(k, gi, b)
                heads = bass.ds(gi * GH, GH)
                gn, bn = (gi, 1) if b == 0 else (gi + 1, 0)
                gp, bp = (gi, 0) if b == 1 else (gi - 1, 1)
                if not first:
                    gate(k, gp, bp, first=second)
                if b == 0:
                    stage(k, gi, first)

                def times_dt(j):
                    dve.wait_ge(s_xtr, U * 2 + j + 1)
                    if not first:
                        dve.wait_ge(s_y2, U * CPB - CPB + 2 * j + 2)
                        dve.wait_ge(s_xend, U * 2 - 2 + j + 1)
                    c = b * CPB + 2 * j
                    dve.tensor_tensor(xdt[:, 2 * j:2 * j + 2, :, :],
                                      p_tr[:, :].rearrange("p (c h d) -> p c h d", c=2, h=GH),
                                      dt[:, c:c + 2, heads].unsqueeze(3).broadcast_to([P, 2, GH, HD]),
                                      ALU.mult).then_inc(s_xdt, 1)

                def decay_scores(c):
                    dve.wait_ge(s_exp, U * CPB + c + 1)
                    dve.scalar_tensor_tensor(mix[:, c % 2, :, :], mix[:, c % 2, :, :], 1.0,
                                             scores[:, b * CPB + c, :].unsqueeze(1).broadcast_to([P, GH, P]),
                                             ALU.min, ALU.mult).then_inc(s_mix, 1)

                def combine(c):
                    n = U * CPB + c
                    yc = y[:, c, :].rearrange("p (h d) -> p h d", h=GH)
                    dve.wait_ge(s_y2, n + 1)
                    dve.tensor_tensor(yc, p_y[:, 1, :, :],
                                      exp_cum[:, b * CPB + c, heads].unsqueeze(2).broadcast_to([P, GH, HD]),
                                      ALU.mult).then_inc(s_car, 1)
                    dve.wait_ge(s_st, n + 1)
                    dve.wait_ge(s_decayed, n + 1)
                    dve.tensor_tensor(state[:, :, :], p_st[:, 0:GC].rearrange("p (h d) -> p h d", h=GH),
                                      decayed[:, :, :], ALU.add).then_inc(s_state, 1)
                    dve.wait_ge(s_car, n + 1)
                    dve.tensor_tensor(yc, p_y[:, 0, :, :], yc, ALU.add).then_inc(s_y, 1)

                times_dt(0)
                decay_scores(0)
                if not first:
                    gate_low(U - 1)
                times_dt(1)
                decay_scores(1)
                if not last:
                    conv_x(k, gn, bn, 0, first)
                combine(0)
                decay_scores(2)
                if not last:
                    conv_x(k, gn, bn, 1, first)
                combine(1)
                decay_scores(3)
                combine(2)
                if not first:
                    accumulate(U - 1, bp, 0)
                    accumulate(U - 1, bp, 1)
                combine(3)
                if not first:
                    accumulate(U - 1, bp, 2)
                    accumulate(U - 1, bp, 3)
                if b == 0 and not first:
                    scale_out(k, gi)

            def scale_out(k, gi):
                for ct in range(CT):
                    dve.wait_ge(s_raw_out, (gi + k * G) * 16 + 16)
                    dve.tensor_scalar(raw_out[:, ct, :], raw_out[:, ct, :],
                                      norm_w[:, bass.ds(gi * CT + ct, 1)], None, ALU.mult).then_inc(s_scaled, 1)

            dve.wait_ge(s_small, SMALL)
            dve.wait_ge(s_const, 14)
            for k in range(batches):
                lns.x_tile = lambda t: x[:, k * T + t, :]
                lns.vector(dve, k)
                V0 = k * CONVS
                v, a, m = dt[:, :, :], work[:, 1, :].rearrange("p (t h) -> p t h", t=T), \
                    work[:, 2, :].rearrange("p (t h) -> p t h", t=T)
                u = work[:, 0, :].rearrange("p (t h) -> p t h", t=T)
                step = link(dve, s_arg, k * 4)
                dve.wait_ge(s_dt, k + 1)
                step(dve.tensor_tensor(v, p_dec[:, :, :].rearrange("p h c -> p (h c)").rearrange("p (t h) -> p t h", t=T),
                                       dt_bias[:, :].unsqueeze(1).broadcast_to([P, T, HEADS]), ALU.add))
                step(dve.tensor_scalar(a, v, -1.0, None, ALU.mult))
                step(dve.tensor_tensor(a, a, v, ALU.min))
                step(dve.tensor_scalar(m, v, 0.0, None, ALU.max))
                for b in range(NB):
                    for ct in range(CT):
                        conv(V0 + b, b, ct, DI // P + ct, bc[:, ct, b * BLK:(b + 1) * BLK])
                dve.wait_ge(s_u, k + 1)
                step = link(dve, s_soft, k * SOFT_STEPS)
                q, r = a, v
                step(dve.tensor_scalar(r, u, 2.0, None, ALU.add))
                step(dve.reciprocal(r, r))
                step(dve.tensor_tensor(u, u, r, ALU.mult))
                step(dve.tensor_tensor(q, u, u, ALU.mult))
                step(dve.tensor_scalar(r, q, 1.0 / 21, None, ALU.mult))
                for c in (19, 17, 15, 13, 11, 9, 7, 5, 3):
                    step(dve.scalar_tensor_tensor(r, r, 1.0 / c, q, ALU.add, ALU.mult))
                step(dve.scalar_tensor_tensor(r, r, 1.0, u, ALU.add, ALU.mult))
                step(dve.scalar_tensor_tensor(v, r, 2.0, m, ALU.mult, ALU.add))
                dve.wait_ge(s_rate, 1)
                step(dve.scalar_tensor_tensor(u, v, -1.0, decay_rate[:, :].unsqueeze(1).broadcast_to([P, T, HEADS]),
                                              ALU.mult, ALU.mult))
                dve.wait_ge(s_cum, k + 1)
                dve.tensor_copy(cum[:, :, :], p_y_flat.rearrange("p (t h) -> p t h", t=T)).then_inc(s_cumc, 1)
                dve.wait_ge(s_cumc, k + 1)
                step(dve.memset(part_l[:, :, 1, :], 0.0))
                step(dve.tensor_copy(part_hm[:, :, 0, :], cum[:, :, :]))
                step(dve.tensor_tensor(a, cum[:, :, :], part_hm[:, :, 0, :], ALU.subtract))
                dve.tensor_copy(part_hm[:, :, 1, :], a).then_inc(s_parts, 1)
                dve.wait_ge(s_parts, k * 2 + 1)
                dve.tensor_tensor(part_l[:, :, 0, :], a, part_hm[:, :, 1, :], ALU.subtract).then_inc(s_parts, 1)
                dve.wait_ge(s_last, k + 1)
                step = link(dve, s_clamp, k * 2)
                dve.wait_ge(s_exps, k * 3 + 2)
                step(dve.tensor_tensor(to_end[:, :, :], p_st[:, :].rearrange("p (t h) -> p t h", t=T),
                                       cum[:, :, :], ALU.subtract))
                step(dve.tensor_scalar(to_end[:, :, :], to_end[:, :, :], 0.0, None, ALU.min))
                for j in range(2):
                    dve.wait_ge(s_score, k * 2 + j + 1)
                    dve.tensor_tensor(scores[:, 4 * j:4 * j + 4, :], p_out[:, j, :].rearrange("p (t l) -> p t l", t=4),
                                      causal[:, :].unsqueeze(1).broadcast_to([P, 4, P]),
                                      ALU.mult).then_inc(s_scorec, 1)
                dve.wait_ge(s_exps, k * 3 + 3)
                for ct in range(CT):
                    conv_x(k, 0, 0, ct, True)
                scale_out(k, 0)
                dve.wait_ge(s_clear, (k + 1) * 2)
                slot(k, 0, 0, first=True)
                slot(k, 0, 1, second=True)
                with dve.Fori(1, G - 1) as gi:
                    slot(k, gi, 0)
                    slot(k, gi, 1)
                slot(k, G - 1, 0)
                slot(k, G - 1, 1, last=True)
                U = (k + 1) * UNITS - 1
                gate(k, G - 1, NB - 1)
                gate_low(U)
                for t in range(TPB):
                    accumulate(U, NB - 1, t)
                dve.wait_ge(s_var, k + 1)
                dve.tensor_scalar(var[:, :], p_y_flat[:, 0:2 * T].rearrange("p (t a) -> p t a", a=2)[:, :, 0],
                                  1.0 / DI, RMS_EPS, ALU.mult, ALU.add).then_inc(s_vara, 1)
                dve.wait_ge(s_root, k + 1)
                refine_rsqrt(dve, link(dve, s_fin, k * FIN_STEPS), rstd[:, :], root[:, :], var[:, :], tmp[:, :])
                for t in range(T):
                    dve.scalar_tensor_tensor(x[:, k * T + t, :], total[:, t, :], rstd[:, t:t + 1],
                                             x[:, k * T + t, :], ALU.mult, ALU.add).then_inc(s_add, 1)

        @block.tensor
        def _(pe):
            def project(bank, piece, b):
                c = slice(b * BLK, (b + 1) * BLK)
                for kk in range(KT):
                    pe.matmul(bank, in_hi[:, piece, kk, :], xt_lo[:, kk, c], start=(kk == 0), stop=False)
                    pe.matmul(bank, in_hi[:, piece, kk, :], xt_hi[:, kk, c], start=False, stop=False)
                    last = pe.matmul(bank, in_lo[:, piece, kk, :], xt_hi[:, kk, c], start=False,
                                     stop=(kk == KT - 1))
                return last

            def project_x(k, gi, b, ct, first=False):
                U, V = unit(k, gi, b)
                if first:
                    pe.wait_ge(s_xraw, V * CT - CT + ct + 1)
                else:
                    pe.wait_ge(s_zs, U * CT - CT + ct + 1)
                if b == 0:
                    pe.wait_ge(s_split_x, (gi + (k * (G + 1) + 1)) * 4 + 2 * ct + 2)
                project(p_proj[:, ct, :], ct, b).then_inc(s_px, 1)

            def project_z(k, gi, b, ct):
                U, V = unit(k, gi, b)
                pe.wait_ge(s_xraw, V * CT + ct + 1)
                if b == 0:
                    pe.wait_ge(s_split_z, gi * 4 + (k * (4 * G + 2) + 2 * ct + 4))
                project(p_proj[:, ct, :], CT + ct, b).then_inc(s_pz, 1)

            def project_out(k, gi, b, tiles, first=False):
                U, _ = unit(k, gi, b)
                for t in tiles:
                    if t == 0:
                        pe.wait_ge(s_glo, U * CT + CT)
                        if b == 0:
                            pe.wait_ge(s_split_out, (gi + k * G) * 4 + 4)
                    if t >= 2:
                        pe.wait_ge(s_acc, U * TPB + t - 1)
                    elif not first:
                        pe.wait_ge(s_acc, U * TPB)
                    c = slice(t * P, (t + 1) * P)
                    for ct in range(CT):
                        pe.matmul(p_out[:, t % 2, :], g_hi[:, ct, c], out_lo[:, ct, :], start=(ct == 0), stop=False)
                        pe.matmul(p_out[:, t % 2, :], g_hi[:, ct, c], out_hi[:, ct, :], start=False, stop=False)
                        last = pe.matmul(p_out[:, t % 2, :], g_lo[:, ct, c], out_hi[:, ct, :], start=False,
                                         stop=(ct == CT - 1))
                    last.then_inc(s_pout, 1)

            def slot(k, gi, b, first=False, second=False, last=False):
                U, V = unit(k, gi, b)
                gn, bn = (gi, 1) if b == 0 else (gi + 1, 0)
                gp, bp = (gi, 0) if b == 1 else (gi - 1, 1)

                def rows(j):
                    if j == 0:
                        pe.wait_ge(s_xs, V * CT + CT)
                        if not first:
                            pe.wait_ge(s_skip, U * CT - CT + 1)
                    else:
                        pe.wait_ge(s_xdt, U * 2 + j)
                    for c in range(2):
                        for ct in range(CT):
                            s = (2 * j + c) * P
                            mm = pe.transpose(p_tr[:, c * GC + ct * P:c * GC + (ct + 1) * P],
                                              xs[:, b, ct, s:s + P], ident[:, :])
                    mm.then_inc(s_xtr, 1)

                def spread(c):
                    if not (first and c == 0):
                        pe.wait_ge(s_exp, U * CPB + c)
                    if b == 0 and c == 0:
                        pe.wait_ge(s_stage, gi + (k * G + 1))
                    s = (b * CPB + c) * P
                    pe.matmul(p_dec[:, :, :], ident16[:, :], never[:, :].unsqueeze(1).broadcast_to([P, GH, P]),
                              start=True, stop=False)
                    for h in range(GH):
                        sel = head_g[:, h:h + 1].broadcast_to([P, P])
                        pe.matmul(p_dec[:, h, :], sel, cum_hm[:, s:s + P], start=False, stop=False)
                        mm = pe.matmul(p_dec[:, h, :], sel, cum_l[:, s:s + P], start=False,
                                       stop=h == GH - 1)
                    mm.then_inc(s_dec, 1)

                def recur(c):
                    s = (b * CPB + c) * P
                    if not (first and c == 0):
                        pe.wait_ge(s_y, U * CPB + c)
                        pe.wait_ge(s_state, U * CPB + c)
                    pe.wait_ge(s_mix, U * CPB + c + 1)
                    pe.matmul(p_y[:, 1, :, :], bc[:, 1, s:s + P], state[:, :, :], start=True, stop=True)
                    for h in range(GH):
                        mm = pe.matmul(p_y[:, 0, h, :], mix[:, c % 2, h, :], xdt[:, c, h, :], start=True, stop=True)
                    mm.then_inc(s_y2, 1)
                    if c % 2 == 0:
                        pe.wait_ge(s_xend, U * 2 + c // 2 + 1)
                    pe.matmul(p_st[:, 0:GC], b_rows[:, b * CPB + c, :],
                              xend[:, c, :, :].rearrange("p h d -> p (h d)"), start=True,
                              stop=True).then_inc(s_st, 1)

                def columns(ct):
                    if ct == 0:
                        pe.wait_ge(s_y, U * CPB + CPB)
                        pe.wait_ge(s_xdt, U * 2 + 2)
                    elif not first:
                        pe.wait_ge(s_acc, U * TPB)
                    for c in range(CPB):
                        mm = pe.transpose((p_tr[:, :], p_out[:, 1, :])[ct][:, c * P:(c + 1) * P],
                                          y[:, c, ct * P:(ct + 1) * P], ident[:, :])
                    mm.then_inc(s_ytr, 1)

                rows(0)
                spread(0)
                if not last:
                    project_x(k, gn, bn, 0)
                rows(1)
                spread(1)
                recur(0)
                if not last:
                    project_x(k, gn, bn, 1)
                spread(2)
                recur(1)
                if not last:
                    project_z(k, gn, bn, 0)
                spread(3)
                recur(2)
                if not last:
                    project_z(k, gn, bn, 1)
                if not first:
                    project_out(k, gp, bp, (0, 1), first=second)
                recur(3)
                if not first:
                    project_out(k, gp, bp, (2, 3))
                for ct in range(CT):
                    columns(ct)

            pe.wait_ge(s_const, 14)
            for k in range(batches):
                lns.tensor(pe, k)
                pe.wait_ge(lns.s_lo, (k + 1) * T)
                pe.wait_ge(s_split_z, k * (4 * G + 2) + 2)
                p_dt = p_dec[:, :, :].rearrange("p h c -> p (h c)")
                for t in range(T):
                    c = slice(t * P, (t + 1) * P)
                    for kk in range(KT):
                        for j, (a, ww) in enumerate([(xt_lo, in_hi), (xt_hi, in_lo), (xt_hi, in_hi)]):
                            mm = pe.matmul(p_dt[:, t * HEADS:(t + 1) * HEADS], a[:, kk, c], ww[:, CT, kk, 0:HEADS],
                                           start=(kk == 0 and j == 0), stop=(kk == KT - 1 and j == 2))
                mm.then_inc(s_dt, 1)
                V0 = k * CONVS
                pe.wait_ge(s_split_x, k * (G + 1) * 4 + 4)
                for b in range(NB):
                    for ct in range(CT):
                        if b > 0:
                            pe.wait_ge(s_xraw, (V0 + b - 1) * CT + ct + 1)
                        project(p_proj[:, ct, :], ct, b).then_inc(s_px, 1)
                pe.wait_ge(s_soft, k * SOFT_STEPS + SOFT_STEPS - 3)
                pe.matmul(p_y_flat, causal[:, :], work[:, 0, :], start=True, stop=True).then_inc(s_cum, 1)
                pe.wait_ge(s_cumc, k + 1)
                pe.matmul(p_st[:, :], ident[:, P - 1:P].broadcast_to([P, P]), cum[:, :, :].rearrange("p t h -> p (t h)"),
                          start=True, stop=True).then_inc(s_last, 1)
                for j, (part, bank) in enumerate([(part_hm, p_tr[:, :].bitcast(BF16)),
                                                  (part_l, p_dt.bitcast(BF16))]):
                    pe.wait_ge(s_parts, k * 2 + j + 1)
                    for t in range(T):
                        mm = pe.transpose(bank[:, t * P:(t + 1) * P],
                                          part[:, t, :, :].rearrange("p a h -> p (a h)"), ident16[:, :])
                    mm.then_inc(s_partt, 1)
                pe.wait_ge(s_xs, (V0 + NB) * CT)
                pe.wait_ge(s_clamp, (k + 1) * 2)
                for j in range(2):
                    bank = (p_y_flat, p_st[:, :])[j]
                    for t in range(4):
                        s = (4 * j + t) * P
                        mm = pe.transpose(bank[:, t * P:(t + 1) * P], bc[:, 0, s:s + P], ident[:, :])
                    mm.then_inc(s_brow, 1)
                for j in range(2):
                    for t in range(4):
                        s = (4 * j + t) * P
                        mm = pe.matmul(p_out[:, j, t * P:(t + 1) * P], bc[:, 0, s:s + P], bc[:, 1, s:s + P],
                                       start=True, stop=True)
                    mm.then_inc(s_score, 1)
                for ct in range(CT):
                    project_x(k, 0, 0, ct, first=True)
                for ct in range(CT):
                    project_z(k, 0, 0, ct)
                pe.wait_ge(s_browc, (k + 1) * 2)
                slot(k, 0, 0, first=True)
                slot(k, 0, 1, second=True)
                with pe.Fori(1, G - 1) as gi:
                    slot(k, gi, 0)
                    slot(k, gi, 1)
                slot(k, G - 1, 0)
                slot(k, G - 1, 1, last=True)
                project_out(k, G - 1, NB - 1, range(TPB))
                pe.wait_ge(s_sqs, (k + 1) * UNITS * CT)
                for t in range(T):
                    mm = pe.matmul(p_y_flat[:, 2 * t:2 * t + 2], square_sum[:, t * P:(t + 1) * P], ones[:, :],
                                   start=True, stop=True)
                mm.then_inc(s_var, 1)



def macaron_block(nc, hidden, ffn, mamba, out):
    batches, length, _ = hidden.shape
    tiles = batches * length // P
    with nc.sbuf_tensor("x", [P, tiles, D], F32) as x:
        ffn_phase(nc, "ffn1", x, hidden, ffn, None)
        mamba_phase(nc, "mamba", x, batches, mamba)
        ffn_phase(nc, "ffn2", x, None, ffn, out)



_FFN = ["wg", "wu", "wd", "sg_w", "sg_b", "su_w", "su_b", "sd_w", "sd_b"]
_MAMBA = ["conv_w", "conv_b", "dt_bias", "A_log", "D_param", "norm_w"]


def kernel(**inputs):
    import numpy as np
    import concourse.bacc as bacc
    from concourse.bass_utils import run_bass_kernel_spmd

    nc = bacc.Bacc("TRN2", target_bir_lowering=False, num_devices=1)
    arrays = {}

    def give(name, a):
        arrays[name] = np.ascontiguousarray(a)
        return nc.dram_tensor(name, arrays[name].shape, mybir.dt.from_np(arrays[name].dtype),
                              kind="ExternalInput").ap()

    hidden = give("hidden", inputs["L0_attn_hidden_states"])
    ffn = {n: give(n, inputs["L0_ffn_" + n]) for n in _FFN}
    ffn["router_t"] = give("router_t", np.asarray(inputs["L0_ffn_router_w"]).T)
    mamba = {n: give(n, inputs["L0_attn_" + n]) for n in _MAMBA}
    mamba["in_t"] = give("in_t", np.asarray(inputs["L0_attn_W_in"]).T)
    mamba["out_t"] = give("out_t", np.asarray(inputs["L0_attn_W_out"]).T)
    out = nc.dram_tensor("out", hidden.shape, F32, kind="ExternalOutput").ap()
    macaron_block(nc, hidden, ffn, mamba, out)
    result = run_bass_kernel_spmd(nc, [arrays], core_ids=[0])
    return result.results[0]["out"]
```

```python
from contextlib import ExitStack

import concourse.bass as bass
from concourse import mybir

F32 = mybir.dt.float32
F32R = mybir.dt.float32r
BF16 = mybir.dt.bfloat16
ALU = mybir.AluOpType
ACT = mybir.ActivationFunctionType
AX = mybir.AxisListType


P = 128
D = 512
KT = D // P
BLK = 512
TPB = BLK // P
LN_EPS = 1e-5


class Sems:

    def __init__(self, nc, ctx, phase):
        self.nc, self.ctx, self.phase = nc, ctx, phase

    def __call__(self, name):
        return self.ctx.enter_context(self.nc.semaphore(f"{self.phase}_{name}"))


def link(eng, sem, base=0):
    n = [0]

    def done(ins):
        n[0] += 1
        ins.then_inc(sem, 1)
        eng.wait_ge(sem, base + n[0])

    return done



class LayerNorm:

    def __init__(self, nc, ctx, sem, tiles, x_tile, xt_hi, xt_lo, ident, psum, xn=None):
        self.tiles, self.blocks = tiles, tiles // TPB
        self.x_tile, self.xt_hi, self.xt_lo, self.ident, self.psum = x_tile, xt_hi, xt_lo, ident, psum

        def sb(name, shape):
            return ctx.enter_context(nc.sbuf_tensor(f"{sem.phase}_{name}", shape, F32))

        self.stat = sb("ln_stats", [P, 2, 6])
        self.moments = sb("ln_moments", [P, tiles, 2])
        self.var = sb("ln_var", [P, tiles])
        self.roots = sb("ln_root", [P, tiles])
        self.rstd = sb("ln_rstd", [P, tiles])
        self.tmp = sb("ln_tmp", [P, tiles])
        self.xn = sb("ln_xn", [P, 2, D]) if xn is None else xn
        self.s_stat, self.s_var, self.s_root = sem("ln_stat"), sem("ln_var"), sem("ln_root")
        self.s_chain, self.s_xn, self.s_tr = sem("ln_chain"), sem("ln_xn"), sem("ln_tr")
        self.s_hi, self.s_lo = sem("ln_hi"), sem("ln_lo")

    def stats(self, eng, call, b, loaded=None):
        if loaded is not None:
            eng.wait_ge(loaded[b], 16)
        n = call * (2 * self.tiles) + b * (2 * TPB)
        for t in range(b * TPB, b * TPB + TPB):
            eng.bn_stats(self.stat[:, t % 2, :], self.x_tile(t)).then_inc(self.s_stat, 1)
            eng.wait_ge(self.s_stat, n + 1)
            eng.bn_aggr(self.moments[:, t, :], self.stat[:, t % 2, :]).then_inc(self.s_stat, 1)
            n += 2
        eng.wait_ge(self.s_stat, n)
        s = slice(b * TPB, b * TPB + TPB)
        eng.tensor_scalar(self.var[:, s], self.moments[:, s, 1], LN_EPS, None,
                          ALU.add).then_inc(self.s_var, 1)

    def root(self, eng, call, b):
        s = slice(b * TPB, b * TPB + TPB)
        eng.wait_ge(self.s_var, call * self.blocks + b + 1)
        eng.activation(self.roots[:, s], self.var[:, s], ACT.Sqrt).then_inc(self.s_root, 1)

    def normalise(self, eng, call, b):
        T = self.tiles
        s = slice(b * TPB, b * TPB + TPB)
        eng.wait_ge(self.s_root, call * self.blocks + b + 1)
        refine_rsqrt(eng, link(eng, self.s_chain, (call * self.blocks + b) * 5), self.rstd[:, s],
                     self.roots[:, s], self.var[:, s], self.tmp[:, s])

        def low(t):
            eng.wait_ge(self.s_hi, call * T + t + 1)
            c = slice(t * P, t * P + P)
            eng.tensor_tensor(self.xt_lo[:, :, c], self.psum(t), self.xt_hi[:, :, c].bitcast(F32),
                              ALU.subtract).then_inc(self.s_lo, 1)

        for t in range(b * TPB, b * TPB + TPB):
            if t >= 2:
                eng.wait_ge(self.s_tr, call * T + t - 1)
            eng.tensor_scalar(self.xn[:, t % 2, :], self.x_tile(t), self.moments[:, t, 0:1],
                              self.rstd[:, t:t + 1], ALU.subtract, ALU.mult).then_inc(self.s_xn, 1)
            if t > b * TPB:
                low(t - 1)
        low(b * TPB + TPB - 1)

    def high(self, eng, call, tiles):
        for t in tiles:
            eng.wait_ge(self.s_tr, call * self.tiles + t + 1)
            eng.activation(self.xt_hi[:, :, t * P:(t + 1) * P], self.psum(t), ACT.Copy).then_inc(self.s_hi, 1)

    def transposes(self, eng, call, tiles):
        T = self.tiles
        for t in tiles:
            eng.wait_ge(self.s_xn, call * T + t + 1)
            if t >= 2:
                eng.wait_ge(self.s_lo, call * T + t - 1)
            for k in range(KT):
                last = eng.transpose(self.psum(t)[:, k, :], self.xn[:, t % 2, k * P:(k + 1) * P],
                                     self.ident)
            last.then_inc(self.s_tr, 1)


def refine_rsqrt(eng, chain, r, root, v, tmp):
    chain(eng.reciprocal(r, root))
    chain(eng.tensor_tensor(tmp, r, r, ALU.mult))
    chain(eng.tensor_tensor(tmp, tmp, v, ALU.mult))
    chain(eng.tensor_scalar(tmp, tmp, -0.5, 1.5, ALU.mult, ALU.add))
    chain(eng.tensor_tensor(r, r, tmp, ALU.mult))


def build_identity(pool, ident, sem, at):
    pool.memset(ident, 0.0).then_inc(sem, 1)
    pool.wait_ge(sem, at + 1)
    pool.affine_select(out=ident, in_=ident, compare_op=ALU.not_equal, fill=1.0, base=0,
                       pattern=[[-1, P]], channel_multiplier=1).then_inc(sem, 1)



def ffn_phase(nc, phase, x, hidden, w, out):
    E, _, I = w["wg"].shape
    IT = I // P
    T = x.shape[1]
    NB = T // TPB
    PAIR = 2 * NB
    LAST = E * NB + NB - 1
    ctx = ExitStack()
    with ctx:
        sem = Sems(nc, ctx, phase)

        def sb(name, shape, dt=F32):
            return ctx.enter_context(nc.sbuf_tensor(f"{phase}_{name}", shape, dt))

        def ps(name, shape):
            return ctx.enter_context(nc.psum_tensor(f"{phase}_{name}", shape, F32))

        xt_hi, xt_lo = sb("xt_hi", [P, KT, T * P], F32R), sb("xt_lo", [P, KT, T * P], F32R)
        ident = sb("ident", [P, P])
        raw_in = sb("raw_in", [P, 2, KT, I])
        raw_out = sb("raw_out", [P, IT, D])
        in_hi, in_lo = sb("in_hi", [P, 2, 2, KT, I], F32R), sb("in_lo", [P, 2, 2, KT, I], F32R)
        out_hi, out_lo = sb("out_hi", [P, 2, IT, D], F32R), sb("out_lo", [P, 2, IT, D], F32R)
        sil = sb("sil", [P, IT, BLK])
        h = sb("h", [P, IT, BLK])
        h_hi, h_lo = sb("h_hi", [P, 2, IT, BLK], F32R), sb("h_lo", [P, 2, IT, BLK], F32R)
        router = sb("router", [P, KT, E])
        router_hi, router_lo = sb("router_hi", [P, KT, E], F32R), sb("router_lo", [P, KT, E], F32R)
        gate_bias, up_bias = sb("gate_bias", [P, IT]), sb("up_bias", [P, IT])
        one = sb("one", [P, 1])
        down_bias = sb("down_bias", [P, D])
        logits_t = sb("logits_t", [E, BLK])
        logits = sb("logits", [P, T, E])
        above = sb("above", [P, T, E, E])
        equal = sb("equal", [P, T, E, E])
        earlier = sb("earlier", [P, E, E])
        rank = sb("rank", [P, T, E])
        chosen = sb("chosen", [P, T, E])
        weight = sb("weight", [P, (E + 1) * T])

        p_gate, p_up = ps("p_gate", [P, IT, BLK]), ps("p_up", [P, IT, BLK])
        p_down = ps("p_down", [P, TPB, D])
        p_logits_t = p_down[0:E, 2, :]
        p_logits = p_down[:, 3, 0:TPB * E]

        s_const, s_small, s_route = sem("const"), sem("small"), sem("route")
        s_x = [sem(f"x{b}") for b in range(NB)]
        s_raw_in, s_raw_out, s_split = sem("raw_in"), sem("raw_out"), sem("split")
        s_gate, s_up, s_down = sem("gate"), sem("up"), sem("down")
        s_sil, s_h, s_hi, s_lo, s_acc = sem("sil"), sem("h"), sem("hi"), sem("lo"), sem("acc")
        s_bias, s_rank, s_weight, s_out = sem("bias"), sem("rank"), sem("weight"), sem("out")
        s_lgt, s_lgt_copy, s_lg, s_lg_copy = sem("lgt"), sem("lgt_copy"), sem("lg"), sem("lg_copy")
        SPLITS = 6

        ln = LayerNorm(nc, ctx, sem, T, lambda t: x[:, t, :], xt_hi, xt_lo, ident[:, :],
                       lambda t: p_down[:, t % 2, :].rearrange("p (k c) -> p k c", k=KT))

        block = ctx.enter_context(nc.Block())

        @block.sync
        def _(sp):
            if hidden is not None:
                rows = hidden.rearrange("a (t p) d -> p a t d", p=P)
                per = rows.shape[2]
                for b in range(NB):
                    a, t = b * TPB // per, b * TPB % per
                    sp.dma_start(x[:, b * TPB:(b + 1) * TPB, :],
                                 rows[:, a, t:t + TPB, :]).then_inc(s_x[b], 16)

            def load(turn, gate, up, down, first=False):
                if not first:
                    sp.wait_ge(s_split, turn * SPLITS - 2)
                sp.dma_start(raw_in[:, 0, :, :], gate.rearrange("(k p) i -> p k i", p=P)).then_inc(s_raw_in, 16)
                sp.dma_start(raw_in[:, 1, :, :], up.rearrange("(k p) i -> p k i", p=P)).then_inc(s_raw_in, 16)
                if not first:
                    sp.wait_ge(s_split, turn * SPLITS)
                sp.dma_start(raw_out[:, :, :], down.rearrange("(k p) d -> p k d", p=P)).then_inc(s_raw_out, 16)

            with nc.allow_non_contiguous_dma(reason="short vectors, once"):
                sp.dma_start(router[:, :, :], w["router_t"].rearrange("(k p) e -> p k e", p=P)).then_inc(s_small, 16)
                sp.dma_start(down_bias[:, :], w["sd_b"].partition_broadcast(P)).then_inc(s_small, 16)
                sp.dma_start(gate_bias[:, :], w["sg_b"].rearrange("(i p) -> p i", p=P)).then_inc(s_small, 16)
                sp.dma_start(up_bias[:, :], w["su_b"].rearrange("(i p) -> p i", p=P)).then_inc(s_small, 16)
            load(0, w["sg_w"], w["su_w"], w["sd_w"], first=True)
            with sp.Fori(0, E) as e:
                load(e + 1, w["wg"][e], w["wu"][e], w["wd"][e])
            if out is not None:
                rows = out.rearrange("a (t p) d -> p a t d", p=P)
                per = rows.shape[2]
                for b in range(NB):
                    a, t = b * TPB // per, b * TPB % per
                    sp.wait_ge(s_acc, (E * NB + b + 1) * TPB)
                    sp.dma_start(rows[:, a, t:t + TPB, :],
                                 x[:, b * TPB:(b + 1) * TPB, :]).then_inc(s_out, 16)
                sp.wait_ge(s_out, 16 * NB)

        @block.gpsimd
        def _(pool):
            build_identity(pool, ident[:, :], s_const, 0)
            pool.memset(one[:, :], 1.0).then_inc(s_const, 1)
            pool.memset(weight[:, E * T:(E + 1) * T], 0.5).then_inc(s_const, 1)
            pool.memset(earlier[:, :, :], 0.0).then_inc(s_const, 1)
            pool.wait_ge(s_const, 5)
            pool.affine_select(out=earlier[:, :, :], in_=earlier[:, :, :], compare_op=ALU.is_ge, fill=1.0,
                               base=0, pattern=[[-1, E], [1, E]], channel_multiplier=0).then_inc(s_const, 1)
            pool.wait_ge(s_small, 64)
            pool.tensor_copy(router_hi[:, :, :], router[:, :, :]).then_inc(s_route, 1)
            pool.wait_ge(s_route, 1)
            pool.tensor_tensor(router_lo[:, :, :], router[:, :, :], router_hi[:, :, :].bitcast(F32),
                               ALU.subtract).then_inc(s_route, 1)
            pool.tensor_scalar(down_bias[:, :], down_bias[:, :], 0.5, None, ALU.mult).then_inc(s_route, 1)

            def split(turn, parity, behind):
                n = [0]

                def part(hi, lo, raw):
                    pool.tensor_tensor(hi, raw, one[:, :].broadcast_to(raw.shape) if len(raw.shape) == 2 else
                                       one[:, :].unsqueeze(1).broadcast_to(raw.shape),
                                       ALU.mult).then_inc(s_split, 1)
                    n[0] += 1
                    pool.wait_ge(s_split, turn * SPLITS + n[0])
                    pool.tensor_tensor(lo, raw, hi.bitcast(F32), ALU.subtract).then_inc(s_split, 1)
                    n[0] += 1

                if behind:
                    pool.wait_ge(s_down, (turn - 1) * NB * TPB)
                for j in range(2):
                    pool.wait_ge(s_raw_in, turn * 32 + 32)
                    part(in_hi[:, parity, j, :, :], in_lo[:, parity, j, :, :], raw_in[:, j, :, :])
                pool.wait_ge(s_raw_out, turn * 16 + 16)
                part(out_hi[:, parity, :, :], out_lo[:, parity, :, :], raw_out[:, :, :])

            split(0, 0, behind=False)
            pool.wait_ge(s_route, 3)
            for t in range(T):
                pool.wait_ge(ln.s_xn, t + 1)
                pool.tensor_tensor(x[:, t, :], x[:, t, :], down_bias[:, :], ALU.add).then_inc(s_bias, 1)
            split(1, 1, behind=False)
            with pool.Fori(1, E // 2) as i:
                split(i * 2, 0, behind=True)
                split(i * 2 + 1, 1, behind=True)
            split(E, 0, behind=True)

        @block.scalar
        def _(act):
            def silu(unit, i, bias=None, first=False):
                act.wait_ge(s_gate, unit * IT + i + 1)
                if not first:
                    act.wait_ge(s_h, unit * IT - IT + i + 1)
                act.activation(sil[:, i, :], p_gate[:, i, :], ACT.Silu,
                               bias=0.0 if bias is None else bias[:, i:i + 1]).then_inc(s_sil, 1)

            def high(unit, parity, first=False):
                for i in range(IT):
                    act.wait_ge(s_h, unit * IT + i + 1)
                    if not first:
                        act.wait_ge(s_down, unit * TPB - TPB)
                    act.activation(h_hi[:, parity, i, :], h[:, i, :], ACT.Copy).then_inc(s_hi, 1)

            def gate(unit, parity):
                for i in range(IT):
                    silu(unit, i)
                high(unit, parity)

            def logits_columns(b):
                act.wait_ge(s_lgt, b + 1)
                act.activation(logits_t[:, :], p_logits_t, ACT.Copy).then_inc(s_lgt_copy, 1)

            def logits_rows(b):
                act.wait_ge(s_lg, b + 1)
                act.activation(logits[:, b * TPB:(b + 1) * TPB, :],
                               p_logits.rearrange("p (t e) -> p t e", t=TPB), ACT.Copy).then_inc(s_lg_copy, 1)

            act.wait_ge(s_small, 64)
            ln.root(act, 0, 0)
            ln.root(act, 0, 1)
            ln.high(act, 0, range(TPB))
            logits_columns(0)
            for b in range(NB - 1):
                nxt = (b + 1) * TPB
                silu(b, 0, gate_bias, first=b == 0)
                logits_rows(b)
                ln.high(act, 0, range(nxt, nxt + 2))
                silu(b, 1, gate_bias, first=b == 0)
                ln.high(act, 0, range(nxt + 2, nxt + TPB))
                if b + 2 < NB:
                    ln.root(act, 0, b + 2)
                    high(b, b % 2, first=b < 2)
                logits_columns(b + 1)
            logits_rows(NB - 1)
            high(NB - 2, NB % 2)
            for i in range(IT):
                silu(NB - 1, i, gate_bias)
            high(NB - 1, (NB - 1) % 2)
            with act.Fori(0, E // 2) as i:
                for u in range(PAIR):
                    gate(i * PAIR + NB + u, u % 2)

        @block.vector
        def _(dve):
            def inner(unit, parity, bias=None, first=False):
                for i in range(IT):
                    dve.wait_ge(s_up, unit * IT + i + 1)
                    dve.wait_ge(s_sil, unit * IT + i + 1)
                    if not first:
                        dve.wait_ge(s_lo, unit * IT - IT + i + 1)
                    if bias is None:
                        dve.tensor_tensor(h[:, i, :], p_up[:, i, :], sil[:, i, :], ALU.mult).then_inc(s_h, 1)
                    else:
                        dve.scalar_tensor_tensor(h[:, i, :], p_up[:, i, :], bias[:, i:i + 1], sil[:, i, :],
                                                 ALU.add, ALU.mult).then_inc(s_h, 1)
                for i in range(IT):
                    dve.wait_ge(s_hi, unit * IT + i + 1)
                    dve.tensor_tensor(h_lo[:, parity, i, :], h[:, i, :],
                                      h_hi[:, parity, i, :].bitcast(F32), ALU.subtract).then_inc(s_lo, 1)

            def accumulate(unit, e, b):
                for t in range(TPB):
                    tile = b * TPB + t
                    dve.wait_ge(s_down, unit * TPB + t + 1)
                    dve.scalar_tensor_tensor(x[:, tile, :], p_down[:, t, :],
                                             weight[:, bass.ds(e * T + tile, 1)], x[:, tile, :],
                                             ALU.mult, ALU.add).then_inc(s_acc, 1)

            SHARED = E
            loaded = s_x if hidden is not None else None
            ln.stats(dve, 0, 0, loaded)
            ln.stats(dve, 0, 1, loaded)
            ln.normalise(dve, 0, 0)
            dve.wait_ge(s_small, 64)
            for b in range(NB - 1):
                if b + 2 < NB:
                    ln.stats(dve, 0, b + 2, loaded)
                ln.normalise(dve, 0, b + 1)
                inner(b, b % 2, up_bias, first=b == 0)
            dve.wait_ge(s_bias, T)
            dve.wait_ge(s_const, 6)
            accumulate(0, SHARED, 0)
            inner(NB - 1, (NB - 1) % 2, up_bias)
            for b in range(1, NB - 1):
                accumulate(b, SHARED, b)
            dve.wait_ge(s_lg_copy, NB)
            l_f = logits[:, :, :].unsqueeze(2).broadcast_to([P, T, E, E])
            l_e = logits[:, :, :].unsqueeze(3).broadcast_to([P, T, E, E])
            dve.tensor_tensor(above[:, :, :, :], l_f, l_e, ALU.is_gt).then_inc(s_rank, 1)
            dve.tensor_tensor(equal[:, :, :, :], l_f, l_e, ALU.is_equal).then_inc(s_rank, 1)
            dve.wait_ge(s_rank, 2)
            dve.tensor_tensor(equal[:, :, :, :], equal[:, :, :, :],
                              earlier[:, :, :].unsqueeze(1).broadcast_to([P, T, E, E]),
                              ALU.mult).then_inc(s_rank, 1)
            dve.wait_ge(s_rank, 3)
            dve.tensor_tensor(above[:, :, :, :], above[:, :, :, :], equal[:, :, :, :],
                              ALU.add).then_inc(s_rank, 1)
            dve.wait_ge(s_rank, 4)
            dve.tensor_reduce(rank[:, :, :], above[:, :, :, :], AX.X, ALU.add).then_inc(s_rank, 1)
            dve.wait_ge(s_rank, 5)
            dve.tensor_scalar(chosen[:, :, :], rank[:, :, :], 2.0, 0.5, ALU.is_lt,
                              ALU.mult).then_inc(s_rank, 1)
            dve.wait_ge(s_rank, 6)
            dve.tensor_tensor(weight[:, 0:E * T].rearrange("p (e t) -> p t e", e=E), chosen[:, :, :],
                              logits[:, :, :], ALU.mult).then_inc(s_weight, 1)
            dve.wait_ge(s_weight, 1)

            inner(NB, NB % 2)
            accumulate(NB - 1, SHARED, NB - 1)
            with dve.Fori(0, E // 2 - 1) as i:
                for u in range(1, PAIR + 1):
                    inner(i * PAIR + NB + u, u % 2)
                    accumulate(i * PAIR + NB + u - 1, i * 2 + (u - 1) // NB, (u - 1) % NB)
            for n in range(LAST - PAIR + 2, LAST + 2):
                if n <= LAST:
                    inner(n, n % 2)
                accumulate(n - 1, (n - 1) // NB - 1, (n - 1) % NB)

        @block.tensor
        def _(pe):
            pe.wait_ge(s_const, 2)
            def inner(unit, turn, parity, b, first=False, tiles=range(IT)):
                c = slice(b * BLK, (b + 1) * BLK)
                for i in tiles:
                    if not first:
                        pe.wait_ge(s_h, unit * IT - IT + i + 1)
                    for j, (bank, done) in enumerate([(p_gate, s_gate), (p_up, s_up)]):
                        if b == 0:
                            pe.wait_ge(s_split, turn * SPLITS + 2 * j + 2)
                        for k in range(KT):
                            wh = in_hi[:, parity, j, k, i * P:(i + 1) * P]
                            wl = in_lo[:, parity, j, k, i * P:(i + 1) * P]
                            pe.matmul(bank[:, i, :], wh, xt_lo[:, k, c], start=(k == 0), stop=False)
                            pe.matmul(bank[:, i, :], wh, xt_hi[:, k, c], start=False, stop=False)
                            last = pe.matmul(bank[:, i, :], wl, xt_hi[:, k, c], start=False,
                                             stop=(k == KT - 1))
                        last.then_inc(done, 1)

            def outer(unit, turn, parity, b, first=False):
                pe.wait_ge(s_lo, unit * IT + IT)
                if b == 0:
                    pe.wait_ge(s_split, turn * SPLITS + SPLITS)
                if first:
                    pe.wait_ge(ln.s_lo, T)
                    pe.wait_ge(s_lg_copy, NB)
                for t in range(TPB):
                    if not first:
                        pe.wait_ge(s_acc, unit * TPB - TPB + t + 1)
                    c = slice(t * P, (t + 1) * P)
                    for k in range(IT):
                        hh, hl = h_hi[:, b % 2, k, c], h_lo[:, b % 2, k, c]
                        pe.matmul(p_down[:, t, :], hh, out_lo[:, parity, k, :], start=(k == 0), stop=False)
                        pe.matmul(p_down[:, t, :], hh, out_hi[:, parity, k, :], start=False, stop=False)
                        last = pe.matmul(p_down[:, t, :], hl, out_hi[:, parity, k, :], start=False,
                                         stop=(k == IT - 1))
                    last.then_inc(s_down, 1)

            def logits_columns(b):
                pe.wait_ge(ln.s_lo, (b + 1) * TPB)
                if b > 0:
                    pe.wait_ge(s_lgt_copy, b)
                c = slice(b * BLK, (b + 1) * BLK)
                for k in range(KT):
                    for j, (a, r) in enumerate([(xt_lo, router_lo), (xt_lo, router_hi),
                                                (xt_hi, router_lo), (xt_hi, router_hi)]):
                        last = pe.matmul(p_logits_t, r[:, k, :], a[:, k, c], start=(k == 0 and j == 0),
                                         stop=(k == KT - 1 and j == 3))
                last.then_inc(s_lgt, 1)

            def logits_rows(b):
                pe.wait_ge(s_lgt_copy, b + 1)
                if b > 0:
                    pe.wait_ge(s_lg_copy, b)
                for t in range(TPB):
                    last = pe.transpose(p_logits[:, t * E:(t + 1) * E], logits_t[:, t * P:(t + 1) * P],
                                        ident[0:E, 0:E])
                last.then_inc(s_lg, 1)

            ln.transposes(pe, 0, range(TPB))
            pe.wait_ge(s_route, 2)
            logits_columns(0)
            for b in range(NB - 1):
                nxt = (b + 1) * TPB
                inner(b, 0, 0, b, first=b == 0, tiles=[0])
                logits_rows(b)
                ln.transposes(pe, 0, range(nxt, nxt + 2))
                inner(b, 0, 0, b, first=b == 0, tiles=range(1, IT))
                ln.transposes(pe, 0, range(nxt + 2, nxt + TPB))
                logits_columns(b + 1)
            logits_rows(NB - 1)
            outer(0, 0, 0, 0, first=True)
            inner(NB - 1, 0, 0, NB - 1)
            for b in range(1, NB - 1):
                outer(b, 0, 0, b)
            with pe.Fori(0, E // 2) as i:
                for u in range(PAIR):
                    turn = i * 2 + u // NB + 1
                    inner(i * PAIR + NB + u, turn, (u // NB + 1) % 2, u % NB)
                    if u == 0:
                        outer(i * PAIR + NB - 1, i * 2, 0, NB - 1)
                    else:
                        outer(i * PAIR + NB + u - 1, i * 2 + (u - 1) // NB + 1, ((u - 1) // NB + 1) % 2,
                              (u - 1) % NB)
            outer(LAST, E, 0, NB - 1)



def mamba_phase(nc, phase, x, batches, w):
    DI, _ = w["out_t"].shape
    HEADS = w["dt_bias"].shape[0]
    HD = DI // HEADS
    N = P
    T = x.shape[1] // batches
    NB = T // TPB
    CT = 2
    GC = CT * P
    GH = GC // HD
    G = DI // GC
    CPB = TPB
    UNITS = G * NB
    TAPS = w["conv_w"].shape[2]
    HALO = TAPS - 1
    CONV_TILES = w["conv_w"].shape[0] // P
    RMS_EPS = 1e-5
    Z0, X0, B0, DT0 = 0, DI, 2 * DI, 2 * DI + 2 * N
    assert NB == 2 and N == P and HEADS * 2 == P
    ctx = ExitStack()
    with ctx:
        sem = Sems(nc, ctx, phase)

        def sb(name, shape, dt=F32):
            return ctx.enter_context(nc.sbuf_tensor(f"{phase}_{name}", shape, dt))

        def ps(name, shape):
            return ctx.enter_context(nc.psum_tensor(f"{phase}_{name}", shape, F32))

        ident, ident16 = sb("ident", [P, P]), sb("ident16", [P, P], BF16)
        causal = sb("causal", [P, P])
        never = sb("never", [P, P], BF16)
        ones = sb("ones", [P, 2])
        one = sb("one", [P, 1])
        head_of = sb("head_of", [P, HEADS], BF16)
        taps = sb("taps", [P, CONV_TILES, TAPS])
        conv_bias = sb("conv_bias", [P, CONV_TILES])
        skip = sb("skip", [P, DI // P])
        norm_w = sb("norm_w", [P, DI // P])
        dt_bias, decay_rate = sb("dt_bias", [P, HEADS]), sb("decay_rate", [P, HEADS])
        xt_hi, xt_lo = sb("xt_hi", [P, KT, T * P], F32R), sb("xt_lo", [P, KT, T * P], F32R)
        raw_x, raw_z = sb("raw_x", [P, KT, GC]), sb("raw_z", [P, KT, GC])
        raw_out = sb("raw_out", [P, CT, D])
        in_hi, in_lo = sb("in_hi", [P, 2 * CT, KT, P], F32R), sb("in_lo", [P, 2 * CT, KT, P], F32R)
        out_hi, out_lo = sb("out_hi", [P, CT, D], F32R), sb("out_lo", [P, CT, D], F32R)
        bc = sb("bc", [P, 2, T * P])
        b_rows = sb("b_rows", [P, T, N])
        scores = sb("scores", [P, T, P])
        dt = sb("dt", [P, T, HEADS])
        cum = sb("cum", [P, T, HEADS])
        exp_cum = sb("exp_cum", [P, T, HEADS])
        to_end = sb("to_end", [P, T, HEADS])
        exp_last = sb("exp_last", [P, T, HEADS])
        cum_hm, cum_l = sb("cum_hm", [P, T * P], BF16), sb("cum_l", [P, T * P], BF16)
        square_sum = sb("square_sum", [P, T * P])
        total = sb("total", [P, T, D])
        neg_cum_g, exp_last_g, to_end_g = (sb(n, [P, T, GH]) for n in ("neg_cum_g", "exp_last_g", "to_end_g"))
        head_g = sb("head_g", [P, GH], BF16)
        state, decayed = sb("state", [P, GH, HD]), sb("decayed", [P, GH, HD])
        xraw = sb("xraw", [P, NB, CT, HALO + BLK])
        xs = sb("xs", [P, 2, CT, BLK])
        zs = sb("zs", [P, 2, CT, BLK])
        xdt = sb("xdt", [P, CPB, GH, HD])
        xend = sb("xend", [P, CPB, GH, HD])
        mix = sb("mix", [P, 2, GH, P])
        y = sb("y", [P, CPB, GC])
        g = sb("g", [P, CT, BLK])
        g_hi, g_lo = sb("g_hi", [P, CT, BLK], F32R), sb("g_lo", [P, CT, BLK], F32R)
        work = zs[:, :, :, :].rearrange("p a c t -> p (a c t)")[:, 0:3 * T * HEADS].rearrange("p (a t) -> p a t", a=3)
        parts = g[:, :, :].rearrange("p c t -> p (c t)").bitcast(BF16).rearrange("p (j t a h) -> p j t a h", j=2, t=T, a=2)
        part_hm = parts[:, 0]
        part_l = parts[:, 1]

        p_proj = ps("p_proj", [P, CT, BLK])
        p_tr, p_dec = ps("p_tr", [P, BLK]), ps("p_dec", [P, GH, P])
        p_y, p_st = ps("p_y", [P, 2, GH, HD]), ps("p_st", [P, BLK])
        p_out = ps("p_out", [P, 2, D])
        p_y_flat = p_y[:, :, :, :].rearrange("p a h d -> p (a h d)")

        s_const, s_small, s_rate = sem("const"), sem("small"), sem("rate")
        s_raw_x, s_raw_z, s_raw_out = sem("raw_x"), sem("raw_z"), sem("raw_out")
        s_split_x, s_split_z, s_scaled, s_split_out = (sem("split_x"), sem("split_z"), sem("scaled"),
                                                       sem("split_out"))
        s_dt, s_arg, s_u, s_soft, s_cum, s_cumc = (sem("dt"), sem("arg"), sem("u"), sem("soft"), sem("cum"),
                                                   sem("cumc"))
        s_parts, s_last, s_clamp, s_exps, s_partt, s_partc = (sem("parts"), sem("last"), sem("clamp"),
                                                              sem("exps"), sem("partt"), sem("partc"))
        s_brow, s_browc, s_score, s_scorec, s_clear = (sem("brow"), sem("browc"), sem("score"),
                                                       sem("scorec"), sem("clear"))
        s_px, s_pz, s_xtr, s_dec, s_y2, s_st, s_ytr, s_pout = (
            sem("px"), sem("pz"), sem("xtr"), sem("dec"), sem("y2"), sem("st"), sem("ytr"), sem("pout"))
        s_xraw, s_xs, s_zs, s_exp, s_ghi, s_sq = (sem("xraw"), sem("xs"), sem("zs"), sem("exp"),
                                                  sem("ghi"), sem("sq"))
        s_conv, s_skip, s_g, s_glo, s_xdt, s_mix = (sem("conv"), sem("skip"), sem("g"), sem("glo"),
                                                    sem("xdt"), sem("mix"))
        s_car, s_y, s_state, s_acc, s_stage = (sem("car"), sem("y"), sem("state"), sem("acc"),
                                               sem("stage"))
        s_xend, s_decayed, s_sqs = sem("xend"), sem("decayed"), sem("sqs")
        s_var, s_vara, s_root, s_fin, s_add = (sem("var"), sem("vara"), sem("root"), sem("fin"),
                                               sem("add"))

        lns = LayerNorm(nc, ctx, sem, T, None, xt_hi, xt_lo, ident[:, :],
                        lambda t: p_out[:, t % 2, :].rearrange("p (k c) -> p k c", k=KT),
                        xn=y[:, :, :].rearrange("p c d -> p (c d)").rearrange("p (a d) -> p a d", a=2))

        var, root, rstd, tmp = lns.var, lns.roots, lns.rstd, lns.tmp

        CONVS = UNITS + NB
        SMALL = 16 * (5 + P // HD)
        SOFT_STEPS = 20
        FIN_STEPS = 5

        def unit(k, gi, b):
            u = gi * NB + b
            return u + k * UNITS, u + NB + k * CONVS

        block = ctx.enter_context(nc.Block())

        @block.sync
        def _(sp):
            with nc.allow_non_contiguous_dma(reason="short vectors, once"):
                sp.dma_start(taps[:, :, :], w["conv_w"].rearrange("(j p) a k -> p j (a k)", p=P)).then_inc(s_small, 16)
                sp.dma_start(conv_bias[:, :], w["conv_b"].rearrange("(j p) -> p j", p=P)).then_inc(s_small, 16)
                sp.dma_start(norm_w[:, :], w["norm_w"].rearrange("(j p) -> p j", p=P)).then_inc(s_small, 16)
                per = P // HD
                d = w["D_param"].rearrange("(j a) -> a j", a=per)
                for a in range(per):
                    sp.dma_start(skip[a * HD:(a + 1) * HD, :], d[a].partition_broadcast(HD)).then_inc(s_small, 16)
                sp.dma_start(dt_bias[:, :], w["dt_bias"].partition_broadcast(P)).then_inc(s_small, 16)
                sp.dma_start(decay_rate[:, :], w["A_log"].partition_broadcast(P)).then_inc(s_small, 16)
            in_t = w["in_t"].rearrange("(k p) c -> p k c", p=P)

            def load_in(stream, x0, z_steps, z0, n=GC):
                if not isinstance(stream, int) or stream > 0:
                    sp.wait_ge(s_split_x, stream * 4)
                    sp.wait_ge(s_split_z, z_steps)
                sp.dma_start(raw_x[:, :, :], in_t[:, :, bass.ds(x0, GC)]).then_inc(s_raw_x, 16)
                sp.dma_start(raw_z[:, :, 0:n], in_t[:, :, bass.ds(z0, n)]).then_inc(s_raw_z, 16)

            def load_out(n, gi):
                if not isinstance(n, int) or n > 0:
                    sp.wait_ge(s_split_out, n * 4)
                sp.dma_start(raw_out[:, :, :],
                             w["out_t"][bass.ds(gi * GC, GC), :].rearrange("(k p) d -> p k d", p=P)).then_inc(s_raw_out, 16)

            for k in range(batches):
                sx, sz = k * (G + 1), k * (4 * G + 2)
                load_in(sx, B0, sz, DT0, HEADS)
                load_in(sx + 1, X0, sz + 2, Z0)
                load_out(k * G, 0)
                with sp.Fori(1, G) as gi:
                    load_in(gi + (sx + 1), gi * GC + X0, gi * 4 + (sz + 2), gi * GC + Z0)
                    load_out(gi + k * G, gi)

        @block.gpsimd
        def _(pool):
            build_identity(pool, ident[:, :], s_const, 0)
            build_identity(pool, ident16[:, :], s_const, 2)
            pool.memset(causal[:, :], 1.0).then_inc(s_const, 1)
            pool.memset(head_of[:, :], 0.0).then_inc(s_const, 1)
            pool.memset(never[:, :], 0.0).then_inc(s_const, 1)
            pool.wait_ge(s_const, 7)
            pool.affine_select(out=never[:, :], in_=never[:, :], compare_op=ALU.is_ge, fill=-1e37, base=0,
                               pattern=[[1, P]], channel_multiplier=-1).then_inc(s_const, 1)
            pool.affine_select(out=causal[:, :], in_=causal[:, :], compare_op=ALU.is_ge, fill=0.0, base=0,
                               pattern=[[1, P]], channel_multiplier=-1).then_inc(s_const, 1)
            for a in range(P // HEADS):
                pool.affine_select(out=head_of[:, :], in_=head_of[:, :], compare_op=ALU.not_equal, fill=1.0,
                                   base=-a * HEADS, pattern=[[-1, HEADS]],
                                   channel_multiplier=1).then_inc(s_const, 1)
                pool.wait_ge(s_const, 10 + a)
            pool.memset(ones[:, :], 1.0).then_inc(s_const, 1)
            pool.memset(one[:, :], 1.0).then_inc(s_const, 1)
            pool.memset(xraw[:, 0, :, 0:HALO], 0.0).then_inc(s_const, 1)
            pool.wait_ge(s_const, 14)

            def split(hi, lo, raw, done, at):
                unit_col = one[:, :] if len(raw.shape) == 2 else one[:, :].unsqueeze(1)
                pool.tensor_tensor(hi, raw, unit_col.broadcast_to(raw.shape), ALU.mult).then_inc(done, 1)
                pool.wait_ge(done, at + 1)
                pool.tensor_tensor(lo, raw, hi.bitcast(F32), ALU.subtract).then_inc(done, 1)

            def split_x(stream, ct):
                pool.wait_ge(s_raw_x, stream * 16 + 16)
                split(in_hi[:, ct, :, :], in_lo[:, ct, :, :], raw_x[:, :, ct * P:(ct + 1) * P],
                      s_split_x, stream * 4 + 2 * ct)

            def split_z(loads, steps, ct):
                pool.wait_ge(s_raw_z, loads * 16)
                split(in_hi[:, CT + ct, :, :], in_lo[:, CT + ct, :, :], raw_z[:, :, ct * P:(ct + 1) * P],
                      s_split_z, steps + 2 * ct)

            def split_out(n, ct):
                pool.wait_ge(s_scaled, n * CT + ct + 1)
                split(out_hi[:, ct, :], out_lo[:, ct, :], raw_out[:, ct, :], s_split_out, n * 4 + 2 * ct)

            def add_squares(U, b, ct, first=False):
                pool.wait_ge(s_sq, U * CT + ct + 1)
                if not first:
                    pool.wait_ge(s_sqs, U * CT + ct)
                c = slice(b * BLK, (b + 1) * BLK)
                pool.tensor_tensor(square_sum[:, c], square_sum[:, c], zs[:, b, ct, :], ALU.add).then_inc(s_sqs, 1)

            def decay_x(k, gi, b, j, first=False):
                U, V = unit(k, gi, b)
                pool.wait_ge(s_xdt, U * 2 + j + 1)
                if not first:
                    pool.wait_ge(s_st, U * CPB - CPB + 2 * j + 2)
                c = b * CPB + 2 * j
                pool.tensor_tensor(xend[:, 2 * j:2 * j + 2, :, :], xdt[:, 2 * j:2 * j + 2, :, :],
                                   to_end_g[:, c:c + 2, :].unsqueeze(3).broadcast_to([P, 2, GH, HD]),
                                   ALU.mult).then_inc(s_xend, 1)

            def slot(k, gi, b, first=False, second=False, last=False, group0=False, last_group=False):
                U, V = unit(k, gi, b)
                gn, bn = (gi, 1) if b == 0 else (gi + 1, 0)

                def decay_state(c):
                    if b > 0 or c > 0:
                        pool.wait_ge(s_state, U * CPB + c)
                    pool.tensor_tensor(decayed[:, :, :], state[:, :, :],
                                       exp_last_g[:, b * CPB + c, :].unsqueeze(2).broadcast_to([P, GH, HD]),
                                       ALU.mult).then_inc(s_decayed, 1)

                def next_x(ct):
                    if b == 0 and not last_group:
                        pool.wait_ge(s_px, V * CT + CT + ct + 1)
                        split_x(gi + (k * (G + 1) + 2), ct)

                def next_z(ct):
                    if b == 1 and not last_group:
                        pool.wait_ge(s_pz, U * CT + ct + 1)
                        split_z(gi + (k * (G + 1) + 3), gi * 4 + (k * (4 * G + 2) + 6), ct)

                def this_out(ct):
                    if b == 1 and not group0:
                        if ct == 0:
                            pool.wait_ge(s_pout, U * TPB - TPB)
                        split_out(gi + k * G, ct)

                decay_state(0)
                decay_x(k, gi, b, 1, first)
                this_out(0)
                decay_state(1)
                this_out(1)
                next_x(0)
                if not first:
                    add_squares(U - 1, 1 - b, 0, second)
                decay_state(2)
                if not first:
                    add_squares(U - 1, 1 - b, 1)
                next_z(0)
                next_x(1)
                decay_state(3)
                next_z(1)
                if not last:
                    decay_x(k, gn, bn, 0)

            for k in range(batches):
                split_x_base = k * (G + 1)
                if k > 0:
                    pool.wait_ge(s_add, k * T)
                pool.memset(square_sum[:, :], 0.0).then_inc(s_clear, 1)
                pool.memset(total[:, :, :], 0.0).then_inc(s_clear, 1)
                if k > 0:
                    pool.wait_ge(s_px, k * CONVS * CT)
                    pool.wait_ge(s_pz, k * UNITS * CT)
                for ct in range(CT):
                    split_x(split_x_base, ct)
                pool.wait_ge(s_raw_z, split_x_base * 16 + 16)
                split(in_hi[:, CT, :, 0:HEADS], in_lo[:, CT, :, 0:HEADS], raw_z[:, :, 0:HEADS],
                      s_split_z, k * (4 * G + 2))
                for ct in range(CT):
                    pool.wait_ge(s_px, (k * CONVS + NB - 1) * CT + ct + 1)
                    split_x(split_x_base + 1, ct)
                pool.wait_ge(s_dt, k + 1)
                for ct in range(CT):
                    split_z(split_x_base + 2, k * (4 * G + 2) + 2, ct)
                if k > 0:
                    pool.wait_ge(s_pout, k * UNITS * TPB)
                for ct in range(CT):
                    split_out(k * G, ct)
                decay_x(k, 0, 0, 0, first=True)
                slot(k, 0, 0, first=True)
                slot(k, 0, 1, second=True, group0=True)
                with pool.Fori(1, G - 1) as gi:
                    slot(k, gi, 0)
                    slot(k, gi, 1)
                slot(k, G - 1, 0, last_group=True)
                slot(k, G - 1, 1, last=True, last_group=True)
                U = (k + 1) * UNITS - 1
                for ct in range(CT):
                    add_squares(U, NB - 1, ct)

        @block.scalar
        def _(act):
            act.wait_ge(s_small, SMALL)
            act.activation(decay_rate[:, :], decay_rate[:, :], ACT.Exp).then_inc(s_rate, 1)

            def raw(V, b, ct, first=False):
                act.wait_ge(s_px, V * CT + ct + 1)
                if not first:
                    act.wait_ge(s_conv, V * (CT * TAPS) - CT * TAPS + (ct + 1) * TAPS)
                if b > 0:
                    act.activation(xraw[:, b, ct, 0:HALO], xraw[:, b - 1, ct, BLK:BLK + HALO], ACT.Copy)
                act.activation(xraw[:, b, ct, HALO:], p_proj[:, ct, :], ACT.Copy).then_inc(s_xraw, 1)

            def silu_x(V, parity, ct):
                act.wait_ge(s_conv, V * (CT * TAPS) + (ct + 1) * TAPS)
                act.activation(xs[:, parity, ct, :], xs[:, parity, ct, :], ACT.Silu).then_inc(s_xs, 1)

            def silu_z(U, parity, ct, young=False):
                act.wait_ge(s_pz, U * CT + ct + 1)
                if not young:
                    act.wait_ge(s_sqs, U * CT - 2 * CT + ct + 1)
                act.activation(zs[:, parity, ct, :], p_proj[:, ct, :], ACT.Silu).then_inc(s_zs, 1)

            def high(U, ct, second=False):
                act.wait_ge(s_g, U * CT + ct + 1)
                if not second:
                    act.wait_ge(s_pout, U * TPB)
                act.activation(g_hi[:, ct, :], g[:, ct, :], ACT.Copy).then_inc(s_ghi, 1)

            def square(U, b, ct):
                act.activation(zs[:, b, ct, :], g[:, ct, :], ACT.Square).then_inc(s_sq, 1)

            def exponents(U, b, c, first=False):
                act.wait_ge(s_dec, U * CPB + c + 1)
                if not (first and c < 2):
                    act.wait_ge(s_y2, U * CPB + c - 1)
                for h in range(GH):
                    ins = act.activation(mix[:, c % 2, h, :], p_dec[:, h, :], ACT.Exp,
                                         bias=neg_cum_g[:, b * CPB + c, h:h + 1])
                ins.then_inc(s_exp, 1)

            def slot(k, gi, b, first=False, second=False, last=False):
                U, V = unit(k, gi, b)
                if not first:
                    for ct in range(CT):
                        high(U - 1, ct, second)
                if not last:
                    raw(V + 1, 1 - b, 0)
                exponents(U, b, 2)
                if not first:
                    for ct in range(CT):
                        square(U - 1, 1 - b, ct)
                if not last:
                    raw(V + 1, 1 - b, 1)
                exponents(U, b, 3)
                if not last:
                    for ct in range(CT):
                        silu_x(V + 1, 1 - b, ct)
                    for ct in range(CT):
                        silu_z(U + 1, 1 - b, ct, first)
                    exponents(U + 1, 1 - b, 0)
                    exponents(U + 1, 1 - b, 1)

            for k in range(batches):
                lns.root(act, k, 0)
                for b in range(NB):
                    if b + 1 < NB:
                        lns.root(act, k, b + 1)
                    lns.high(act, k, range(b * TPB, (b + 1) * TPB))
                V0 = k * CONVS
                for b in range(NB):
                    for ct in range(CT):
                        raw(V0 + b, b, ct, first=b == 0 and k == 0)
                act.wait_ge(s_arg, (k + 1) * 4)
                act.activation(work[:, 0, :], work[:, 1, :], ACT.Exp).then_inc(s_u, 1)
                act.wait_ge(s_cumc, k + 1)
                act.activation(exp_cum[:, :, :], cum[:, :, :], ACT.Exp).then_inc(s_exps, 1)
                act.wait_ge(s_last, k + 1)
                act.activation(exp_last[:, :, :], p_st[:, :].rearrange("p (t h) -> p t h", t=T),
                               ACT.Exp).then_inc(s_exps, 1)
                act.wait_ge(s_clamp, (k + 1) * 2)
                act.activation(to_end[:, :, :], to_end[:, :, :], ACT.Exp).then_inc(s_exps, 1)
                act.wait_ge(s_partt, k * 2 + 1)
                act.activation(cum_hm[:, :], p_tr[:, :].bitcast(BF16), ACT.Copy).then_inc(s_partc, 1)
                act.wait_ge(s_partt, k * 2 + 2)
                act.activation(cum_l[:, :], p_dec[:, :, :].rearrange("p h c -> p (h c)").bitcast(BF16),
                               ACT.Copy).then_inc(s_partc, 1)
                for b in range(NB):
                    for ct in range(CT):
                        act.wait_ge(s_conv, (V0 + b) * (CT * TAPS) + (ct + 1) * TAPS)
                        c = slice(b * BLK, (b + 1) * BLK)
                        act.activation(bc[:, ct, c], bc[:, ct, c], ACT.Silu).then_inc(s_xs, 1)
                for j in range(2):
                    act.wait_ge(s_brow, k * 2 + j + 1)
                    act.activation(b_rows[:, 4 * j:4 * j + 4, :], (p_y_flat, p_st[:, :])[j].rearrange("p (t n) -> p t n", t=4),
                                   ACT.Copy).then_inc(s_browc, 1)
                U0, V0 = unit(k, 0, 0)
                for ct in range(CT):
                    raw(V0, 0, ct)
                for ct in range(CT):
                    silu_x(V0, 0, ct)
                for ct in range(CT):
                    silu_z(U0, 0, ct, True)
                for c in range(2):
                    exponents(U0, 0, c, first=True)
                slot(k, 0, 0, first=True)
                slot(k, 0, 1, second=True)
                with act.Fori(1, G - 1) as gi:
                    slot(k, gi, 0)
                    slot(k, gi, 1)
                slot(k, G - 1, 0)
                slot(k, G - 1, 1, last=True)
                for ct in range(CT):
                    high((k + 1) * UNITS - 1, ct)
                for ct in range(CT):
                    square((k + 1) * UNITS - 1, NB - 1, ct)
                act.wait_ge(s_vara, k + 1)
                act.activation(root[:, :], var[:, :], ACT.Sqrt).then_inc(s_root, 1)

        @block.vector
        def _(dve):
            def conv_step(V, b, ct, tile, dst, i):
                n = V * (CT * TAPS) + ct * TAPS
                src = xraw[:, b, ct, :]
                tap = taps[:, bass.ds(tile, 1), :]
                if i == 0:
                    dve.wait_ge(s_xraw, V * CT + ct + 1)
                    dve.tensor_scalar(dst, src[:, HALO:HALO + BLK], tap[:, 0, HALO:HALO + 1],
                                      conv_bias[:, bass.ds(tile, 1)], ALU.mult, ALU.add).then_inc(s_conv, 1)
                else:
                    dve.wait_ge(s_conv, n + i)
                    j = HALO - i
                    dve.scalar_tensor_tensor(dst, src[:, j:j + BLK], tap[:, 0, j:j + 1], dst,
                                             ALU.mult, ALU.add).then_inc(s_conv, 1)

            def conv_x(k, gi, b, ct, steps, young=False):
                U, V = unit(k, gi, b)
                if not young and 0 in steps:
                    dve.wait_ge(s_skip, U * CT - 2 * CT + CT)
                for i in steps:
                    conv_step(V, b, ct, gi * CT + ct, xs[:, b, ct, :], i)

            def gate(k, gi, b, first=False):
                U, V = unit(k, gi, b)
                for ct in range(CT):
                    dve.wait_ge(s_ytr, U * CT + ct + 1)
                    if not first:
                        dve.wait_ge(s_sq, U * CT - CT + ct + 1)
                        dve.wait_ge(s_glo, U * CT - CT + ct + 1)
                    dve.scalar_tensor_tensor(g[:, ct, :], xs[:, b, ct, :], skip[:, bass.ds(gi * CT + ct, 1)],
                                             p_out[:, ct, :], ALU.mult,
                                             ALU.add).then_inc(s_skip, 1)
                for ct in range(CT):
                    dve.wait_ge(s_skip, U * CT + ct + 1)
                    dve.wait_ge(s_zs, U * CT + ct + 1)
                    dve.tensor_tensor(g[:, ct, :], g[:, ct, :], zs[:, b, ct, :], ALU.mult).then_inc(s_g, 1)

            def gate_low(U):
                for ct in range(CT):
                    dve.wait_ge(s_ghi, U * CT + ct + 1)
                    dve.tensor_tensor(g_lo[:, ct, :], g[:, ct, :], g_hi[:, ct, :].bitcast(F32),
                                      ALU.subtract).then_inc(s_glo, 1)

            def accumulate(U, b, t):
                dve.wait_ge(s_pout, U * TPB + t + 1)
                tile = b * TPB + t
                dve.tensor_tensor(total[:, tile, :], p_out[:, t % 2, :], total[:, tile, :],
                                  ALU.add).then_inc(s_acc, 1)

            def stage(k, gi, first=False):
                heads = bass.ds(gi * GH, GH)
                U, _ = unit(k, gi, 0)
                if not first:
                    dve.wait_ge(s_exp, U * CPB)
                    dve.wait_ge(s_decayed, U * CPB)
                    dve.wait_ge(s_xend, U * 2)
                    dve.wait_ge(s_state, U * CPB)
                dve.memset(state[:, :, :], 0.0)
                dve.tensor_scalar(neg_cum_g[:, :, :], cum[:, :, heads], -1.0, None, ALU.mult)
                dve.tensor_copy(exp_last_g[:, :, :], exp_last[:, :, heads])
                dve.tensor_copy(head_g[:, :], head_of[:, heads])
                dve.tensor_copy(to_end_g[:, :, :], to_end[:, :, heads]).then_inc(s_stage, 1)

            def times_dt(k, gi, b, j, first=False):
                U, V = unit(k, gi, b)
                heads = bass.ds(gi * GH, GH)
                dve.wait_ge(s_xtr, U * 2 + j + 1)
                if not first:
                    dve.wait_ge(s_y2, U * CPB - CPB + 2 * j + 2)
                    dve.wait_ge(s_xend, U * 2 - 2 + j + 1)
                c = b * CPB + 2 * j
                dve.tensor_tensor(xdt[:, 2 * j:2 * j + 2, :, :],
                                  p_tr[:, :].rearrange("p (c h d) -> p c h d", c=2, h=GH),
                                  dt[:, c:c + 2, heads].unsqueeze(3).broadcast_to([P, 2, GH, HD]),
                                  ALU.mult).then_inc(s_xdt, 1)

            def decay_scores(U, b, c):
                dve.wait_ge(s_exp, U * CPB + c + 1)
                dve.scalar_tensor_tensor(mix[:, c % 2, :, :], mix[:, c % 2, :, :], 1.0,
                                         scores[:, b * CPB + c, :].unsqueeze(1).broadcast_to([P, GH, P]),
                                         ALU.min, ALU.mult).then_inc(s_mix, 1)

            def slot(k, gi, b, first=False, second=False, last=False, group0=False):
                U, V = unit(k, gi, b)
                heads = bass.ds(gi * GH, GH)
                gn, bn = (gi, 1) if b == 0 else (gi + 1, 0)
                gp, bp = (gi, 0) if b == 1 else (gi - 1, 1)

                def combine(c):
                    n = U * CPB + c
                    yc = y[:, c, :].rearrange("p (h d) -> p h d", h=GH)
                    dve.wait_ge(s_y2, n + 1)
                    dve.tensor_tensor(yc, p_y[:, 1, :, :],
                                      exp_cum[:, b * CPB + c, heads].unsqueeze(2).broadcast_to([P, GH, HD]),
                                      ALU.mult).then_inc(s_car, 1)
                    dve.wait_ge(s_st, n + 1)
                    dve.wait_ge(s_decayed, n + 1)
                    dve.tensor_tensor(state[:, :, :], p_st[:, 0:GC].rearrange("p (h d) -> p h d", h=GH),
                                      decayed[:, :, :], ALU.add).then_inc(s_state, 1)
                    dve.wait_ge(s_car, n + 1)
                    dve.tensor_tensor(yc, p_y[:, 0, :, :], yc, ALU.add).then_inc(s_y, 1)

                def conv(ct, steps):
                    if not last:
                        conv_x(k, gn, bn, ct, steps, first)

                def add_out(t):
                    if not first:
                        accumulate(U - 1, bp, t)

                if not first:
                    gate(k, gp, bp, first=second)
                combine(0)
                decay_scores(U, b, 1)
                if not first:
                    gate_low(U - 1)
                conv(0, (0, 1))
                decay_scores(U, b, 2)
                combine(1)
                conv(0, (2, 3))
                if b == 0 and not group0:
                    scale_out(k, gi)
                conv(1, (0,))
                decay_scores(U, b, 3)
                conv(1, (1,))
                combine(2)
                conv(1, (2, 3))
                add_out(0)
                add_out(1)
                combine(3)
                if last:
                    add_out(2)
                    add_out(3)
                else:
                    if b == 1:
                        stage(k, gn)
                    times_dt(k, gn, bn, 0)
                    add_out(2)
                    decay_scores(U + 1, bn, 0)
                    add_out(3)
                    times_dt(k, gn, bn, 1)

            def scale_out(k, gi):
                for ct in range(CT):
                    dve.wait_ge(s_raw_out, (gi + k * G) * 16 + 16)
                    dve.tensor_scalar(raw_out[:, ct, :], raw_out[:, ct, :],
                                      norm_w[:, bass.ds(gi * CT + ct, 1)], None, ALU.mult).then_inc(s_scaled, 1)

            dve.wait_ge(s_small, SMALL)
            dve.wait_ge(s_const, 14)
            for k in range(batches):
                lns.x_tile = lambda t: x[:, k * T + t, :]
                lns.stats(dve, k, 0)
                for b in range(NB):
                    if b + 1 < NB:
                        lns.stats(dve, k, b + 1)
                    lns.normalise(dve, k, b)
                V0 = k * CONVS
                v, a, m = dt[:, :, :], work[:, 1, :].rearrange("p (t h) -> p t h", t=T), \
                    work[:, 2, :].rearrange("p (t h) -> p t h", t=T)
                u = work[:, 0, :].rearrange("p (t h) -> p t h", t=T)
                step = link(dve, s_arg, k * 4)
                dve.wait_ge(s_dt, k + 1)
                step(dve.tensor_tensor(v, p_dec[:, :, :].rearrange("p h c -> p (h c)").rearrange("p (t h) -> p t h", t=T),
                                       dt_bias[:, :].unsqueeze(1).broadcast_to([P, T, HEADS]), ALU.add))
                step(dve.tensor_scalar(a, v, -1.0, None, ALU.mult))
                step(dve.tensor_tensor(a, a, v, ALU.min))
                step(dve.tensor_scalar(m, v, 0.0, None, ALU.max))
                for b in range(NB):
                    for ct in range(CT):
                        for i in range(TAPS):
                            conv_step(V0 + b, b, ct, DI // P + ct, bc[:, ct, b * BLK:(b + 1) * BLK], i)
                dve.wait_ge(s_u, k + 1)
                step = link(dve, s_soft, k * SOFT_STEPS)
                q, r = a, v
                step(dve.tensor_scalar(r, u, 2.0, None, ALU.add))
                step(dve.reciprocal(r, r))
                step(dve.tensor_tensor(u, u, r, ALU.mult))
                step(dve.tensor_tensor(q, u, u, ALU.mult))
                step(dve.tensor_scalar(r, q, 1.0 / 21, None, ALU.mult))
                for c in (19, 17, 15, 13, 11, 9, 7, 5, 3):
                    step(dve.scalar_tensor_tensor(r, r, 1.0 / c, q, ALU.add, ALU.mult))
                step(dve.scalar_tensor_tensor(r, r, 1.0, u, ALU.add, ALU.mult))
                step(dve.scalar_tensor_tensor(v, r, 2.0, m, ALU.mult, ALU.add))
                dve.wait_ge(s_rate, 1)
                step(dve.scalar_tensor_tensor(u, v, -1.0, decay_rate[:, :].unsqueeze(1).broadcast_to([P, T, HEADS]),
                                              ALU.mult, ALU.mult))
                dve.wait_ge(s_cum, k + 1)
                dve.tensor_copy(cum[:, :, :], p_y_flat.rearrange("p (t h) -> p t h", t=T)).then_inc(s_cumc, 1)
                dve.wait_ge(s_cumc, k + 1)
                step(dve.memset(part_l[:, :, 1, :], 0.0))
                step(dve.tensor_copy(part_hm[:, :, 0, :], cum[:, :, :]))
                step(dve.tensor_tensor(a, cum[:, :, :], part_hm[:, :, 0, :], ALU.subtract))
                dve.tensor_copy(part_hm[:, :, 1, :], a).then_inc(s_parts, 1)
                dve.wait_ge(s_parts, k * 2 + 1)
                dve.tensor_tensor(part_l[:, :, 0, :], a, part_hm[:, :, 1, :], ALU.subtract).then_inc(s_parts, 1)
                dve.wait_ge(s_last, k + 1)
                step = link(dve, s_clamp, k * 2)
                dve.wait_ge(s_exps, k * 3 + 2)
                step(dve.tensor_tensor(to_end[:, :, :], p_st[:, :].rearrange("p (t h) -> p t h", t=T),
                                       cum[:, :, :], ALU.subtract))
                step(dve.tensor_scalar(to_end[:, :, :], to_end[:, :, :], 0.0, None, ALU.min))
                for j in range(2):
                    dve.wait_ge(s_score, k * 2 + j + 1)
                    dve.tensor_tensor(scores[:, 4 * j:4 * j + 4, :], p_out[:, j, :].rearrange("p (t l) -> p t l", t=4),
                                      causal[:, :].unsqueeze(1).broadcast_to([P, 4, P]),
                                      ALU.mult).then_inc(s_scorec, 1)
                dve.wait_ge(s_exps, k * 3 + 3)
                for ct in range(CT):
                    conv_x(k, 0, 0, ct, range(TAPS), True)
                scale_out(k, 0)
                dve.wait_ge(s_clear, (k + 1) * 2)
                stage(k, 0, first=True)
                times_dt(k, 0, 0, 0, first=True)
                decay_scores(k * UNITS, 0, 0)
                times_dt(k, 0, 0, 1, first=True)
                slot(k, 0, 0, first=True, group0=True)
                slot(k, 0, 1, second=True)
                with dve.Fori(1, G - 1) as gi:
                    slot(k, gi, 0)
                    slot(k, gi, 1)
                slot(k, G - 1, 0)
                slot(k, G - 1, 1, last=True)
                U = (k + 1) * UNITS - 1
                gate(k, G - 1, NB - 1)
                gate_low(U)
                for t in range(TPB):
                    accumulate(U, NB - 1, t)
                dve.wait_ge(s_var, k + 1)
                dve.tensor_scalar(var[:, :], p_y_flat[:, 0:2 * T].rearrange("p (t a) -> p t a", a=2)[:, :, 0],
                                  1.0 / DI, RMS_EPS, ALU.mult, ALU.add).then_inc(s_vara, 1)
                dve.wait_ge(s_root, k + 1)
                refine_rsqrt(dve, link(dve, s_fin, k * FIN_STEPS), rstd[:, :], root[:, :], var[:, :], tmp[:, :])
                for t in range(T):
                    dve.scalar_tensor_tensor(x[:, k * T + t, :], total[:, t, :], rstd[:, t:t + 1],
                                             x[:, k * T + t, :], ALU.mult, ALU.add).then_inc(s_add, 1)

        @block.tensor
        def _(pe):
            def project(bank, piece, b):
                c = slice(b * BLK, (b + 1) * BLK)
                for kk in range(KT):
                    pe.matmul(bank, in_hi[:, piece, kk, :], xt_lo[:, kk, c], start=(kk == 0), stop=False)
                    pe.matmul(bank, in_hi[:, piece, kk, :], xt_hi[:, kk, c], start=False, stop=False)
                    last = pe.matmul(bank, in_lo[:, piece, kk, :], xt_hi[:, kk, c], start=False,
                                     stop=(kk == KT - 1))
                return last

            def project_x(k, gi, b, ct, first=False):
                U, V = unit(k, gi, b)
                if first:
                    pe.wait_ge(s_xraw, V * CT - CT + ct + 1)
                else:
                    pe.wait_ge(s_zs, U * CT - CT + ct + 1)
                if b == 0:
                    pe.wait_ge(s_split_x, (gi + (k * (G + 1) + 1)) * 4 + 2 * ct + 2)
                project(p_proj[:, ct, :], ct, b).then_inc(s_px, 1)

            def project_z(k, gi, b, ct):
                U, V = unit(k, gi, b)
                pe.wait_ge(s_xraw, V * CT + ct + 1)
                if b == 0:
                    pe.wait_ge(s_split_z, gi * 4 + (k * (4 * G + 2) + 2 * ct + 4))
                project(p_proj[:, ct, :], CT + ct, b).then_inc(s_pz, 1)

            def project_out(k, gi, b, tiles):
                U, _ = unit(k, gi, b)
                for t in tiles:
                    if t == 0:
                        pe.wait_ge(s_glo, U * CT + CT)
                        if b == 0:
                            pe.wait_ge(s_split_out, (gi + k * G) * 4 + 4)
                    if t >= 2:
                        pe.wait_ge(s_acc, U * TPB + t - 1)
                    c = slice(t * P, (t + 1) * P)
                    for ct in range(CT):
                        pe.matmul(p_out[:, t % 2, :], g_hi[:, ct, c], out_lo[:, ct, :], start=(ct == 0), stop=False)
                        pe.matmul(p_out[:, t % 2, :], g_hi[:, ct, c], out_hi[:, ct, :], start=False, stop=False)
                        last = pe.matmul(p_out[:, t % 2, :], g_lo[:, ct, c], out_hi[:, ct, :], start=False,
                                         stop=(ct == CT - 1))
                    last.then_inc(s_pout, 1)

            def rows(k, gi, b, j, first=False):
                U, V = unit(k, gi, b)
                if j == 0:
                    pe.wait_ge(s_xs, V * CT + CT)
                if not (first and j == 0):
                    pe.wait_ge(s_xdt, U * 2 + j)
                for c in range(2):
                    for ct in range(CT):
                        s = (2 * j + c) * P
                        mm = pe.transpose(p_tr[:, c * GC + ct * P:c * GC + (ct + 1) * P],
                                          xs[:, b, ct, s:s + P], ident[:, :])
                mm.then_inc(s_xtr, 1)

            def spread(k, gi, b, c, first=False):
                U, V = unit(k, gi, b)
                if not (first and c == 0):
                    pe.wait_ge(s_exp, U * CPB + c)
                if b == 0 and c == 0:
                    pe.wait_ge(s_stage, gi + (k * G + 1))
                s = (b * CPB + c) * P
                pe.matmul(p_dec[:, :, :], ident16[:, :], never[:, :].unsqueeze(1).broadcast_to([P, GH, P]),
                          start=True, stop=False)
                for h in range(GH):
                    sel = head_g[:, h:h + 1].broadcast_to([P, P])
                    pe.matmul(p_dec[:, h, :], sel, cum_hm[:, s:s + P], start=False, stop=False)
                    mm = pe.matmul(p_dec[:, h, :], sel, cum_l[:, s:s + P], start=False,
                                   stop=h == GH - 1)
                mm.then_inc(s_dec, 1)

            def slot(k, gi, b, first=False, last=False):
                U, V = unit(k, gi, b)
                gn, bn = (gi, 1) if b == 0 else (gi + 1, 0)
                gp, bp = (gi, 0) if b == 1 else (gi - 1, 1)

                def recur(c):
                    s = (b * CPB + c) * P
                    if not (first and c == 0):
                        pe.wait_ge(s_y, U * CPB + c)
                        pe.wait_ge(s_state, U * CPB + c)
                    pe.wait_ge(s_mix, U * CPB + c + 1)
                    pe.matmul(p_y[:, 1, :, :], bc[:, 1, s:s + P], state[:, :, :], start=True, stop=True)
                    for h in range(GH):
                        mm = pe.matmul(p_y[:, 0, h, :], mix[:, c % 2, h, :], xdt[:, c, h, :], start=True, stop=True)
                    mm.then_inc(s_y2, 1)
                    if c % 2 == 0:
                        pe.wait_ge(s_xend, U * 2 + c // 2 + 1)
                    pe.matmul(p_st[:, 0:GC], b_rows[:, b * CPB + c, :],
                              xend[:, c, :, :].rearrange("p h d -> p (h d)"), start=True,
                              stop=True).then_inc(s_st, 1)

                def columns(ct):
                    if ct == 0:
                        pe.wait_ge(s_y, U * CPB + CPB)
                    if not first:
                        pe.wait_ge(s_acc, U * TPB - 1 + ct)
                    for c in range(CPB):
                        mm = pe.transpose(p_out[:, ct, c * P:(c + 1) * P],
                                          y[:, c, ct * P:(ct + 1) * P], ident[:, :])
                    mm.then_inc(s_ytr, 1)

                recur(0)
                if not last:
                    project_x(k, gn, bn, 0)
                spread(k, gi, b, 2)
                recur(1)
                if not last:
                    project_x(k, gn, bn, 1)
                spread(k, gi, b, 3)
                recur(2)
                if not first:
                    project_out(k, gp, bp, (0, 1))
                recur(3)
                if not last:
                    project_z(k, gn, bn, 0)
                    rows(k, gn, bn, 0)
                    project_z(k, gn, bn, 1)
                    spread(k, gn, bn, 0)
                if not first:
                    project_out(k, gp, bp, (2, 3))
                columns(0)
                if not last:
                    rows(k, gn, bn, 1)
                    spread(k, gn, bn, 1)
                columns(1)

            pe.wait_ge(s_const, 14)
            for k in range(batches):
                lns.transposes(pe, k, range(T))
                pe.wait_ge(lns.s_lo, (k + 1) * T)
                pe.wait_ge(s_split_z, k * (4 * G + 2) + 2)
                p_dt = p_dec[:, :, :].rearrange("p h c -> p (h c)")
                for t in range(T):
                    c = slice(t * P, (t + 1) * P)
                    for kk in range(KT):
                        for j, (a, ww) in enumerate([(xt_lo, in_hi), (xt_hi, in_lo), (xt_hi, in_hi)]):
                            mm = pe.matmul(p_dt[:, t * HEADS:(t + 1) * HEADS], a[:, kk, c], ww[:, CT, kk, 0:HEADS],
                                           start=(kk == 0 and j == 0), stop=(kk == KT - 1 and j == 2))
                mm.then_inc(s_dt, 1)
                V0 = k * CONVS
                pe.wait_ge(s_split_x, k * (G + 1) * 4 + 4)
                for b in range(NB):
                    for ct in range(CT):
                        if b > 0:
                            pe.wait_ge(s_xraw, (V0 + b - 1) * CT + ct + 1)
                        project(p_proj[:, ct, :], ct, b).then_inc(s_px, 1)
                pe.wait_ge(s_soft, k * SOFT_STEPS + SOFT_STEPS - 3)
                pe.matmul(p_y_flat, causal[:, :], work[:, 0, :], start=True, stop=True).then_inc(s_cum, 1)
                pe.wait_ge(s_cumc, k + 1)
                pe.matmul(p_st[:, :], ident[:, P - 1:P].broadcast_to([P, P]), cum[:, :, :].rearrange("p t h -> p (t h)"),
                          start=True, stop=True).then_inc(s_last, 1)
                for j, (part, bank) in enumerate([(part_hm, p_tr[:, :].bitcast(BF16)),
                                                  (part_l, p_dt.bitcast(BF16))]):
                    pe.wait_ge(s_parts, k * 2 + j + 1)
                    for t in range(T):
                        mm = pe.transpose(bank[:, t * P:(t + 1) * P],
                                          part[:, t, :, :].rearrange("p a h -> p (a h)"), ident16[:, :])
                    mm.then_inc(s_partt, 1)
                pe.wait_ge(s_xs, (V0 + NB) * CT)
                pe.wait_ge(s_clamp, (k + 1) * 2)
                for j in range(2):
                    bank = (p_y_flat, p_st[:, :])[j]
                    for t in range(4):
                        s = (4 * j + t) * P
                        mm = pe.transpose(bank[:, t * P:(t + 1) * P], bc[:, 0, s:s + P], ident[:, :])
                    mm.then_inc(s_brow, 1)
                for j in range(2):
                    for t in range(4):
                        s = (4 * j + t) * P
                        mm = pe.matmul(p_out[:, j, t * P:(t + 1) * P], bc[:, 0, s:s + P], bc[:, 1, s:s + P],
                                       start=True, stop=True)
                    mm.then_inc(s_score, 1)
                for ct in range(CT):
                    project_x(k, 0, 0, ct, first=True)
                for ct in range(CT):
                    project_z(k, 0, 0, ct)
                pe.wait_ge(s_browc, (k + 1) * 2)
                for j in range(2):
                    rows(k, 0, 0, j, first=True)
                    spread(k, 0, 0, j, first=True)
                slot(k, 0, 0, first=True)
                slot(k, 0, 1)
                with pe.Fori(1, G - 1) as gi:
                    slot(k, gi, 0)
                    slot(k, gi, 1)
                slot(k, G - 1, 0)
                slot(k, G - 1, 1, last=True)
                project_out(k, G - 1, NB - 1, range(TPB))
                pe.wait_ge(s_sqs, (k + 1) * UNITS * CT)
                for t in range(T):
                    mm = pe.matmul(p_y_flat[:, 2 * t:2 * t + 2], square_sum[:, t * P:(t + 1) * P], ones[:, :],
                                   start=True, stop=True)
                mm.then_inc(s_var, 1)



def macaron_block(nc, hidden, ffn, mamba, out):
    batches, length, _ = hidden.shape
    tiles = batches * length // P
    with nc.sbuf_tensor("x", [P, tiles, D], F32) as x:
        ffn_phase(nc, "ffn1", x, hidden, ffn, None)
        mamba_phase(nc, "mamba", x, batches, mamba)
        ffn_phase(nc, "ffn2", x, None, ffn, out)



_FFN = ["wg", "wu", "wd", "sg_w", "sg_b", "su_w", "su_b", "sd_w", "sd_b"]
_MAMBA = ["conv_w", "conv_b", "dt_bias", "A_log", "D_param", "norm_w"]


def kernel(**inputs):
    import numpy as np
    import concourse.bacc as bacc
    from concourse.bass_utils import run_bass_kernel_spmd

    nc = bacc.Bacc("TRN2", target_bir_lowering=False, num_devices=1)
    arrays = {}

    def give(name, a):
        arrays[name] = np.ascontiguousarray(a)
        return nc.dram_tensor(name, arrays[name].shape, mybir.dt.from_np(arrays[name].dtype),
                              kind="ExternalInput").ap()

    hidden = give("hidden", inputs["L0_attn_hidden_states"])
    ffn = {n: give(n, inputs["L0_ffn_" + n]) for n in _FFN}
    ffn["router_t"] = give("router_t", np.asarray(inputs["L0_ffn_router_w"]).T)
    mamba = {n: give(n, inputs["L0_attn_" + n]) for n in _MAMBA}
    mamba["in_t"] = give("in_t", np.asarray(inputs["L0_attn_W_in"]).T)
    mamba["out_t"] = give("out_t", np.asarray(inputs["L0_attn_W_out"]).T)
    out = nc.dram_tensor("out", hidden.shape, F32, kind="ExternalOutput").ap()
    macaron_block(nc, hidden, ffn, mamba, out)
    result = run_bass_kernel_spmd(nc, [arrays], core_ids=[0])
    return result.results[0]["out"]
```

```python
from contextlib import ExitStack

import concourse.bass as bass
from concourse import mybir

F32 = mybir.dt.float32
F32R = mybir.dt.float32r
BF16 = mybir.dt.bfloat16
ALU = mybir.AluOpType
ACT = mybir.ActivationFunctionType
AX = mybir.AxisListType


P = 128
D = 512
KT = D // P
BLK = 512
TPB = BLK // P
LN_EPS = 1e-5


class Sems:

    def __init__(self, nc, ctx, phase):
        self.nc, self.ctx, self.phase = nc, ctx, phase

    def __call__(self, name):
        return self.ctx.enter_context(self.nc.semaphore(f"{self.phase}_{name}"))


def link(eng, sem, base=0):
    n = [0]

    def done(ins):
        n[0] += 1
        ins.then_inc(sem, 1)
        eng.wait_ge(sem, base + n[0])

    return done



class LayerNorm:

    def __init__(self, nc, ctx, sem, tiles, x_tile, xt_hi, xt_lo, ident, psum, xn=None):
        self.tiles, self.blocks = tiles, tiles // TPB
        self.x_tile, self.xt_hi, self.xt_lo, self.ident, self.psum = x_tile, xt_hi, xt_lo, ident, psum

        def sb(name, shape):
            return ctx.enter_context(nc.sbuf_tensor(f"{sem.phase}_{name}", shape, F32))

        self.stat = sb("ln_stats", [P, 2, 6])
        self.moments = sb("ln_moments", [P, tiles, 2])
        self.var = sb("ln_var", [P, tiles])
        self.roots = sb("ln_root", [P, tiles])
        self.rstd = sb("ln_rstd", [P, tiles])
        self.tmp = sb("ln_tmp", [P, tiles])
        self.xn = sb("ln_xn", [P, 2, D]) if xn is None else xn
        self.s_stat, self.s_var, self.s_root = sem("ln_stat"), sem("ln_var"), sem("ln_root")
        self.s_chain, self.s_xn, self.s_tr = sem("ln_chain"), sem("ln_xn"), sem("ln_tr")
        self.s_hi, self.s_lo = sem("ln_hi"), sem("ln_lo")

    def stats(self, eng, call, b, loaded=None):
        if loaded is not None:
            eng.wait_ge(loaded[b], 16)
        n = call * (2 * self.tiles) + b * (2 * TPB)
        for t in range(b * TPB, b * TPB + TPB):
            eng.bn_stats(self.stat[:, t % 2, :], self.x_tile(t)).then_inc(self.s_stat, 1)
            eng.wait_ge(self.s_stat, n + 1)
            eng.bn_aggr(self.moments[:, t, :], self.stat[:, t % 2, :]).then_inc(self.s_stat, 1)
            n += 2
        eng.wait_ge(self.s_stat, n)
        s = slice(b * TPB, b * TPB + TPB)
        eng.tensor_scalar(self.var[:, s], self.moments[:, s, 1], LN_EPS, None,
                          ALU.add).then_inc(self.s_var, 1)

    def root(self, eng, call, b):
        s = slice(b * TPB, b * TPB + TPB)
        eng.wait_ge(self.s_var, call * self.blocks + b + 1)
        eng.activation(self.roots[:, s], self.var[:, s], ACT.Sqrt).then_inc(self.s_root, 1)

    def normalise(self, eng, call, b):
        T = self.tiles
        s = slice(b * TPB, b * TPB + TPB)
        eng.wait_ge(self.s_root, call * self.blocks + b + 1)
        refine_rsqrt(eng, link(eng, self.s_chain, (call * self.blocks + b) * 5), self.rstd[:, s],
                     self.roots[:, s], self.var[:, s], self.tmp[:, s])

        def low(t):
            eng.wait_ge(self.s_hi, call * T + t + 1)
            c = slice(t * P, t * P + P)
            eng.tensor_tensor(self.xt_lo[:, :, c], self.psum(t), self.xt_hi[:, :, c].bitcast(F32),
                              ALU.subtract).then_inc(self.s_lo, 1)

        for t in range(b * TPB, b * TPB + TPB):
            if t >= 2:
                eng.wait_ge(self.s_tr, call * T + t - 1)
            eng.tensor_scalar(self.xn[:, t % 2, :], self.x_tile(t), self.moments[:, t, 0:1],
                              self.rstd[:, t:t + 1], ALU.subtract, ALU.mult).then_inc(self.s_xn, 1)
            if t > b * TPB:
                low(t - 1)
        low(b * TPB + TPB - 1)

    def high(self, eng, call, tiles):
        for t in tiles:
            eng.wait_ge(self.s_tr, call * self.tiles + t + 1)
            eng.activation(self.xt_hi[:, :, t * P:(t + 1) * P], self.psum(t), ACT.Copy).then_inc(self.s_hi, 1)

    def transposes(self, eng, call, tiles):
        T = self.tiles
        for t in tiles:
            eng.wait_ge(self.s_xn, call * T + t + 1)
            if t >= 2:
                eng.wait_ge(self.s_lo, call * T + t - 1)
            for k in range(KT):
                last = eng.transpose(self.psum(t)[:, k, :], self.xn[:, t % 2, k * P:(k + 1) * P],
                                     self.ident)
            last.then_inc(self.s_tr, 1)


def refine_rsqrt(eng, chain, r, root, v, tmp):
    chain(eng.reciprocal(r, root))
    chain(eng.tensor_tensor(tmp, r, r, ALU.mult))
    chain(eng.tensor_tensor(tmp, tmp, v, ALU.mult))
    chain(eng.tensor_scalar(tmp, tmp, -0.5, 1.5, ALU.mult, ALU.add))
    chain(eng.tensor_tensor(r, r, tmp, ALU.mult))


def build_identity(pool, ident, sem, at):
    pool.memset(ident, 0.0).then_inc(sem, 1)
    pool.wait_ge(sem, at + 1)
    pool.affine_select(out=ident, in_=ident, compare_op=ALU.not_equal, fill=1.0, base=0,
                       pattern=[[-1, P]], channel_multiplier=1).then_inc(sem, 1)



def ffn_phase(nc, phase, x, hidden, w, out):
    E, _, I = w["wg"].shape
    IT = I // P
    T = x.shape[1]
    NB = T // TPB
    PAIR = 2 * NB
    LAST = E * NB + NB - 1
    ctx = ExitStack()
    with ctx:
        sem = Sems(nc, ctx, phase)

        def sb(name, shape, dt=F32):
            return ctx.enter_context(nc.sbuf_tensor(f"{phase}_{name}", shape, dt))

        def ps(name, shape):
            return ctx.enter_context(nc.psum_tensor(f"{phase}_{name}", shape, F32))

        xt_hi, xt_lo = sb("xt_hi", [P, KT, T * P], F32R), sb("xt_lo", [P, KT, T * P], F32R)
        ident = sb("ident", [P, P])
        raw_in = sb("raw_in", [P, 2, KT, I])
        raw_out = sb("raw_out", [P, IT, D])
        in_hi, in_lo = sb("in_hi", [P, 2, 2, KT, I], F32R), sb("in_lo", [P, 2, 2, KT, I], F32R)
        out_hi, out_lo = sb("out_hi", [P, 2, IT, D], F32R), sb("out_lo", [P, 2, IT, D], F32R)
        sil = sb("sil", [P, IT, BLK])
        h = sb("h", [P, IT, BLK])
        h_hi, h_lo = sb("h_hi", [P, 2, IT, BLK], F32R), sb("h_lo", [P, 2, IT, BLK], F32R)
        router = sb("router", [P, KT, E])
        router_hi, router_lo = sb("router_hi", [P, KT, E], F32R), sb("router_lo", [P, KT, E], F32R)
        gate_bias, up_bias = sb("gate_bias", [P, IT]), sb("up_bias", [P, IT])
        one = sb("one", [P, 1])
        down_bias = sb("down_bias", [P, D])
        logits_t = sb("logits_t", [E, BLK])
        logits = sb("logits", [P, T, E])
        above = sb("above", [P, T, E, E])
        equal = sb("equal", [P, T, E, E])
        earlier = sb("earlier", [P, E, E])
        rank = sb("rank", [P, T, E])
        chosen = sb("chosen", [P, T, E])
        weight = sb("weight", [P, (E + 1) * T])

        p_gate, p_up = ps("p_gate", [P, IT, BLK]), ps("p_up", [P, IT, BLK])
        p_down = ps("p_down", [P, TPB, D])
        p_logits_t = p_down[0:E, 2, :]
        p_logits = p_down[:, 3, 0:TPB * E]

        s_const, s_small, s_router, s_route = sem("const"), sem("small"), sem("router"), sem("route")
        s_x = [sem(f"x{b}") for b in range(NB)]
        s_raw_in, s_raw_out, s_split = sem("raw_in"), sem("raw_out"), sem("split")
        s_gate, s_up, s_down = sem("gate"), sem("up"), sem("down")
        s_sil, s_h, s_hi, s_lo, s_acc = sem("sil"), sem("h"), sem("hi"), sem("lo"), sem("acc")
        s_bias, s_rank, s_weight, s_out = sem("bias"), sem("rank"), sem("weight"), sem("out")
        s_lgt, s_lgt_copy, s_lg, s_lg_copy = sem("lgt"), sem("lgt_copy"), sem("lg"), sem("lg_copy")
        SPLITS = 6

        ln = LayerNorm(nc, ctx, sem, T, lambda t: x[:, t, :], xt_hi, xt_lo, ident[:, :],
                       lambda t: p_down[:, t % 2, :].rearrange("p (k c) -> p k c", k=KT))

        block = ctx.enter_context(nc.Block())

        @block.sync
        def _(sp):
            def load_x(blocks):
                rows = hidden.rearrange("a (t p) d -> p a t d", p=P)
                per = rows.shape[2]
                for b in blocks:
                    a, t = b * TPB // per, b * TPB % per
                    sp.dma_start(x[:, b * TPB:(b + 1) * TPB, :],
                                 rows[:, a, t:t + TPB, :]).then_inc(s_x[b], 16)

            def load(turn, gate, up, down, first=False):
                if not first:
                    sp.wait_ge(s_split, turn * SPLITS - 2)
                sp.dma_start(raw_in[:, 0, :, :], gate.rearrange("(k p) i -> p k i", p=P)).then_inc(s_raw_in, 16)
                sp.dma_start(raw_in[:, 1, :, :], up.rearrange("(k p) i -> p k i", p=P)).then_inc(s_raw_in, 16)
                if not first:
                    sp.wait_ge(s_split, turn * SPLITS)
                sp.dma_start(raw_out[:, :, :], down.rearrange("(k p) d -> p k d", p=P)).then_inc(s_raw_out, 16)

            if hidden is not None:
                load_x([0])
            sp.dma_start(router[:, :, :], w["router_t"].rearrange("(k p) e -> p k e", p=P)).then_inc(s_router, 16)
            load(0, w["sg_w"], w["su_w"], w["sd_w"], first=True)
            with nc.allow_non_contiguous_dma(reason="short vectors, once"):
                sp.dma_start(down_bias[:, :], w["sd_b"].partition_broadcast(P)).then_inc(s_small, 16)
                sp.dma_start(gate_bias[:, :], w["sg_b"].rearrange("(i p) -> p i", p=P)).then_inc(s_small, 16)
                sp.dma_start(up_bias[:, :], w["su_b"].rearrange("(i p) -> p i", p=P)).then_inc(s_small, 16)
            if hidden is not None:
                load_x(range(1, NB))
            with sp.Fori(0, E) as e:
                load(e + 1, w["wg"][e], w["wu"][e], w["wd"][e])
            if out is not None:
                rows = out.rearrange("a (t p) d -> p a t d", p=P)
                per = rows.shape[2]
                for b in range(NB):
                    a, t = b * TPB // per, b * TPB % per
                    sp.wait_ge(s_acc, (E * NB + b + 1) * TPB)
                    sp.dma_start(rows[:, a, t:t + TPB, :],
                                 x[:, b * TPB:(b + 1) * TPB, :]).then_inc(s_out, 16)
                sp.wait_ge(s_out, 16 * NB)

        @block.gpsimd
        def _(pool):
            build_identity(pool, ident[:, :], s_const, 0)
            pool.memset(one[:, :], 1.0).then_inc(s_const, 1)
            pool.memset(weight[:, E * T:(E + 1) * T], 0.5).then_inc(s_const, 1)
            pool.memset(earlier[:, :, :], 0.0).then_inc(s_const, 1)
            pool.wait_ge(s_const, 5)
            pool.affine_select(out=earlier[:, :, :], in_=earlier[:, :, :], compare_op=ALU.is_ge, fill=1.0,
                               base=0, pattern=[[-1, E], [1, E]], channel_multiplier=0).then_inc(s_const, 1)

            def split_part(turn, at, hi, lo, raw):
                pool.tensor_tensor(hi, raw, one[:, :].unsqueeze(1).broadcast_to(raw.shape),
                                   ALU.mult).then_inc(s_split, 1)
                pool.wait_ge(s_split, turn * SPLITS + at + 1)
                pool.tensor_tensor(lo, raw, hi.bitcast(F32), ALU.subtract).then_inc(s_split, 1)

            def split_in(turn, parity):
                pool.wait_ge(s_raw_in, turn * 32 + 32)
                for j in range(2):
                    split_part(turn, 2 * j, in_hi[:, parity, j, :, :], in_lo[:, parity, j, :, :], raw_in[:, j, :, :])

            def split_out(turn, parity):
                pool.wait_ge(s_raw_out, turn * 16 + 16)
                split_part(turn, 4, out_hi[:, parity, :, :], out_lo[:, parity, :, :], raw_out[:, :, :])

            def split(turn, parity, behind):
                if behind:
                    pool.wait_ge(s_down, (turn - 1) * NB * TPB)
                split_in(turn, parity)
                split_out(turn, parity)

            pool.wait_ge(s_router, 16)
            pool.tensor_copy(router_hi[:, :, :], router[:, :, :]).then_inc(s_route, 1)
            pool.wait_ge(s_route, 1)
            pool.tensor_tensor(router_lo[:, :, :], router[:, :, :], router_hi[:, :, :].bitcast(F32),
                               ALU.subtract).then_inc(s_route, 1)
            split_in(0, 0)
            pool.wait_ge(s_small, 48)
            pool.tensor_scalar(down_bias[:, :], down_bias[:, :], 0.5, None, ALU.mult).then_inc(s_route, 1)
            split_out(0, 0)
            pool.wait_ge(s_route, 3)
            for t in range(T):
                pool.wait_ge(ln.s_xn, t + 1)
                pool.tensor_tensor(x[:, t, :], x[:, t, :], down_bias[:, :], ALU.add).then_inc(s_bias, 1)
            split(1, 1, behind=False)
            with pool.Fori(1, E // 2) as i:
                split(i * 2, 0, behind=True)
                split(i * 2 + 1, 1, behind=True)
            split(E, 0, behind=True)

        @block.scalar
        def _(act):
            def silu(unit, i, bias=None, first=False):
                act.wait_ge(s_gate, unit * IT + i + 1)
                if not first:
                    act.wait_ge(s_h, unit * IT - IT + i + 1)
                act.activation(sil[:, i, :], p_gate[:, i, :], ACT.Silu,
                               bias=0.0 if bias is None else bias[:, i:i + 1]).then_inc(s_sil, 1)

            def high(unit, parity, first=False):
                for i in range(IT):
                    act.wait_ge(s_h, unit * IT + i + 1)
                    if not first:
                        act.wait_ge(s_down, unit * TPB - TPB)
                    act.activation(h_hi[:, parity, i, :], h[:, i, :], ACT.Copy).then_inc(s_hi, 1)

            def gate(unit, parity):
                for i in range(IT):
                    silu(unit, i)
                high(unit, parity)

            def logits_columns(b):
                act.wait_ge(s_lgt, b + 1)
                act.activation(logits_t[:, :], p_logits_t, ACT.Copy).then_inc(s_lgt_copy, 1)

            def logits_rows(b):
                act.wait_ge(s_lg, b + 1)
                act.activation(logits[:, b * TPB:(b + 1) * TPB, :],
                               p_logits.rearrange("p (t e) -> p t e", t=TPB), ACT.Copy).then_inc(s_lg_copy, 1)

            ln.root(act, 0, 0)
            ln.high(act, 0, range(TPB))
            ln.root(act, 0, 1)
            logits_columns(0)
            act.wait_ge(s_small, 48)
            for b in range(NB - 1):
                nxt = (b + 1) * TPB
                silu(b, 0, gate_bias, first=b == 0)
                logits_rows(b)
                ln.high(act, 0, range(nxt, nxt + 2))
                silu(b, 1, gate_bias, first=b == 0)
                ln.high(act, 0, range(nxt + 2, nxt + TPB))
                if b + 2 < NB:
                    ln.root(act, 0, b + 2)
                    high(b, b % 2, first=b < 2)
                logits_columns(b + 1)
            logits_rows(NB - 1)
            high(NB - 2, NB % 2)
            for i in range(IT):
                silu(NB - 1, i, gate_bias)
            high(NB - 1, (NB - 1) % 2)
            with act.Fori(0, E // 2) as i:
                for u in range(PAIR):
                    gate(i * PAIR + NB + u, u % 2)

        @block.vector
        def _(dve):
            def product(unit, bias=None, first=False):
                for i in range(IT):
                    dve.wait_ge(s_up, unit * IT + i + 1)
                    dve.wait_ge(s_sil, unit * IT + i + 1)
                    if not first:
                        dve.wait_ge(s_lo, unit * IT - IT + i + 1)
                    if bias is None:
                        dve.tensor_tensor(h[:, i, :], p_up[:, i, :], sil[:, i, :], ALU.mult).then_inc(s_h, 1)
                    else:
                        dve.scalar_tensor_tensor(h[:, i, :], p_up[:, i, :], bias[:, i:i + 1], sil[:, i, :],
                                                 ALU.add, ALU.mult).then_inc(s_h, 1)

            def low(unit, parity):
                for i in range(IT):
                    dve.wait_ge(s_hi, unit * IT + i + 1)
                    dve.tensor_tensor(h_lo[:, parity, i, :], h[:, i, :],
                                      h_hi[:, parity, i, :].bitcast(F32), ALU.subtract).then_inc(s_lo, 1)

            def inner(unit, parity, bias=None, first=False):
                product(unit, bias, first)
                low(unit, parity)

            def accumulate(unit, e, b):
                for t in range(TPB):
                    tile = b * TPB + t
                    dve.wait_ge(s_down, unit * TPB + t + 1)
                    dve.scalar_tensor_tensor(x[:, tile, :], p_down[:, t, :],
                                             weight[:, bass.ds(e * T + tile, 1)], x[:, tile, :],
                                             ALU.mult, ALU.add).then_inc(s_acc, 1)

            SHARED = E
            loaded = s_x if hidden is not None else None
            ln.stats(dve, 0, 0, loaded)
            ln.normalise(dve, 0, 0)
            ln.stats(dve, 0, 1, loaded)
            dve.wait_ge(s_small, 48)
            for b in range(NB - 1):
                if b + 2 < NB:
                    ln.stats(dve, 0, b + 2, loaded)
                ln.normalise(dve, 0, b + 1)
                inner(b, b % 2, up_bias, first=b == 0)
            dve.wait_ge(s_bias, T)
            dve.wait_ge(s_const, 6)
            accumulate(0, SHARED, 0)
            product(NB - 1, up_bias)
            accumulate(1, SHARED, 1)
            low(NB - 1, (NB - 1) % 2)
            for b in range(2, NB - 1):
                accumulate(b, SHARED, b)
            dve.wait_ge(s_lg_copy, NB)
            l_f = logits[:, :, :].unsqueeze(2).broadcast_to([P, T, E, E])
            l_e = logits[:, :, :].unsqueeze(3).broadcast_to([P, T, E, E])
            dve.tensor_tensor(above[:, :, :, :], l_f, l_e, ALU.is_gt).then_inc(s_rank, 1)
            dve.tensor_tensor(equal[:, :, :, :], l_f, l_e, ALU.is_equal).then_inc(s_rank, 1)
            dve.wait_ge(s_rank, 2)
            dve.tensor_tensor(equal[:, :, :, :], equal[:, :, :, :],
                              earlier[:, :, :].unsqueeze(1).broadcast_to([P, T, E, E]),
                              ALU.mult).then_inc(s_rank, 1)
            dve.wait_ge(s_rank, 3)
            dve.tensor_tensor(above[:, :, :, :], above[:, :, :, :], equal[:, :, :, :],
                              ALU.add).then_inc(s_rank, 1)
            dve.wait_ge(s_rank, 4)
            dve.tensor_reduce(rank[:, :, :], above[:, :, :, :], AX.X, ALU.add).then_inc(s_rank, 1)
            dve.wait_ge(s_rank, 5)
            dve.tensor_scalar(chosen[:, :, :], rank[:, :, :], 2.0, 0.5, ALU.is_lt,
                              ALU.mult).then_inc(s_rank, 1)
            dve.wait_ge(s_rank, 6)
            dve.tensor_tensor(weight[:, 0:E * T].rearrange("p (e t) -> p t e", e=E), chosen[:, :, :],
                              logits[:, :, :], ALU.mult).then_inc(s_weight, 1)
            dve.wait_ge(s_weight, 1)

            inner(NB, NB % 2)
            accumulate(NB - 1, SHARED, NB - 1)
            with dve.Fori(0, E // 2 - 1) as i:
                for u in range(1, PAIR + 1):
                    inner(i * PAIR + NB + u, u % 2)
                    accumulate(i * PAIR + NB + u - 1, i * 2 + (u - 1) // NB, (u - 1) % NB)
            for n in range(LAST - PAIR + 2, LAST + 2):
                if n <= LAST:
                    inner(n, n % 2)
                accumulate(n - 1, (n - 1) // NB - 1, (n - 1) % NB)

        @block.tensor
        def _(pe):
            pe.wait_ge(s_const, 2)
            def inner(unit, turn, parity, b, first=False, tiles=range(IT)):
                c = slice(b * BLK, (b + 1) * BLK)
                for i in tiles:
                    if not first:
                        pe.wait_ge(s_h, unit * IT - IT + i + 1)
                    for j, (bank, done) in enumerate([(p_gate, s_gate), (p_up, s_up)]):
                        if b == 0:
                            pe.wait_ge(s_split, turn * SPLITS + 2 * j + 2)
                        for k in range(KT):
                            wh = in_hi[:, parity, j, k, i * P:(i + 1) * P]
                            wl = in_lo[:, parity, j, k, i * P:(i + 1) * P]
                            pe.matmul(bank[:, i, :], wh, xt_lo[:, k, c], start=(k == 0), stop=False)
                            pe.matmul(bank[:, i, :], wh, xt_hi[:, k, c], start=False, stop=False)
                            last = pe.matmul(bank[:, i, :], wl, xt_hi[:, k, c], start=False,
                                             stop=(k == KT - 1))
                        last.then_inc(done, 1)

            def outer(unit, turn, parity, b, first=False):
                pe.wait_ge(s_lo, unit * IT + IT)
                if b == 0:
                    pe.wait_ge(s_split, turn * SPLITS + SPLITS)
                if first:
                    pe.wait_ge(ln.s_lo, T)
                    pe.wait_ge(s_lg_copy, NB)
                for t in range(TPB):
                    if not first:
                        pe.wait_ge(s_acc, unit * TPB - TPB + t + 1)
                    c = slice(t * P, (t + 1) * P)
                    for k in range(IT):
                        hh, hl = h_hi[:, b % 2, k, c], h_lo[:, b % 2, k, c]
                        pe.matmul(p_down[:, t, :], hh, out_lo[:, parity, k, :], start=(k == 0), stop=False)
                        pe.matmul(p_down[:, t, :], hh, out_hi[:, parity, k, :], start=False, stop=False)
                        last = pe.matmul(p_down[:, t, :], hl, out_hi[:, parity, k, :], start=False,
                                         stop=(k == IT - 1))
                    last.then_inc(s_down, 1)

            def logits_columns(b):
                pe.wait_ge(ln.s_lo, (b + 1) * TPB)
                if b > 0:
                    pe.wait_ge(s_lgt_copy, b)
                c = slice(b * BLK, (b + 1) * BLK)
                for k in range(KT):
                    for j, (a, r) in enumerate([(xt_lo, router_lo), (xt_lo, router_hi),
                                                (xt_hi, router_lo), (xt_hi, router_hi)]):
                        last = pe.matmul(p_logits_t, r[:, k, :], a[:, k, c], start=(k == 0 and j == 0),
                                         stop=(k == KT - 1 and j == 3))
                last.then_inc(s_lgt, 1)

            def logits_rows(b):
                pe.wait_ge(s_lgt_copy, b + 1)
                if b > 0:
                    pe.wait_ge(s_lg_copy, b)
                for t in range(TPB):
                    last = pe.transpose(p_logits[:, t * E:(t + 1) * E], logits_t[:, t * P:(t + 1) * P],
                                        ident[0:E, 0:E])
                last.then_inc(s_lg, 1)

            ln.transposes(pe, 0, range(TPB))
            pe.wait_ge(s_route, 2)
            logits_columns(0)
            for b in range(NB - 1):
                nxt = (b + 1) * TPB
                inner(b, 0, 0, b, first=b == 0, tiles=[0])
                logits_rows(b)
                ln.transposes(pe, 0, range(nxt, nxt + 2))
                inner(b, 0, 0, b, first=b == 0, tiles=range(1, IT))
                ln.transposes(pe, 0, range(nxt + 2, nxt + TPB))
                logits_columns(b + 1)
            logits_rows(NB - 1)
            outer(0, 0, 0, 0, first=True)
            inner(NB - 1, 0, 0, NB - 1)
            for b in range(1, NB - 1):
                outer(b, 0, 0, b)
            with pe.Fori(0, E // 2) as i:
                for u in range(PAIR):
                    turn = i * 2 + u // NB + 1
                    inner(i * PAIR + NB + u, turn, (u // NB + 1) % 2, u % NB)
                    if u == 0:
                        outer(i * PAIR + NB - 1, i * 2, 0, NB - 1)
                    else:
                        outer(i * PAIR + NB + u - 1, i * 2 + (u - 1) // NB + 1, ((u - 1) // NB + 1) % 2,
                              (u - 1) % NB)
            outer(LAST, E, 0, NB - 1)



def mamba_phase(nc, phase, x, batches, w):
    DI, _ = w["out_t"].shape
    HEADS = w["dt_bias"].shape[0]
    HD = DI // HEADS
    N = P
    T = x.shape[1] // batches
    NB = T // TPB
    CT = 2
    GC = CT * P
    GH = GC // HD
    G = DI // GC
    CPB = TPB
    UNITS = G * NB
    TAPS = w["conv_w"].shape[2]
    HALO = TAPS - 1
    CONV_TILES = w["conv_w"].shape[0] // P
    PARTS = 3
    RMS_EPS = 1e-5
    Z0, X0, B0, DT0 = 0, DI, 2 * DI, 2 * DI + 2 * N
    assert NB == 2 and N == P and HEADS * 2 == P
    ctx = ExitStack()
    with ctx:
        sem = Sems(nc, ctx, phase)

        def sb(name, shape, dt=F32):
            return ctx.enter_context(nc.sbuf_tensor(f"{phase}_{name}", shape, dt))

        def ps(name, shape):
            return ctx.enter_context(nc.psum_tensor(f"{phase}_{name}", shape, F32))

        ident, ident16 = sb("ident", [P, P]), sb("ident16", [P, P], BF16)
        causal = sb("causal", [P, P])
        ones = sb("ones", [P, 2])
        one = sb("one", [P, 1])
        head_of = sb("head_of", [PARTS * GH, GH], BF16)
        taps = sb("taps", [P, CONV_TILES, TAPS])
        conv_bias = sb("conv_bias", [P, CONV_TILES])
        skip = sb("skip", [P, DI // P])
        norm_w = sb("norm_w", [P, DI // P])
        dt_bias, decay_rate = sb("dt_bias", [P, HEADS]), sb("decay_rate", [P, HEADS])
        xt_hi, xt_lo = sb("xt_hi", [P, KT, T * P], F32R), sb("xt_lo", [P, KT, T * P], F32R)
        raw_x, raw_z = sb("raw_x", [P, KT, GC]), sb("raw_z", [P, KT, GC])
        raw_out = sb("raw_out", [P, CT, D])
        in_hi, in_lo = sb("in_hi", [P, 2 * CT, KT, P], F32R), sb("in_lo", [P, 2 * CT, KT, P], F32R)
        out_hi, out_lo = sb("out_hi", [P, CT, D], F32R), sb("out_lo", [P, CT, D], F32R)
        bc = sb("bc", [P, 2, T * P])
        b_rows = sb("b_rows", [P, T, N])
        scores = sb("scores", [P, T, P])
        dt = sb("dt", [P, T, HEADS])
        cum = sb("cum", [P, T, HEADS])
        exp_cum = sb("exp_cum", [P, T, HEADS])
        to_end = sb("to_end", [P, T, HEADS])
        exp_last = sb("exp_last", [P, T, HEADS])
        square_sum = sb("square_sum", [P, T * P])
        total = sb("total", [P, T, D])
        var, root, rstd, tmp = (sb(n, [P, T]) for n in ("var", "root", "rstd", "tmp"))
        neg_cum_g, exp_last_g, to_end_g = (sb(n, [P, T, GH]) for n in ("neg_cum_g", "exp_last_g", "to_end_g"))
        cum_g = sb("cum_g", [PARTS * GH, T * P], BF16)
        state, decayed = sb("state", [P, GH, HD]), sb("decayed", [P, GH, HD])
        xraw = sb("xraw", [P, NB, CT, HALO + BLK])
        xs = sb("xs", [P, 2, CT, BLK])
        zs = sb("zs", [P, 2, CT, BLK])
        xdt = sb("xdt", [P, CPB, GH, HD])
        xend = sb("xend", [P, CPB, GH, HD])
        mix = sb("mix", [P, 2, GH, P])
        y = sb("y", [P, CPB, GC])
        g = sb("g", [P, CT, BLK])
        g_hi, g_lo = sb("g_hi", [P, CT, BLK], F32R), sb("g_lo", [P, CT, BLK], F32R)
        cum_hm, cum_l = (mix[:, j, :, :].rearrange("p h l -> p (h l)").bitcast(BF16) for j in range(2))
        xdt_flat = xdt[:, :, :, :].rearrange("p c h d -> p (c h d)")
        xend_flat = xend[:, :, :, :].rearrange("p c h d -> p (c h d)")
        work = [xdt_flat[:, 0:T * HEADS], xdt_flat[:, T * HEADS:2 * T * HEADS], xend_flat[:, 0:T * HEADS]]
        dt_t = xend_flat[0:HEADS, 0:T * P]
        parts = g[:, :, :].rearrange("p c t -> p (c t)").bitcast(BF16).rearrange("p (j t a h) -> p j t a h", j=2, t=T, a=2)
        part_hm = parts[:, 0]
        part_l = parts[:, 1]

        p_proj = ps("p_proj", [P, CT, BLK])
        p_tr, p_dec = ps("p_tr", [P, BLK]), ps("p_dec", [P, GH, P])
        p_y, p_st = ps("p_y", [P, 2, GH, HD]), ps("p_st", [P, BLK])
        p_out = ps("p_out", [P, 2, D])
        p_var = p_out[:, 0, 0:2 * T]
        p_dt_t = (p_tr[0:HEADS, :], p_dec[:, :, :].rearrange("p h c -> p (h c)")[0:HEADS, :])
        p_y_flat = p_y[:, :, :, :].rearrange("p a h d -> p (a h d)")

        s_const, s_small, s_rate = sem("const"), sem("small"), sem("rate")
        s_raw_x, s_raw_z, s_raw_out = sem("raw_x"), sem("raw_z"), sem("raw_out")
        s_split_x, s_split_z, s_scaled, s_split_out = (sem("split_x"), sem("split_z"), sem("scaled"),
                                                       sem("split_out"))
        s_dtt, s_dtt_copy = sem("dtt"), sem("dtt_copy")
        s_dt, s_arg, s_u, s_soft, s_cum, s_cumc = (sem("dt"), sem("arg"), sem("u"), sem("soft"), sem("cum"),
                                                   sem("cumc"))
        s_parts, s_last, s_clamp, s_exps, s_partt, s_partc = (sem("parts"), sem("last"), sem("clamp"),
                                                              sem("exps"), sem("partt"), sem("partc"))
        s_brow, s_browc, s_score, s_clear = sem("brow"), sem("browc"), sem("score"), sem("clear")
        s_px, s_pz, s_xtr, s_dec, s_y2, s_st, s_ytr, s_pout = (
            sem("px"), sem("pz"), sem("xtr"), sem("dec"), sem("y2"), sem("st"), sem("ytr"), sem("pout"))
        s_xraw, s_xs, s_zs, s_exp, s_ghi, s_sq = (sem("xraw"), sem("xs"), sem("zs"), sem("exp"),
                                                  sem("ghi"), sem("sq"))
        s_conv, s_skip, s_g, s_glo, s_xdt, s_mix = (sem("conv"), sem("skip"), sem("g"), sem("glo"),
                                                    sem("xdt"), sem("mix"))
        s_car, s_y, s_state, s_acc = sem("car"), sem("y"), sem("state"), sem("acc")
        s_xend, s_decayed, s_sqs, s_min = sem("xend"), sem("decayed"), sem("sqs"), sem("min")
        s_stored, s_cumg = sem("stored"), sem("cumg")
        cum_parts = nc.dram_tensor(f"{phase}_cum_parts", [batches, PARTS, HEADS, T * P], BF16).ap()
        s_var, s_vara, s_root, s_fin, s_add = (sem("var"), sem("vara"), sem("root"), sem("fin"),
                                               sem("add"))

        lns = LayerNorm(nc, ctx, sem, T, None, xt_hi, xt_lo, ident[:, :],
                        lambda t: (p_y_flat, p_st[:, :])[t % 2].rearrange("p (k c) -> p k c", k=KT),
                        xn=y[:, :, :].rearrange("p c d -> p (c d)").rearrange("p (a d) -> p a d", a=2))

        CLEARS = 1 + CPB
        CONVS = UNITS + NB
        SMALL = 16 * (5 + P // HD)
        SOFT_STEPS = 20
        FIN_STEPS = 5

        def unit(k, gi, b):
            u = gi * NB + b
            return u + k * UNITS, u + NB + k * CONVS

        block = ctx.enter_context(nc.Block())

        @block.sync
        def _(sp):
            in_t = w["in_t"].rearrange("(k p) c -> p k c", p=P)

            def load_in(stream, x0, z_steps, z0, n=GC):
                if not isinstance(stream, int) or stream > 0:
                    sp.wait_ge(s_split_x, stream * 4)
                    sp.wait_ge(s_split_z, z_steps)
                sp.dma_start(raw_x[:, :, :], in_t[:, :, bass.ds(x0, GC)]).then_inc(s_raw_x, 16)
                sp.dma_start(raw_z[:, :, 0:n], in_t[:, :, bass.ds(z0, n)]).then_inc(s_raw_z, 16)

            def load_out(n, gi):
                if not isinstance(n, int) or n > 0:
                    sp.wait_ge(s_split_out, n * 4)
                sp.dma_start(raw_out[:, :, :],
                             w["out_t"][bass.ds(gi * GC, GC), :].rearrange("(k p) d -> p k d", p=P)).then_inc(s_raw_out, 16)

            def load_cum(k, gi):
                for a in range(PARTS):
                    sp.dma_start(cum_g[a * GH:(a + 1) * GH, :],
                                 cum_parts[k, a, bass.ds(gi * GH, GH)]).then_inc(s_cumg, 16)

            for k in range(batches):
                sx, sz = k * (G + 1), k * (4 * G + 2)
                load_in(sx, B0, sz, DT0, HEADS)
                if k == 0:
                    with nc.allow_non_contiguous_dma(reason="short vectors, once"):
                        sp.dma_start(taps[:, :, :],
                                     w["conv_w"].rearrange("(j p) a k -> p j (a k)", p=P)).then_inc(s_small, 16)
                        sp.dma_start(conv_bias[:, :], w["conv_b"].rearrange("(j p) -> p j", p=P)).then_inc(s_small, 16)
                        sp.dma_start(norm_w[:, :], w["norm_w"].rearrange("(j p) -> p j", p=P)).then_inc(s_small, 16)
                        per = P // HD
                        d = w["D_param"].rearrange("(j a) -> a j", a=per)
                        for a in range(per):
                            sp.dma_start(skip[a * HD:(a + 1) * HD, :], d[a].partition_broadcast(HD)).then_inc(s_small, 16)
                        sp.dma_start(dt_bias[:, :], w["dt_bias"].partition_broadcast(P)).then_inc(s_small, 16)
                        sp.dma_start(decay_rate[:, :], w["A_log"].partition_broadcast(P)).then_inc(s_small, 16)
                load_in(sx + 1, X0, sz + 2, Z0)
                load_out(k * G, 0)
                for a in range(PARTS):
                    sp.wait_ge(s_partc, k * 2 + a // 2 + 1)
                    part = (cum_hm, cum_l)[a // 2]
                    sp.dma_start(cum_parts[k, a],
                                 part[a % 2 * HEADS:(a % 2 + 1) * HEADS, :]).then_inc(s_stored, 16)
                sp.wait_ge(s_stored, (k + 1) * PARTS * 16)
                load_cum(k, 0)
                with sp.Fori(1, G) as gi:
                    load_in(gi + (sx + 1), gi * GC + X0, gi * 4 + (sz + 2), gi * GC + Z0)
                    sp.wait_ge(s_min, gi * (NB * CPB) + k * UNITS * CPB)
                    load_cum(k, gi)
                    load_out(gi + k * G, gi)

        @block.gpsimd
        def _(pool):
            build_identity(pool, ident[:, :], s_const, 0)
            build_identity(pool, ident16[:, :], s_const, 2)
            pool.memset(causal[:, :], 1.0).then_inc(s_const, 1)
            pool.memset(head_of[:, :], 0.0).then_inc(s_const, 1)
            pool.wait_ge(s_const, 6)
            pool.affine_select(out=causal[:, :], in_=causal[:, :], compare_op=ALU.is_ge, fill=0.0, base=0,
                               pattern=[[1, P]], channel_multiplier=-1).then_inc(s_const, 1)
            for a in range(PARTS):
                pool.affine_select(out=head_of[:, :], in_=head_of[:, :], compare_op=ALU.not_equal, fill=1.0,
                                   base=-a * GH, pattern=[[-1, GH]],
                                   channel_multiplier=1).then_inc(s_const, 1)
                pool.wait_ge(s_const, 8 + a)
            pool.memset(ones[:, :], 1.0).then_inc(s_const, 1)
            pool.memset(one[:, :], 1.0).then_inc(s_const, 1)
            pool.memset(xraw[:, 0, :, 0:HALO], 0.0).then_inc(s_const, 1)
            pool.wait_ge(s_const, 13)

            def split(hi, lo, raw, done, at):
                unit_col = one[:, :] if len(raw.shape) == 2 else one[:, :].unsqueeze(1)
                pool.tensor_tensor(hi, raw, unit_col.broadcast_to(raw.shape), ALU.mult).then_inc(done, 1)
                pool.wait_ge(done, at + 1)
                pool.tensor_tensor(lo, raw, hi.bitcast(F32), ALU.subtract).then_inc(done, 1)

            def split_x(stream, ct):
                pool.wait_ge(s_raw_x, stream * 16 + 16)
                split(in_hi[:, ct, :, :], in_lo[:, ct, :, :], raw_x[:, :, ct * P:(ct + 1) * P],
                      s_split_x, stream * 4 + 2 * ct)

            def split_z(loads, steps, ct):
                pool.wait_ge(s_raw_z, loads * 16)
                split(in_hi[:, CT + ct, :, :], in_lo[:, CT + ct, :, :], raw_z[:, :, ct * P:(ct + 1) * P],
                      s_split_z, steps + 2 * ct)

            def split_out(n, ct):
                pool.wait_ge(s_scaled, n * CT + ct + 1)
                split(out_hi[:, ct, :], out_lo[:, ct, :], raw_out[:, ct, :], s_split_out, n * 4 + 2 * ct)

            def add_squares(U, b, ct, first=False):
                pool.wait_ge(s_sq, U * CT + ct + 1)
                if not first:
                    pool.wait_ge(s_sqs, U * CT + ct)
                c = slice(b * BLK, (b + 1) * BLK)
                pool.tensor_tensor(square_sum[:, c], square_sum[:, c], zs[:, b, ct, :], ALU.add).then_inc(s_sqs, 1)

            def decay_x(k, gi, b, j, first=False):
                U, V = unit(k, gi, b)
                pool.wait_ge(s_xdt, U * 2 + j + 1)
                if not first:
                    pool.wait_ge(s_st, U * CPB - CPB + 2 * j + 2)
                c = b * CPB + 2 * j
                pool.tensor_tensor(xend[:, 2 * j:2 * j + 2, :, :], xdt[:, 2 * j:2 * j + 2, :, :],
                                   to_end_g[:, c:c + 2, :].unsqueeze(3).broadcast_to([P, 2, GH, HD]),
                                   ALU.mult).then_inc(s_xend, 1)

            def decay_scores(U, b, c):
                pool.wait_ge(s_exp, U * CPB + c + 1)
                pool.tensor_tensor(mix[:, c % 2, :, :], mix[:, c % 2, :, :],
                                   scores[:, b * CPB + c, :].unsqueeze(1).broadcast_to([P, GH, P]),
                                   ALU.mult).then_inc(s_mix, 1)

            def slot(k, gi, b, first=False, second=False, last=False, group0=False, last_group=False):
                U, V = unit(k, gi, b)
                gn, bn = (gi, 1) if b == 0 else (gi + 1, 0)

                def decay_state(c):
                    if b > 0 or c > 0:
                        pool.wait_ge(s_state, U * CPB + c)
                    pool.tensor_tensor(decayed[:, :, :], state[:, :, :],
                                       exp_last_g[:, b * CPB + c, :].unsqueeze(2).broadcast_to([P, GH, HD]),
                                       ALU.mult).then_inc(s_decayed, 1)

                def next_x(ct):
                    if b == 0 and not last_group:
                        pool.wait_ge(s_px, V * CT + CT + ct + 1)
                        split_x(gi + (k * (G + 1) + 2), ct)

                def next_z(ct):
                    if b == ct and not last_group:
                        pool.wait_ge(s_pz, (U - b) * CT + CT + ct + 1)
                        split_z(gi + (k * (G + 1) + 3), gi * 4 + (k * (4 * G + 2) + 6), ct)

                def this_out(ct):
                    if b == 1:
                        if ct == 0 and not (k == 0 and group0):
                            pool.wait_ge(s_pout, U * TPB - TPB)
                        split_out(gi + k * G, ct)

                def clear(c):
                    if first:
                        if k > 0:
                            pool.wait_ge(s_add, k * T)
                        n = T // CPB
                        pool.memset(total[:, c * n:(c + 1) * n, :], 0.0).then_inc(s_clear, 1)

                decay_state(0)
                decay_scores(U, b, 1)
                clear(0)
                next_z(1)
                decay_x(k, gi, b, 1, first)
                decay_state(1)
                decay_scores(U, b, 2)
                clear(1)
                this_out(0)
                if last:
                    this_out(1)
                decay_state(2)
                decay_scores(U, b, 3)
                clear(2)
                if not first:
                    add_squares(U - 1, 1 - b, 0, second)
                decay_state(3)
                clear(3)
                if not first:
                    add_squares(U - 1, 1 - b, 1)
                if not last:
                    this_out(1)
                next_x(0)
                next_x(1)
                if not last:
                    decay_x(k, gn, bn, 0)
                next_z(0)
                if not last:
                    decay_scores(U + 1, bn, 0)

            def last_squares(k):
                for ct in range(CT):
                    add_squares((k + 1) * UNITS - 1, NB - 1, ct)

            for k in range(batches):
                split_x_base = k * (G + 1)
                if k > 0:
                    pool.wait_ge(s_px, k * CONVS * CT)
                    pool.wait_ge(s_pz, k * UNITS * CT)
                pool.wait_ge(s_raw_z, split_x_base * 16 + 16)
                split(in_hi[:, CT, :, 0:HEADS], in_lo[:, CT, :, 0:HEADS], raw_z[:, :, 0:HEADS],
                      s_split_z, k * (4 * G + 2))
                if k > 0:
                    last_squares(k - 1)
                for ct in range(CT):
                    split_x(split_x_base, ct)
                if k > 0:
                    pool.wait_ge(s_var, k)
                pool.memset(square_sum[:, :], 0.0).then_inc(s_clear, 1)
                for ct in range(CT):
                    pool.wait_ge(s_px, (k * CONVS + NB - 1) * CT + ct + 1)
                    split_x(split_x_base + 1, ct)
                pool.wait_ge(s_dt, k + 1)
                for ct in range(CT):
                    split_z(split_x_base + 2, k * (4 * G + 2) + 2, ct)
                if k > 0:
                    pool.wait_ge(s_pout, k * UNITS * TPB)
                decay_x(k, 0, 0, 0, first=True)
                decay_scores(k * UNITS, 0, 0)
                slot(k, 0, 0, first=True)
                pool.wait_ge(s_clear, (k + 1) * CLEARS)
                slot(k, 0, 1, second=True, group0=True)
                with pool.Fori(1, G - 1) as gi:
                    slot(k, gi, 0)
                    slot(k, gi, 1)
                slot(k, G - 1, 0, last_group=True)
                slot(k, G - 1, 1, last=True, last_group=True)
            last_squares(batches - 1)

        @block.scalar
        def _(act):
            def raw(V, b, ct, first=False):
                act.wait_ge(s_px, V * CT + ct + 1)
                if not first:
                    act.wait_ge(s_conv, V * (CT * TAPS) - 2 * CT * TAPS + (ct + 1) * TAPS)
                if b > 0:
                    act.activation(xraw[:, b, ct, 0:HALO], xraw[:, b - 1, ct, BLK:BLK + HALO], ACT.Copy)
                act.activation(xraw[:, b, ct, HALO:], p_proj[:, ct, :], ACT.Copy).then_inc(s_xraw, 1)

            def silu_x(V, parity, ct):
                act.wait_ge(s_conv, V * (CT * TAPS) + (ct + 1) * TAPS)
                act.activation(xs[:, parity, ct, :], xs[:, parity, ct, :], ACT.Silu).then_inc(s_xs, 1)

            def silu_z(U, parity, ct, young=False):
                act.wait_ge(s_pz, U * CT + ct + 1)
                if not young:
                    act.wait_ge(s_sqs, U * CT - 2 * CT + ct + 1)
                act.activation(zs[:, parity, ct, :], p_proj[:, ct, :], ACT.Silu).then_inc(s_zs, 1)

            def rms_root(k):
                act.wait_ge(s_vara, k + 1)
                act.activation(root[:, :], var[:, :], ACT.Sqrt).then_inc(s_root, 1)

            def high(U, ct, second=False):
                act.wait_ge(s_g, U * CT + ct + 1)
                if not second:
                    act.wait_ge(s_pout, U * TPB)
                act.activation(g_hi[:, ct, :], g[:, ct, :], ACT.Copy).then_inc(s_ghi, 1)

            def square(U, b, ct):
                act.activation(zs[:, b, ct, :], g[:, ct, :], ACT.Square).then_inc(s_sq, 1)

            def exponents(U, b, c):
                act.wait_ge(s_min, U * CPB + c + 1)
                for h in range(GH):
                    ins = act.activation(mix[:, c % 2, h, :], mix[:, c % 2, h, :], ACT.Exp,
                                         bias=neg_cum_g[:, b * CPB + c, h:h + 1])
                ins.then_inc(s_exp, 1)

            def slot(k, gi, b, first=False, second=False, last=False):
                U, V = unit(k, gi, b)
                if not first:
                    for ct in range(CT):
                        high(U - 1, ct, second)
                if not last:
                    raw(V + 1, 1 - b, 0)
                exponents(U, b, 2)
                if not first:
                    for ct in range(CT):
                        square(U - 1, 1 - b, ct)
                if not last:
                    raw(V + 1, 1 - b, 1)
                exponents(U, b, 3)
                if not last:
                    for ct in range(CT):
                        silu_x(V + 1, 1 - b, ct)
                    for ct in range(CT):
                        silu_z(U + 1, 1 - b, ct, first)
                    exponents(U + 1, 1 - b, 0)
                    exponents(U + 1, 1 - b, 1)

            for k in range(batches):
                V0 = k * CONVS

                def dt_copy(b):
                    act.wait_ge(s_dtt, k * NB + b + 1)
                    act.activation(dt_t[:, b * BLK:(b + 1) * BLK], p_dt_t[b], ACT.Copy).then_inc(s_dtt_copy, 1)

                if k == 0:
                    for b in range(NB):
                        lns.root(act, k, b)
                lns.high(act, k, range(TPB))
                dt_copy(0)
                lns.high(act, k, range(TPB, TPB + 2))
                raw(V0, 0, 0, first=k == 0)
                lns.high(act, k, range(TPB + 2, T))
                dt_copy(1)
                if k > 0:
                    rms_root(k - 1)
                raw(V0, 0, 1, first=k == 0)
                if k == 0:
                    act.wait_ge(s_small, SMALL)
                    act.activation(decay_rate[:, :], decay_rate[:, :], ACT.Exp).then_inc(s_rate, 1)
                act.wait_ge(s_arg, (k + 1) * 4)
                act.activation(work[0], work[1], ACT.Exp).then_inc(s_u, 1)
                for ct in range(CT):
                    raw(V0 + 1, 1, ct, first=k == 0)
                U0, V_first = unit(k, 0, 0)
                for ct in range(CT):
                    raw(V_first, 0, ct)
                for ct in range(CT):
                    silu_z(U0, 0, ct, True)
                for b in range(NB):
                    for ct in range(CT):
                        act.wait_ge(s_conv, (V0 + b) * (CT * TAPS) + (ct + 1) * TAPS)
                        c = slice(b * BLK, (b + 1) * BLK)
                        act.activation(bc[:, ct, c], bc[:, ct, c], ACT.Silu).then_inc(s_xs, 1)
                act.wait_ge(s_cumc, k + 1)
                act.activation(exp_cum[:, :, :], cum[:, :, :], ACT.Exp).then_inc(s_exps, 1)
                act.wait_ge(s_last, k + 1)
                act.activation(exp_last[:, :, :], p_st[:, :].rearrange("p (t h) -> p t h", t=T),
                               ACT.Exp).then_inc(s_exps, 1)
                act.wait_ge(s_clamp, (k + 1) * 2)
                act.activation(to_end[:, :, :], to_end[:, :, :], ACT.Exp).then_inc(s_exps, 1)
                act.wait_ge(s_partt, k * 2 + 1)
                act.activation(cum_hm[:, :], p_tr[:, :].bitcast(BF16), ACT.Copy).then_inc(s_partc, 1)
                act.wait_ge(s_partt, k * 2 + 2)
                act.activation(cum_l[:, :], p_dec[:, :, :].rearrange("p h c -> p (h c)").bitcast(BF16),
                               ACT.Copy).then_inc(s_partc, 1)
                for j in range(2):
                    act.wait_ge(s_brow, k * 2 + j + 1)
                    act.activation(b_rows[:, 4 * j:4 * j + 4, :],
                                   (p_y_flat, p_st[:, :])[j].rearrange("p (t n) -> p t n", t=4),
                                   ACT.Copy).then_inc(s_browc, 1)
                for ct in range(CT):
                    silu_x(V_first, 0, ct)
                for c in range(2):
                    exponents(U0, 0, c)
                slot(k, 0, 0, first=True)
                slot(k, 0, 1, second=True)
                with act.Fori(1, G - 1) as gi:
                    slot(k, gi, 0)
                    slot(k, gi, 1)
                slot(k, G - 1, 0)
                slot(k, G - 1, 1, last=True)
                if k + 1 < batches:
                    for b in range(NB):
                        lns.root(act, k + 1, b)
                for ct in range(CT):
                    high((k + 1) * UNITS - 1, ct)
                for ct in range(CT):
                    square((k + 1) * UNITS - 1, NB - 1, ct)
            rms_root(batches - 1)

        @block.vector
        def _(dve):
            def conv_step(V, b, ct, tile, dst, i):
                n = V * (CT * TAPS) + ct * TAPS
                src = xraw[:, b, ct, :]
                tap = taps[:, bass.ds(tile, 1), :]
                if i == 0:
                    dve.wait_ge(s_xraw, V * CT + ct + 1)
                    dve.tensor_scalar(dst, src[:, HALO:HALO + BLK], tap[:, 0, HALO:HALO + 1],
                                      conv_bias[:, bass.ds(tile, 1)], ALU.mult, ALU.add).then_inc(s_conv, 1)
                else:
                    dve.wait_ge(s_conv, n + i)
                    j = HALO - i
                    dve.scalar_tensor_tensor(dst, src[:, j:j + BLK], tap[:, 0, j:j + 1], dst,
                                             ALU.mult, ALU.add).then_inc(s_conv, 1)

            def conv_x(k, gi, b, ct, steps, young=False):
                U, V = unit(k, gi, b)
                if not young and 0 in steps:
                    dve.wait_ge(s_skip, U * CT - 2 * CT + CT)
                for i in steps:
                    conv_step(V, b, ct, gi * CT + ct, xs[:, b, ct, :], i)

            def gate(k, gi, b, first=False):
                U, V = unit(k, gi, b)
                for ct in range(CT):
                    dve.wait_ge(s_ytr, U * CT + ct + 1)
                    if not first:
                        dve.wait_ge(s_sq, U * CT - CT + ct + 1)
                        dve.wait_ge(s_glo, U * CT - CT + ct + 1)
                    dve.scalar_tensor_tensor(g[:, ct, :], xs[:, b, ct, :], skip[:, bass.ds(gi * CT + ct, 1)],
                                             p_out[:, ct, :], ALU.mult,
                                             ALU.add).then_inc(s_skip, 1)
                for ct in range(CT):
                    dve.wait_ge(s_skip, U * CT + ct + 1)
                    dve.wait_ge(s_zs, U * CT + ct + 1)
                    dve.tensor_tensor(g[:, ct, :], g[:, ct, :], zs[:, b, ct, :], ALU.mult).then_inc(s_g, 1)

            def gate_low(U):
                for ct in range(CT):
                    dve.wait_ge(s_ghi, U * CT + ct + 1)
                    dve.tensor_tensor(g_lo[:, ct, :], g[:, ct, :], g_hi[:, ct, :].bitcast(F32),
                                      ALU.subtract).then_inc(s_glo, 1)

            def accumulate(U, b, t):
                dve.wait_ge(s_pout, U * TPB + t + 1)
                tile = b * TPB + t
                dve.tensor_tensor(total[:, tile, :], p_out[:, t % 2, :], total[:, tile, :],
                                  ALU.add).then_inc(s_acc, 1)

            def stage(k, gi, first=False):
                heads = bass.ds(gi * GH, GH)
                U, _ = unit(k, gi, 0)
                if not first:
                    dve.wait_ge(s_exp, U * CPB)
                    dve.wait_ge(s_decayed, U * CPB)
                    dve.wait_ge(s_xend, U * 2)
                    dve.wait_ge(s_state, U * CPB)
                dve.memset(state[:, :, :], 0.0)
                dve.tensor_scalar(neg_cum_g[:, :, :], cum[:, :, heads], -1.0, None, ALU.mult)
                dve.tensor_copy(exp_last_g[:, :, :], exp_last[:, :, heads])
                dve.tensor_copy(to_end_g[:, :, :], to_end[:, :, heads])

            def times_dt(k, gi, b, j, first=False):
                U, V = unit(k, gi, b)
                heads = bass.ds(gi * GH, GH)
                dve.wait_ge(s_xtr, U * 2 + j + 1)
                if not first:
                    dve.wait_ge(s_y2, U * CPB - CPB + 2 * j + 2)
                    dve.wait_ge(s_xend, U * 2 - 2 + j + 1)
                c = b * CPB + 2 * j
                dve.tensor_tensor(xdt[:, 2 * j:2 * j + 2, :, :],
                                  p_tr[:, :].rearrange("p (c h d) -> p c h d", c=2, h=GH),
                                  dt[:, c:c + 2, heads].unsqueeze(3).broadcast_to([P, 2, GH, HD]),
                                  ALU.mult).then_inc(s_xdt, 1)

            def clamp(k, gi, b, c, first=False):
                U, _ = unit(k, gi, b)
                dve.wait_ge(s_dec, U * CPB + c + 1)
                if not (first and c < 2):
                    dve.wait_ge(s_y2, U * CPB + c - 1)
                cum_s = cum[:, b * CPB + c, bass.ds(gi * GH, GH)]
                dve.tensor_tensor(mix[:, c % 2, :, :], p_dec[:, :, :],
                                  cum_s.unsqueeze(2).broadcast_to([P, GH, P]), ALU.min).then_inc(s_min, 1)

            def slot(k, gi, b, first=False, second=False, last=False, group0=False):
                U, V = unit(k, gi, b)
                heads = bass.ds(gi * GH, GH)
                gn, bn = (gi, 1) if b == 0 else (gi + 1, 0)
                gp, bp = (gi, 0) if b == 1 else (gi - 1, 1)

                def combine(c):
                    n = U * CPB + c
                    yc = y[:, c, :].rearrange("p (h d) -> p h d", h=GH)
                    dve.wait_ge(s_y2, n + 1)
                    dve.tensor_tensor(yc, p_y[:, 1, :, :],
                                      exp_cum[:, b * CPB + c, heads].unsqueeze(2).broadcast_to([P, GH, HD]),
                                      ALU.mult).then_inc(s_car, 1)
                    dve.wait_ge(s_st, n + 1)
                    dve.wait_ge(s_decayed, n + 1)
                    dve.tensor_tensor(state[:, :, :], p_st[:, 0:GC].rearrange("p (h d) -> p h d", h=GH),
                                      decayed[:, :, :], ALU.add).then_inc(s_state, 1)
                    dve.wait_ge(s_car, n + 1)
                    dve.tensor_tensor(yc, p_y[:, 0, :, :], yc, ALU.add).then_inc(s_y, 1)

                def conv(ct, steps):
                    if not last:
                        conv_x(k, gn, bn, ct, steps, first)

                def add_out(t):
                    if not first:
                        accumulate(U - 1, bp, t)

                def next_stats(n):
                    if last and k + 1 < batches:
                        layer_norm_of(k + 1)
                        lns.stats(dve, k + 1, n)

                if not first:
                    gate(k, gp, bp, first=second)
                combine(0)
                clamp(k, gi, b, 2)
                if not first:
                    gate_low(U - 1)
                conv(0, (0, 1))
                next_stats(0)
                combine(1)
                conv(0, (2,))
                clamp(k, gi, b, 3)
                conv(0, (3,))
                conv(1, (0, 1))
                next_stats(1)
                if last:
                    add_out(0)
                combine(2)
                if last:
                    add_out(1)
                conv(1, (2, 3))
                if b == 0 and not group0:
                    scale_out(k, gi)
                combine(3)
                if not last:
                    if b == 1:
                        stage(k, gn)
                    times_dt(k, gn, bn, 0)
                    clamp(k, gn, bn, 0)
                for t in range(2 if last else 0, CPB - 1):
                    add_out(t)
                if last:
                    add_out(3)
                else:
                    add_out(3)
                    times_dt(k, gn, bn, 1)
                    clamp(k, gn, bn, 1)

            def scale_out(k, gi):
                for ct in range(CT):
                    dve.wait_ge(s_raw_out, (gi + k * G) * 16 + 16)
                    dve.tensor_scalar(raw_out[:, ct, :], raw_out[:, ct, :],
                                      norm_w[:, bass.ds(gi * CT + ct, 1)], None, ALU.mult).then_inc(s_scaled, 1)

            def layer_norm_of(k):
                lns.x_tile = lambda t: x[:, k * T + t, :]

            def mean_square(k):
                dve.wait_ge(s_var, k + 1)
                dve.tensor_scalar(var[:, :], p_var.rearrange("p (t a) -> p t a", a=2)[:, :, 0],
                                  1.0 / DI, RMS_EPS, ALU.mult, ALU.add).then_inc(s_vara, 1)

            def finish(k):
                dve.wait_ge(s_root, k + 1)
                refine_rsqrt(dve, link(dve, s_fin, k * FIN_STEPS), rstd[:, :], root[:, :], var[:, :], tmp[:, :])
                for t in range(T):
                    dve.scalar_tensor_tensor(x[:, k * T + t, :], total[:, t, :], rstd[:, t:t + 1],
                                             x[:, k * T + t, :], ALU.mult, ALU.add).then_inc(s_add, 1)

            layer_norm_of(0)
            for b in range(NB):
                lns.stats(dve, 0, b)
            for k in range(batches):
                lns.normalise(dve, k, 0)
                if k > 0:
                    for t in range(TPB):
                        accumulate(k * UNITS - 1, NB - 1, t)
                lns.normalise(dve, k, 1)
                if k > 0:
                    mean_square(k - 1)
                else:
                    dve.wait_ge(s_small, SMALL)
                    dve.wait_ge(s_const, 13)
                V0 = k * CONVS

                def conv_bc(b, ct, i):
                    conv_step(V0 + b, b, ct, DI // P + ct, bc[:, ct, b * BLK:(b + 1) * BLK], i)

                v = dt[:, :, :]
                u, a, m = (x_.rearrange("p (t h) -> p t h", t=T) for x_ in work)
                step = link(dve, s_arg, k * 4)
                dve.wait_ge(s_dt, k + 1)
                step(dve.tensor_tensor(v, p_y_flat.rearrange("p (t h) -> p t h", t=T),
                                       dt_bias[:, :].unsqueeze(1).broadcast_to([P, T, HEADS]), ALU.add))
                step(dve.tensor_scalar(a, v, -1.0, None, ALU.mult))
                step(dve.tensor_tensor(a, a, v, ALU.min))
                step(dve.tensor_scalar(m, v, 0.0, None, ALU.max))
                for ct in range(CT):
                    for i in range(TAPS):
                        conv_bc(0, ct, i)
                dve.wait_ge(s_u, k + 1)
                step = link(dve, s_soft, k * SOFT_STEPS)
                q, r = a, v
                step(dve.tensor_scalar(r, u, 2.0, None, ALU.add))
                step(dve.reciprocal(r, r))
                step(dve.tensor_tensor(u, u, r, ALU.mult))
                step(dve.tensor_tensor(q, u, u, ALU.mult))
                step(dve.tensor_scalar(r, q, 1.0 / 21, None, ALU.mult))
                for n, c in enumerate((19, 17, 15, 13, 11, 9, 7, 5, 3)):
                    if n > 0:
                        dve.wait_ge(s_soft, k * SOFT_STEPS + 5 + n)
                    dve.scalar_tensor_tensor(r, r, 1.0 / c, q, ALU.add, ALU.mult).then_inc(s_soft, 1)
                    if n < CT * TAPS:
                        conv_bc(1, n // TAPS, n % TAPS)
                dve.wait_ge(s_soft, k * SOFT_STEPS + 14)
                step = link(dve, s_soft, k * SOFT_STEPS + 14)
                step(dve.scalar_tensor_tensor(r, r, 1.0, u, ALU.add, ALU.mult))
                step(dve.scalar_tensor_tensor(v, r, 2.0, m, ALU.mult, ALU.add))
                dve.wait_ge(s_rate, 1)
                step(dve.scalar_tensor_tensor(u, v, -1.0, decay_rate[:, :].unsqueeze(1).broadcast_to([P, T, HEADS]),
                                              ALU.mult, ALU.mult))
                conv_x(k, 0, 0, 0, (0, 1), True)
                dve.wait_ge(s_cum, k + 1)
                dve.tensor_copy(cum[:, :, :], p_y_flat.rearrange("p (t h) -> p t h", t=T)).then_inc(s_cumc, 1)
                conv_x(k, 0, 0, 0, (2,), True)
                dve.wait_ge(s_cumc, k + 1)
                step(dve.memset(part_l[:, :, 1, :], 0.0))
                step(dve.tensor_copy(part_hm[:, :, 0, :], cum[:, :, :]))
                step(dve.tensor_tensor(a, cum[:, :, :], part_hm[:, :, 0, :], ALU.subtract))
                dve.tensor_copy(part_hm[:, :, 1, :], a).then_inc(s_parts, 1)
                conv_x(k, 0, 0, 0, (3,), True)
                dve.wait_ge(s_parts, k * 2 + 1)
                dve.tensor_tensor(part_l[:, :, 0, :], a, part_hm[:, :, 1, :], ALU.subtract).then_inc(s_parts, 1)
                dve.wait_ge(s_last, k + 1)
                step = link(dve, s_clamp, k * 2)
                dve.wait_ge(s_exps, k * 3 + 2)
                step(dve.tensor_tensor(to_end[:, :, :], p_st[:, :].rearrange("p (t h) -> p t h", t=T),
                                       cum[:, :, :], ALU.subtract))
                step(dve.tensor_scalar(to_end[:, :, :], to_end[:, :, :], 0.0, None, ALU.min))
                for j in range(2):
                    dve.wait_ge(s_score, k * 2 + j + 1)
                    dve.tensor_tensor(scores[:, 4 * j:4 * j + 4, :], p_out[:, j, :].rearrange("p (t l) -> p t l", t=4),
                                      causal[:, :].unsqueeze(1).broadcast_to([P, 4, P]),
                                      ALU.mult)
                conv_x(k, 0, 0, 1, range(TAPS), True)
                dve.wait_ge(s_exps, k * 3 + 3)
                stage(k, 0, first=True)
                times_dt(k, 0, 0, 0, first=True)
                clamp(k, 0, 0, 0, first=True)
                times_dt(k, 0, 0, 1, first=True)
                clamp(k, 0, 0, 1, first=True)
                scale_out(k, 0)
                if k > 0:
                    finish(k - 1)
                slot(k, 0, 0, first=True, group0=True)
                dve.wait_ge(s_clear, (k + 1) * CLEARS)
                slot(k, 0, 1, second=True)
                with dve.Fori(1, G - 1) as gi:
                    slot(k, gi, 0)
                    slot(k, gi, 1)
                slot(k, G - 1, 0)
                slot(k, G - 1, 1, last=True)
                U = (k + 1) * UNITS - 1
                gate(k, G - 1, NB - 1)
                gate_low(U)
            for t in range(TPB):
                accumulate(batches * UNITS - 1, NB - 1, t)
            mean_square(batches - 1)
            finish(batches - 1)

        @block.tensor
        def _(pe):
            def project(bank, piece, b):
                c = slice(b * BLK, (b + 1) * BLK)
                for kk in range(KT):
                    pe.matmul(bank, in_hi[:, piece, kk, :], xt_lo[:, kk, c], start=(kk == 0), stop=False)
                    pe.matmul(bank, in_hi[:, piece, kk, :], xt_hi[:, kk, c], start=False, stop=False)
                    last = pe.matmul(bank, in_lo[:, piece, kk, :], xt_hi[:, kk, c], start=False,
                                     stop=(kk == KT - 1))
                return last

            def project_x(k, gi, b, ct, first=False):
                U, V = unit(k, gi, b)
                if first:
                    pe.wait_ge(s_xraw, V * CT - CT + ct + 1)
                else:
                    pe.wait_ge(s_zs, U * CT - CT + ct + 1)
                if b == 0:
                    pe.wait_ge(s_split_x, (gi + (k * (G + 1) + 1)) * 4 + 2 * ct + 2)
                project(p_proj[:, ct, :], ct, b).then_inc(s_px, 1)

            def project_z(k, gi, b, ct):
                U, V = unit(k, gi, b)
                pe.wait_ge(s_xraw, V * CT + ct + 1)
                if b == 0:
                    pe.wait_ge(s_split_z, gi * 4 + (k * (4 * G + 2) + 2 * ct + 4))
                project(p_proj[:, ct, :], CT + ct, b).then_inc(s_pz, 1)

            def project_out(k, gi, b, tiles):
                U, _ = unit(k, gi, b)
                for t in tiles:
                    if t == 0:
                        pe.wait_ge(s_glo, U * CT + CT)
                        if b == 0:
                            pe.wait_ge(s_split_out, (gi + k * G) * 4 + 4)
                    if t >= 2:
                        pe.wait_ge(s_acc, U * TPB + t - 1)
                    c = slice(t * P, (t + 1) * P)
                    for ct in range(CT):
                        pe.matmul(p_out[:, t % 2, :], g_hi[:, ct, c], out_lo[:, ct, :], start=(ct == 0), stop=False)
                        pe.matmul(p_out[:, t % 2, :], g_hi[:, ct, c], out_hi[:, ct, :], start=False, stop=False)
                        last = pe.matmul(p_out[:, t % 2, :], g_lo[:, ct, c], out_hi[:, ct, :], start=False,
                                         stop=(ct == CT - 1))
                    last.then_inc(s_pout, 1)

            def rows(k, gi, b, j, first=False):
                U, V = unit(k, gi, b)
                if j == 0:
                    pe.wait_ge(s_xs, V * CT + CT)
                if not (first and j == 0):
                    pe.wait_ge(s_xdt, U * 2 + j)
                for c in range(2):
                    for ct in range(CT):
                        s = (2 * j + c) * P
                        mm = pe.transpose(p_tr[:, c * GC + ct * P:c * GC + (ct + 1) * P],
                                          xs[:, b, ct, s:s + P], ident[:, :])
                mm.then_inc(s_xtr, 1)

            def spread(k, gi, b, c, first=False):
                U, V = unit(k, gi, b)
                if not (first and c == 0):
                    pe.wait_ge(s_min, U * CPB + c)
                if b == 0 and c == 0:
                    pe.wait_ge(s_cumg, gi * (PARTS * 16) + (k * G + 1) * (PARTS * 16))
                s = (b * CPB + c) * P
                for h in range(GH):
                    mm = pe.matmul(p_dec[:, h, :], head_of[:, h:h + 1].broadcast_to([PARTS * GH, P]),
                                   cum_g[:, s:s + P], start=True, stop=True)
                mm.then_inc(s_dec, 1)

            def slot(k, gi, b, first=False, last=False):
                U, V = unit(k, gi, b)
                gn, bn = (gi, 1) if b == 0 else (gi + 1, 0)
                gp, bp = (gi, 0) if b == 1 else (gi - 1, 1)

                def recur(c):
                    s = (b * CPB + c) * P
                    if not (first and c == 0):
                        pe.wait_ge(s_y, U * CPB + c)
                        pe.wait_ge(s_state, U * CPB + c)
                    pe.wait_ge(s_mix, U * CPB + c + 1)
                    if c % 2 == 0:
                        pe.wait_ge(s_xdt, U * 2 + c // 2 + 1)
                    pe.matmul(p_y[:, 1, :, :], bc[:, 1, s:s + P], state[:, :, :], start=True, stop=True)
                    for h in range(GH):
                        mm = pe.matmul(p_y[:, 0, h, :], mix[:, c % 2, h, :], xdt[:, c, h, :], start=True, stop=True)
                    mm.then_inc(s_y2, 1)
                    if c % 2 == 0:
                        pe.wait_ge(s_xend, U * 2 + c // 2 + 1)
                    pe.matmul(p_st[:, 0:GC], b_rows[:, b * CPB + c, :],
                              xend[:, c, :, :].rearrange("p h d -> p (h d)"), start=True,
                              stop=True).then_inc(s_st, 1)

                def columns(ct):
                    if ct == 0:
                        pe.wait_ge(s_y, U * CPB + CPB)
                    if not first:
                        pe.wait_ge(s_acc, U * TPB - 1 + ct)
                    for c in range(CPB):
                        mm = pe.transpose(p_out[:, ct, c * P:(c + 1) * P],
                                          y[:, c, ct * P:(ct + 1) * P], ident[:, :])
                    mm.then_inc(s_ytr, 1)

                recur(0)
                if not last:
                    project_x(k, gn, bn, 0)
                spread(k, gi, b, 2)
                recur(1)
                if not last:
                    project_x(k, gn, bn, 1)
                spread(k, gi, b, 3)
                if last:
                    project_out(k, gp, bp, (0,))
                recur(2)
                if last:
                    project_out(k, gp, bp, (1,))
                else:
                    project_z(k, gn, bn, 0)
                recur(3)
                if last:
                    project_out(k, gp, bp, (2, 3))
                else:
                    project_z(k, gn, bn, 1)
                    rows(k, gn, bn, 0)
                    spread(k, gn, bn, 0)
                    if not first:
                        project_out(k, gp, bp, range(TPB))
                columns(0)
                if not last:
                    rows(k, gn, bn, 1)
                    spread(k, gn, bn, 1)
                columns(1)

            def mean_square(k):
                pe.wait_ge(s_sqs, (k + 1) * UNITS * CT)
                pe.wait_ge(s_acc, (k + 1) * UNITS * TPB)
                for t in range(T):
                    mm = pe.matmul(p_var[:, 2 * t:2 * t + 2], square_sum[:, t * P:(t + 1) * P], ones[:, :],
                                   start=True, stop=True)
                mm.then_inc(s_var, 1)

            pe.wait_ge(s_const, 13)
            for k in range(batches):
                V0 = k * CONVS

                def dt_columns(b):
                    pe.wait_ge(lns.s_lo, k * T + (b + 1) * TPB)
                    if b == 0:
                        pe.wait_ge(s_split_z, k * (4 * G + 2) + 2)
                    c = slice(b * BLK, (b + 1) * BLK)
                    for kk in range(KT):
                        for j, (a, ww) in enumerate([(xt_lo, in_hi), (xt_hi, in_lo), (xt_hi, in_hi)]):
                            mm = pe.matmul(p_dt_t[b], ww[:, CT, kk, 0:HEADS], a[:, kk, c],
                                           start=(kk == 0 and j == 0), stop=(kk == KT - 1 and j == 2))
                    mm.then_inc(s_dtt, 1)

                def project_bc(b, ct):
                    if b == 0:
                        pe.wait_ge(s_split_x, k * (G + 1) * 4 + 2 * ct + 2)
                    else:
                        pe.wait_ge(s_xraw, (V0 + b - 1) * CT + ct + 1)
                    project(p_proj[:, ct, :], ct, b).then_inc(s_px, 1)

                if k == 0:
                    lns.transposes(pe, k, range(TPB))
                    dt_columns(0)
                else:
                    lns.transposes(pe, k, range(2))
                    project_out(k - 1, G - 1, NB - 1, (0,))
                    lns.transposes(pe, k, range(2, TPB))
                    project_out(k - 1, G - 1, NB - 1, (1,))
                    dt_columns(0)
                    project_out(k - 1, G - 1, NB - 1, (2, 3))
                lns.transposes(pe, k, range(TPB, TPB + 2))
                project_bc(0, 0)
                lns.transposes(pe, k, range(TPB + 2, T))
                if k > 0:
                    mean_square(k - 1)
                dt_columns(1)
                pe.wait_ge(s_dtt_copy, (k + 1) * NB)
                for t in range(T):
                    mm = pe.transpose(p_y_flat[:, t * HEADS:(t + 1) * HEADS], dt_t[:, t * P:(t + 1) * P],
                                      ident[0:HEADS, 0:HEADS])
                mm.then_inc(s_dt, 1)
                project_bc(0, 1)
                for ct in range(CT):
                    project_bc(1, ct)
                for ct in range(CT):
                    project_x(k, 0, 0, ct, first=True)
                for ct in range(CT):
                    project_z(k, 0, 0, ct)
                pe.wait_ge(s_soft, k * SOFT_STEPS + SOFT_STEPS - 3)
                pe.matmul(p_y_flat, causal[:, :], work[0], start=True, stop=True).then_inc(s_cum, 1)
                pe.wait_ge(s_cumc, k + 1)
                pe.matmul(p_st[:, :], ident[:, P - 1:P].broadcast_to([P, P]), cum[:, :, :].rearrange("p t h -> p (t h)"),
                          start=True, stop=True).then_inc(s_last, 1)
                for j, (part, bank) in enumerate([(part_hm, p_tr[:, :].bitcast(BF16)),
                                                  (part_l, p_dec[:, :, :].rearrange("p h c -> p (h c)").bitcast(BF16))]):
                    pe.wait_ge(s_parts, k * 2 + j + 1)
                    for t in range(T):
                        mm = pe.transpose(bank[:, t * P:(t + 1) * P],
                                          part[:, t, :, :].rearrange("p a h -> p (a h)"), ident16[:, :])
                    mm.then_inc(s_partt, 1)
                pe.wait_ge(s_xs, (V0 + NB) * CT)
                pe.wait_ge(s_clamp, (k + 1) * 2)
                for j in range(2):
                    bank = (p_y_flat, p_st[:, :])[j]
                    for t in range(4):
                        s = (4 * j + t) * P
                        mm = pe.transpose(bank[:, t * P:(t + 1) * P], bc[:, 0, s:s + P], ident[:, :])
                    mm.then_inc(s_brow, 1)
                for j in range(2):
                    for t in range(4):
                        s = (4 * j + t) * P
                        mm = pe.matmul(p_out[:, j, t * P:(t + 1) * P], bc[:, 0, s:s + P], bc[:, 1, s:s + P],
                                       start=True, stop=True)
                    mm.then_inc(s_score, 1)
                pe.wait_ge(s_browc, (k + 1) * 2)
                for j in range(2):
                    rows(k, 0, 0, j, first=True)
                    spread(k, 0, 0, j, first=True)
                slot(k, 0, 0, first=True)
                slot(k, 0, 1)
                with pe.Fori(1, G - 1) as gi:
                    slot(k, gi, 0)
                    slot(k, gi, 1)
                slot(k, G - 1, 0)
                slot(k, G - 1, 1, last=True)
            project_out(batches - 1, G - 1, NB - 1, range(TPB))
            mean_square(batches - 1)



def macaron_block(nc, hidden, ffn, mamba, out):
    batches, length, _ = hidden.shape
    tiles = batches * length // P
    with nc.sbuf_tensor("x", [P, tiles, D], F32) as x:
        ffn_phase(nc, "ffn1", x, hidden, ffn, None)
        mamba_phase(nc, "mamba", x, batches, mamba)
        ffn_phase(nc, "ffn2", x, None, ffn, out)



_FFN = ["wg", "wu", "wd", "sg_w", "sg_b", "su_w", "su_b", "sd_w", "sd_b"]
_MAMBA = ["conv_w", "conv_b", "dt_bias", "A_log", "D_param", "norm_w"]


def kernel(**inputs):
    import numpy as np
    import concourse.bacc as bacc
    from concourse.bass_utils import run_bass_kernel_spmd

    nc = bacc.Bacc("TRN2", target_bir_lowering=False, num_devices=1)
    arrays = {}

    def give(name, a):
        arrays[name] = np.ascontiguousarray(a)
        return nc.dram_tensor(name, arrays[name].shape, mybir.dt.from_np(arrays[name].dtype),
                              kind="ExternalInput").ap()

    hidden = give("hidden", inputs["L0_attn_hidden_states"])
    ffn = {n: give(n, inputs["L0_ffn_" + n]) for n in _FFN}
    ffn["router_t"] = give("router_t", np.asarray(inputs["L0_ffn_router_w"]).T)
    mamba = {n: give(n, inputs["L0_attn_" + n]) for n in _MAMBA}
    mamba["in_t"] = give("in_t", np.asarray(inputs["L0_attn_W_in"]).T)
    mamba["out_t"] = give("out_t", np.asarray(inputs["L0_attn_W_out"]).T)
    out = nc.dram_tensor("out", hidden.shape, F32, kind="ExternalOutput").ap()
    macaron_block(nc, hidden, ffn, mamba, out)
    result = run_bass_kernel_spmd(nc, [arrays], core_ids=[0])
    return result.results[0]["out"]
```
